# Optimizing a Trainium2 kernel written in Bass

```python
import numpy as np
import jax
import jax.numpy as jnp

def _softmax(x, axis=-1):
    return jax.nn.softmax(x, axis=axis)

def _gelu(x):
    return jax.nn.gelu(x, approximate=True)

def _silu(x):
    return jax.nn.silu(x)

def _sigmoid(x):
    return jax.nn.sigmoid(x)

def _layernorm(x, axis=-1, eps=1e-05):
    m = jnp.mean(x, axis=axis, keepdims=True)
    v = jnp.var(x, axis=axis, keepdims=True)
    return (x - m) / jnp.sqrt(v + eps)

def _scatter_add(tgt, idx, src, axis=0):
    return tgt.at[idx].add(src)

def _segment_sum(src, seg, n):
    return jax.ops.segment_sum(src, seg, n)
kernel_name = 'mk_adaln_d1_jaxref_r4_982c0a'

def setup_inputs(seed: int=0):
    np.random.seed(seed)
    _w = jnp.asarray

    def _L0_attn_setup():
        import jax, jax.numpy as jnp
        import numpy as np
        H = 16
        KVH = 4
        D = 128
        HID = 512
        EPS = 1e-06
        GROUPS = H // KVH

        def elu_plus_one(x):
            return jax.nn.elu(x) + 1.0

        def _repeat_kv(x, b, s):
            x = x.reshape(b, s, KVH, 1, D)
            x = jnp.broadcast_to(x, (b, s, KVH, GROUPS, D))
            return x.reshape(b, s, H * D)

        def _split_heads(x, b, s, nh):
            return x.reshape(b, s, nh, D).transpose(0, 2, 1, 3)
        key = jax.random.key(seed)
        ks = jax.random.split(key, 8)
        s = 0.02
        return {'hidden_states': jax.random.normal(ks[0], (2, 1024, HID), jnp.float32), 'Wq': jax.random.normal(ks[1], (H * D, HID), jnp.float32) * s, 'bq': jnp.zeros((H * D,), jnp.float32), 'Wk': jax.random.normal(ks[2], (KVH * D, HID), jnp.float32) * s, 'bk': jnp.zeros((KVH * D,), jnp.float32), 'Wv': jax.random.normal(ks[3], (KVH * D, HID), jnp.float32) * s, 'bv': jnp.zeros((KVH * D,), jnp.float32), 'Wo': jax.random.normal(ks[4], (HID, H * D), jnp.float32) * s}
    _L0_attn_in = _L0_attn_setup()

    def _L0_ffn_setup():
        import jax, jax.numpy as jnp
        import numpy as np
        D = 512
        H = 352
        E = 8
        TOP_K = 2
        B, S = (4, 512)

        def _swiglu(x, Wg, Wu, Wd):
            return jax.nn.silu(x @ Wg) * (x @ Wu) @ Wd
        key = jax.random.key(seed)
        ks = jax.random.split(key, 10)
        sc = 0.02
        x = jax.random.normal(ks[0], (B, S, D), dtype=jnp.float32)
        Wg_s = jax.random.normal(ks[1], (D, H), dtype=jnp.float32) * sc
        Wu_s = jax.random.normal(ks[2], (D, H), dtype=jnp.float32) * sc
        Wd_s = jax.random.normal(ks[3], (H, D), dtype=jnp.float32) * sc
        Wg = jax.random.normal(ks[4], (E, D, H), dtype=jnp.float32) * sc
        Wu = jax.random.normal(ks[5], (E, D, H), dtype=jnp.float32) * sc
        Wd = jax.random.normal(ks[6], (E, H, D), dtype=jnp.float32) * sc
        Wr = jax.random.normal(ks[7], (D, E), dtype=jnp.float32) * sc
        br = jax.random.normal(ks[8], (E,), dtype=jnp.float32) * sc
        rb = jnp.zeros((E,), dtype=jnp.float32)
        return {'x': x, 'Wg_s': Wg_s, 'Wu_s': Wu_s, 'Wd_s': Wd_s, 'Wg': Wg, 'Wu': Wu, 'Wd': Wd, 'Wr': Wr, 'br': br, 'rb': rb}
    _L0_ffn_in = _L0_ffn_setup()
    _L0_c = _w((lambda *s: np.random.randn(*s).astype(np.float32) * 0.05)(4, 512))
    _L0_wmod = _w((lambda *s: np.random.randn(*s).astype(np.float32) * 0.05)(512, 6 * 512) * 512 ** (-0.5))
    _d = {'L0_attn_hidden_states': _L0_attn_in['hidden_states'], 'L0_attn_Wq': _L0_attn_in['Wq'], 'L0_attn_bq': _L0_attn_in['bq'], 'L0_attn_Wk': _L0_attn_in['Wk'], 'L0_attn_bk': _L0_attn_in['bk'], 'L0_attn_Wv': _L0_attn_in['Wv'], 'L0_attn_bv': _L0_attn_in['bv'], 'L0_attn_Wo': _L0_attn_in['Wo'], 'L0_ffn_Wg_s': _L0_ffn_in['Wg_s'], 'L0_ffn_Wu_s': _L0_ffn_in['Wu_s'], 'L0_ffn_Wd_s': _L0_ffn_in['Wd_s'], 'L0_ffn_Wg': _L0_ffn_in['Wg'], 'L0_ffn_Wu': _L0_ffn_in['Wu'], 'L0_ffn_Wd': _L0_ffn_in['Wd'], 'L0_ffn_Wr': _L0_ffn_in['Wr'], 'L0_ffn_br': _L0_ffn_in['br'], 'L0_ffn_rb': _L0_ffn_in['rb'], 'L0_c': _L0_c, 'L0_wmod': _L0_wmod}
    _x0 = _d['L0_attn_hidden_states']
    _d['L0_attn_hidden_states'] = jax.random.normal(jax.random.fold_in(jax.random.key(seed), 1), (4, 1024, 512), dtype=_x0.dtype)
    del _x0
    return _d

def reference(L0_attn_hidden_states, L0_attn_Wq, L0_attn_bq, L0_attn_Wk, L0_attn_bk, L0_attn_Wv, L0_attn_bv, L0_attn_Wo, L0_ffn_Wg_s, L0_ffn_Wu_s, L0_ffn_Wd_s, L0_ffn_Wg, L0_ffn_Wu, L0_ffn_Wd, L0_ffn_Wr, L0_ffn_br, L0_ffn_rb, L0_c, L0_wmod):

    def _L0_attn_ref(hidden_states, Wq, bq, Wk, bk, Wv, bv, Wo):
        import jax, jax.numpy as jnp
        import numpy as np
        H = 16
        KVH = 4
        D = 128
        HID = 512
        EPS = 1e-06
        GROUPS = H // KVH

        def elu_plus_one(x):
            return jax.nn.elu(x) + 1.0

        def _repeat_kv(x, b, s):
            x = x.reshape(b, s, KVH, 1, D)
            x = jnp.broadcast_to(x, (b, s, KVH, GROUPS, D))
            return x.reshape(b, s, H * D)

        def _split_heads(x, b, s, nh):
            return x.reshape(b, s, nh, D).transpose(0, 2, 1, 3)
        b, s, _ = hidden_states.shape
        q = hidden_states @ Wq.T + bq
        k = hidden_states @ Wk.T + bk
        v = hidden_states @ Wv.T + bv
        k = _repeat_kv(k, b, s)
        v = _repeat_kv(v, b, s)
        q = _split_heads(q, b, s, H)
        k = _split_heads(k, b, s, H)
        v = _split_heads(v, b, s, H)
        sq = elu_plus_one(q)
        sk = elu_plus_one(k)
        kv = jnp.einsum('bhsd,bhse->bhde', sk, v)
        qkv = jnp.einsum('bhsd,bhde->bhse', sq, kv)
        k_sum = sk.sum(axis=2)
        norm = jnp.einsum('bhsd,bhd->bhs', sq, k_sum)
        attn = qkv / (norm[..., None] + EPS)
        attn = attn.transpose(0, 2, 1, 3).reshape(b, s, H * D)
        return attn @ Wo.T

    def _L0_ffn_ref(x, Wg_s, Wu_s, Wd_s, Wg, Wu, Wd, Wr, br, rb):
        import jax, jax.numpy as jnp
        import numpy as np
        D = 512
        H = 352
        E = 8
        TOP_K = 2
        B, S = (4, 512)

        def _swiglu(x, Wg, Wu, Wd):
            return jax.nn.silu(x @ Wg) * (x @ Wu) @ Wd
        shared_out = _swiglu(x, Wg_s, Wu_s, Wd_s)
        logits = x @ Wr + br + rb
        probs = jax.nn.sigmoid(logits)
        top_v, top_i = jax.lax.top_k(probs, TOP_K)
        top_v = top_v / jnp.sum(top_v, axis=-1, keepdims=True)
        w = jnp.sum(top_v[..., None] * jax.nn.one_hot(top_i, E, dtype=x.dtype), axis=-2)
        routed_out = jnp.zeros_like(x)
        for e in range(E):
            routed_out = routed_out + _swiglu(x, Wg[e], Wu[e], Wd[e]) * w[..., e:e + 1]
        return shared_out + routed_out
    x = L0_attn_hidden_states
    mod = (_silu(L0_c) @ L0_wmod).reshape(L0_c.shape[0], 6, 1, -1)
    sa, ca, ga, sb, cb, gb = (mod[:, 0], mod[:, 1], mod[:, 2], mod[:, 3], mod[:, 4], mod[:, 5])
    ga = (2 * (ga >= 0) - 1) * jnp.maximum(jnp.abs(ga), 0.25)
    gb = (2 * (gb >= 0) - 1) * jnp.maximum(jnp.abs(gb), 0.25)
    h = _layernorm(x, axis=-1) * (1 + ca) + sa
    x = x + ga * _L0_attn_ref(h, L0_attn_Wq, L0_attn_bq, L0_attn_Wk, L0_attn_bk, L0_attn_Wv, L0_attn_bv, L0_attn_Wo)
    h = _layernorm(x, axis=-1) * (1 + cb) + sb
    x = x + gb * _L0_ffn_ref(h, L0_ffn_Wg_s, L0_ffn_Wu_s, L0_ffn_Wd_s, L0_ffn_Wg, L0_ffn_Wu, L0_ffn_Wd, L0_ffn_Wr, L0_ffn_br, L0_ffn_rb)
    return x

_drawn_inputs = setup_inputs


def setup_inputs(seed=0):
    import zlib

    import numpy as np

    out = dict(_drawn_inputs(seed))
    spreads = {'L0_attn_bq': (0.0, 0.8),
     'L0_attn_bk': (0.0, 2.0),
     'L0_attn_bv': (0.0, 0.377),
     'L0_ffn_rb': (0.0, 0.8)}
    factors = {'L0_attn_Wq': 8.0,
     'L0_attn_Wk': 8.0,
     'L0_attn_Wv': 8.0,
     'L0_ffn_Wg_s': 5.693,
     'L0_ffn_Wu_s': 5.589,
     'L0_ffn_Wd_s': 5.569,
     'L0_ffn_Wg': 7.999,
     'L0_ffn_Wu': 7.85,
     'L0_ffn_Wd': 7.841,
     'L0_ffn_Wr': 8.0,
     'L0_ffn_br': 8.0}
    for name, (base, spread) in spreads.items():
        noise = np.random.default_rng([zlib.crc32(name.encode()), seed]).standard_normal(out[name].shape)
        drawn = base * np.exp(spread * noise) if base else spread * noise
        out[name] = jnp.asarray(drawn.astype(out[name].dtype))
    for name, factor in factors.items():
        out[name] = (out[name] * factor).astype(out[name].dtype)
    return out
```

```python
from contextlib import ExitStack

import numpy as np

import concourse.bass as bass
from concourse import mybir

F32 = mybir.dt.float32
F32R = mybir.dt.float32r
I32 = mybir.dt.int32
U32 = mybir.dt.uint32
ALU = mybir.AluOpType
ACT = mybir.ActivationFunctionType
AX_X = mybir.AxisListType.X

P = 128
B, S, D = 4, 1024, 512
HEADS, KVH = 16, 4
GROUP = HEADS // KVH
KC = D // P
BLK = 512
TB = BLK // P
BB = S // BLK
TPB = S // P
TOK = B * S
TILES = TOK // P
EXPERTS, TOPK, FF = 8, 2, 352
FCH = [P, P, FF - 2 * P]
LN_EPS, NORM_EPS = 1e-5, 1e-6
MAG = 0.25
SA, CA, GA, SB, CB, GB = range(6)
ROWS = [GA, SB, CB, GB]
R_GA, R_SB, R_CB, R_GB = range(4)


class Count:

    def __init__(self, sem, head):
        self.sem = sem
        self.head = head

    def start(self, eng):
        eng.sem_inc(self.sem, self.head)

    def wait(self, eng, n):
        eng.wait_ge(self.sem, n + self.head)


class Stage(ExitStack):

    def __init__(self, nc, name):
        super().__init__()
        self.nc, self.name, self.sems = nc, name, []

    def sem(self, name):
        self.sems.append(self.enter_context(self.nc.semaphore(f"{self.name}_{name}")))
        return self.sems[-1]

    def count(self, name, head=0):
        return Count(self.sem(name), head)

    def clear(self):
        with self.nc.Block() as block:
            @block.gpsimd
            def _(pool):
                for s in self.sems:
                    pool.sem_clear(s)

    def block(self):
        self.callback(self.clear)
        return self.enter_context(self.nc.Block())


def setup(nc, io, keep):
    with Stage(nc, "set") as ctx:
        sem = ctx.sem

        def sb(name, shape, dt=F32):
            return ctx.enter_context(nc.sbuf_tensor(name, shape, dt))

        wkv_raw = sb("wkv_raw", [P, 2, KC, D])
        wmod = sb("wmod", [P, 3, KC, 2 * D])
        cT = sb("cT", [P, KC * B])
        den = sb("den", [P, KC * B])
        sc = sb("sc", [P, KC, B])
        rows = sb("rows", [B, len(ROWS), D])
        gabs = sb("gabs", [B, 2, D])
        mag = sb("mag", [B, 2, D])
        sgn = sb("sgn", [B, 2, D])
        ones_f = sb("ones_f", [P, P])
        psR = ctx.enter_context(nc.psum_tensor("psR", [P, 4, D], F32))
        psC = ctx.enter_context(nc.psum_tensor("psC", [P, D], F32))

        c_in = sem("c_in")
        wmod_in = [sem(f"wmod_in{n}") for n in range(3)]
        wkv_in = [sem(f"wkv_in{n}") for n in range(2)]
        e_done, den_done, rec_done, sc_done = sem("e_done"), sem("den_done"), sem("rec_done"), sem("sc_done")
        ident_zero, ident_done = sem("ident_zero"), sem("ident_done")
        ones_set, ones_done = sem("ones_set"), sem("ones_done")
        rows_mm, cols_mm = sem("rows_mm"), sem("cols_mm")
        abs_done, mag_done, sgn_done, rows_done = sem("abs_done"), sem("mag_done"), sem("sgn_done"), sem("rows_done")
        cols_done = sem("cols_done")
        hi_done, lo_done = sem("hi_done"), sem("lo_done")
        rows_out = sem("rows_out")
        block = ctx.block()

        @block.sync
        def _(sp):
            sp.dma_start(cT[:, :], io["cT"]).then_inc(c_in, 16)
            for n in range(2):
                sp.dma_start(wkv_raw[:, n], io["wkvT"][:, n]).then_inc(wkv_in[n], 16)
            for n in range(3):
                sp.dma_start(wmod[:, n], io["wmod"][:, n]).then_inc(wmod_in[n], 16)
            sp.wait_ge(rows_done, 4)
            sp.dma_start(io["modrows"].rearrange("v b d -> b v d"), rows[:, :, :]).then_inc(rows_out, 16)
            sp.wait_ge(rows_out, 16)

        @block.gpsimd
        def _(pool):
            pool.memset(keep["ident"][:, :], 0.0).then_inc(ident_zero, 1)
            pool.wait_ge(ident_zero, 1)
            pool.affine_select(out=keep["ident"][:, :], in_=keep["ident"][:, :], compare_op=ALU.not_equal, fill=1.0,
                               base=0, pattern=[[-1, P]], channel_multiplier=1).then_inc(ident_done, 1)

        @block.scalar
        def _(act):
            act.wait_ge(c_in, 16)
            act.activation(den[:, :], cT[:, :], ACT.Exp, scale=-1.0).then_inc(e_done, 1)
            for n in range(2):
                act.wait_ge(wkv_in[n], 16)
                act.activation(keep["wkv_hi"][:, n], wkv_raw[:, n], ACT.Copy).then_inc(hi_done, 1)
            act.wait_ge(rows_mm, 4)
            for n, v in enumerate((R_GA, R_GB)):
                act.activation(gabs[:, n], psR[0:B, v], ACT.Abs).then_inc(abs_done, 1)

        @block.vector
        def _(dve):
            dve.memset(ones_f[:, :], 1.0).then_inc(ones_set, 1)
            dve.wait_ge(ones_set, 1)
            dve.tensor_copy(keep["ones"][:, :], ones_f[:, :]).then_inc(ones_done, 1)
            dve.wait_ge(e_done, 1)
            dve.tensor_scalar_add(den[:, :], den[:, :], 1.0).then_inc(den_done, 1)
            dve.wait_ge(den_done, 1)
            dve.reciprocal(den[:, :], den[:, :]).then_inc(rec_done, 1)
            dve.wait_ge(rec_done, 1)
            dve.tensor_tensor(sc[:, :, :].rearrange("p c b -> p (c b)"), cT[:, :], den[:, :], ALU.mult).then_inc(sc_done, 1)
            for n in range(2):
                dve.wait_ge(hi_done, n + 1)
                dve.tensor_tensor(keep["wkv_lo"][:, n], wkv_raw[:, n], keep["wkv_hi"][:, n].bitcast(F32),
                                  ALU.subtract).then_inc(lo_done, 1)
            dve.wait_ge(cols_mm, 2)
            cols = psC[:, 0:2 * KC * B].rearrange("p (v n b) -> p b v n", v=2, n=KC)
            dve.tensor_copy(keep["modc"][:, :, SA], cols[:, :, SA]).then_inc(cols_done, 1)
            dve.tensor_scalar_add(keep["modc"][:, :, CA], cols[:, :, CA], 1.0).then_inc(cols_done, 1)
            dve.wait_ge(rows_mm, 4)
            dve.tensor_copy(rows[:, R_SB], psR[0:B, R_SB]).then_inc(rows_done, 1)
            dve.tensor_scalar_add(rows[:, R_CB], psR[0:B, R_CB], 1.0).then_inc(rows_done, 1)
            for n, v in enumerate((R_GA, R_GB)):
                dve.wait_ge(abs_done, n + 1)
                dve.tensor_scalar_max(mag[:, n], gabs[:, n], MAG).then_inc(mag_done, 1)
                dve.tensor_scalar(sgn[:, n], psR[0:B, v], 0.0, 2.0, ALU.is_ge, ALU.mult).then_inc(sgn_done, 1)
                dve.wait_ge(mag_done, n + 1)
                dve.wait_ge(sgn_done, n + 1)
                dve.scalar_tensor_tensor(rows[:, v], sgn[:, n], -1.0, mag[:, n], ALU.add, ALU.mult).then_inc(rows_done, 1)

        @block.tensor
        def _(pe):
            pe.wait_ge(sc_done, 1)
            pe.wait_ge(wmod_in[0], 16)
            for v in (SA, CA):
                for n in range(KC):
                    at = (v * KC + n) * B
                    for c in range(KC):
                        last = pe.matmul(psC[:, at:at + B], wmod[:, 0, c, v * D + n * P:v * D + (n + 1) * P],
                                         sc[:, c, :], start=(c == 0), stop=(c == KC - 1))
                last.then_inc(cols_mm, 1)
            for r, v in enumerate(ROWS):
                pe.wait_ge(wmod_in[v // 2], 16)
                for c in range(KC):
                    last = pe.matmul(psR[0:B, r], sc[:, c, :], wmod[:, v // 2, c, (v % 2) * D:(v % 2 + 1) * D],
                                     start=(c == 0), stop=(c == KC - 1))
                last.then_inc(rows_mm, 1)


def keys_values(nc, io, keep):
    with Stage(nc, "kv") as ctx:
        sem, count = ctx.sem, ctx.count

        def sb(name, shape, dt=F32):
            return ctx.enter_context(nc.sbuf_tensor(name, shape, dt))

        def psum(name, shape):
            return ctx.enter_context(nc.psum_tensor(name, shape, F32))

        QW = 4
        hT = [sb(f"hT{q}", [P, 2, KC, BLK], F32R) for q in range(BB)]
        xt = sb("xt", [P, TB, D])
        zt = sb("zt", [P, TB, D])
        st = sb("st", [P, TB, 6])
        mv = sb("mv", [P, TB, 2])
        spare = sb("spare", [P, 1])
        var = sb("var", [P, TB])
        sd = sb("sd", [P, TB])
        rstd = sb("rstd", [P, TB])
        nmr = sb("nmr", [P, TB])
        hf = sb("hf", [P, 2, BLK])
        bkv = sb("bkv", [P, 2, D])
        kb = sb("kb", [P, D])
        uk = sb("uk", [P, D])
        ek = sb("ek", [P, D])
        rk = sb("rk", [P, D])
        kf = sb("kf", [P, D])
        vf = sb("vf", [P, D])
        kvs = sb("kvs", [P, 2, 2, P])
        ksb = sb("ksb", [P, D])
        kr = sb("kr", [P, 2, 2, D], F32R)
        vr = sb("vr", [P, 2, 2, D], F32R)
        wq_raw = sb("wq_raw", [P, QW, KC, P])
        psT = [psum(f"psT{n}", [P, BLK]) for n in range(2)]
        psK = [psum(f"psK{n}", [P, D]) for n in range(2)]
        psV = psum("psV", [P, D])
        psKV = [psum(f"psKV{n}", [P, D]) for n in range(2)]
        psS = psum("psS", [P, D])

        bkv_in, x_in, wq_in = sem("bkv_in"), sem("x_in"), sem("wq_in")
        hT_out = [sem(f"hT_out{q}") for q in range(BB)]
        x_used = count("x_used", 1)
        bn_done, ag_done, var_done = count("bn_done"), count("ag_done", 1), count("var_done")
        sd_done, rstd_done, nmr_done = count("sd_done"), count("rstd_done"), count("nmr_done", 1)
        z_done = count("z_done")
        tr_done = count("tr_done", KC)
        hf_done = count("hf_done", 2)
        hi_done = count("h_hi_done")
        lo_done = count("h_lo_done", 2)
        k_mm, v_mm = count("k_mm"), count("v_mm", TB + 1)
        kb_done = count("kb_done", 2)
        vb_done = count("vb_done", 2)
        u_done = count("u_done")
        er_done = count("er_done", 1)
        k_done = count("k_done", 1)
        k_hi, k_lo = count("k_hi"), count("k_lo", 1)
        v_hi, v_lo = count("v_hi"), count("v_lo", 1)
        kv_mm = count("kv_mm", 2)
        sums_done = count("sums_done", 5)
        ks_mm = count("ks_mm")
        wqh_done, wql_done = count("wqh_done"), count("wql_done", 1)

        block = ctx.block()
        x_blocks = io["x"].rearrange("(g j p) d -> g p j d", j=TB, p=P)


        @block.sync
        def _(sp):
            def load_x(g):
                x_used.wait(sp, g)
                sp.dma_start(xt[:, :, :], x_blocks[g]).then_inc(x_in, 16)

            def store_h(i, q):
                lo_done.wait(sp, KC * (BB * i + q + 1))
                sp.dma_start(io["hTs"][BB * i + q], hT[q][:, :, :, :].bitcast(F32)).then_inc(hT_out[q], 16)

            for n, name in enumerate(("bk", "bv")):
                sp.dma_start(bkv[:, n], io[name].partition_broadcast(P)).then_inc(bkv_in, 16)
            for q in range(BB):
                sp.sem_inc(hT_out[q], 16)
            load_x(0)
            load_x(1)
            with sp.Fori(0, B - 1) as i:
                store_h(i, 0)
                load_x(BB * i + 2)
                store_h(i, 1)
                load_x(BB * i + 3)
            store_h(B - 1, 0)
            store_h(B - 1, 1)
            for q in range(BB):
                sp.wait_ge(hT_out[q], 16 * (B + 1))

        @block.gpsimd
        def _(pool):
            wql_done.start(pool)
            for n in range(HEADS // QW):
                part = slice(QW * n, QW * (n + 1))
                wql_done.wait(pool, n)
                pool.dma_start(wq_raw[:, :, :, :], io["wqT"][:, part]).then_inc(wq_in, 16)
                pool.wait_ge(wq_in, 16 * (n + 1))
                pool.tensor_copy(keep["wq_hi"][:, part], wq_raw[:, :, :, :]).then_inc(wqh_done.sem, 1)
                wqh_done.wait(pool, n + 1)
                pool.tensor_tensor(keep["wq_lo"][:, part], wq_raw[:, :, :, :], keep["wq_hi"][:, part].bitcast(F32),
                                   ALU.subtract).then_inc(wql_done.sem, 1)

        @block.scalar
        def _(act):
            def front_norm(g):
                var_done.wait(act, g + 1)
                act.activation(sd[:, :], var[:, :], ACT.Sqrt).then_inc(sd_done.sem, 1)
                nmr_done.wait(act, g + 1)
                tr_done.wait(act, KC * g)
                for j in range(TB):
                    done = act.activation(zt[:, j], xt[:, j], ACT.Identity, bias=nmr[:, j:j + 1],
                                          scale=rstd[:, j:j + 1]).then_inc(z_done.sem, 1)

            def front_free(g):
                z_done.wait(act, TB * (g + 1))
                act.sem_inc(x_used.sem, 1)

            def front_hi(g, q, chunks, out_wait):
                for c in chunks:
                    if c == 0:
                        act.wait_ge(hT_out[q], out_wait)
                        v_mm.wait(act, TB * g - TB)
                    hf_done.wait(act, KC * g + c + 1)
                    act.activation(hT[q][:, 0, c], hf[:, c % 2], ACT.Copy).then_inc(hi_done.sem, 1)

            def tile(t, tt):
                kb_done.wait(act, t + 1)
                k_done.wait(act, t)
                er_done.wait(act, t)
                act.activation(uk[:, :], kb[:, :], ACT.Relu, scale=-1.0).then_inc(u_done.sem, 1)
                act.activation(rk[:, :], kb[:, :], ACT.Relu)
                u_done.wait(act, t + 1)
                act.activation(ek[:, :], uk[:, :], ACT.Exp, scale=-1.0).then_inc(er_done.sem, 1)
                vb_done.wait(act, t + 1)
                kv_mm.wait(act, t - 1)
                act.activation(vr[:, tt % 2, 0], vf[:, :], ACT.Copy).then_inc(v_hi.sem, 1)
                k_done.wait(act, t + 1)
                act.activation(kr[:, tt % 2, 0], kf[:, :], ACT.Copy).then_inc(k_hi.sem, 1)

            x_used.start(act)
            er_done.start(act)
            front_norm(0)
            front_free(0)
            front_hi(0, 0, range(KC), 16)

            def batch(i, last):
                for q in range(BB):
                    for j in range(TB):
                        tt = q * TB + j
                        tile(TPB * i + tt, tt)
                        ahead = not (last and q == BB - 1)
                        nq, ng = (q + 1) % BB, BB * i + q + 1
                        if ahead and j == 0:
                            front_norm(ng)
                        if ahead and j == 1:
                            front_free(ng)
                        if ahead and j in (1, 2):
                            front_hi(ng, nq, range(2 * (j - 1), 2 * j), 16 * (i + 1 + (q + 1) // BB))

            with act.Fori(0, B - 1) as i:
                batch(i, False)
            batch(B - 1, True)

        @block.vector
        def _(dve):
            def front_stats(g):
                dve.wait_ge(x_in, 16 * (g + 1))
                ag_done.wait(dve, TB * g)
                for j in range(TB):
                    dve.bn_stats(st[:, j], xt[:, j]).then_inc(bn_done.sem, 1)
                bn_done.wait(dve, TB * (g + 1))
                nmr_done.wait(dve, g)
                dve.memset(spare[:, :], 0.0)
                for j in range(TB):
                    dve.bn_aggr(mv[:, j], st[:, j]).then_inc(ag_done.sem, 1)
                ag_done.wait(dve, TB * (g + 1))
                dve.tensor_scalar_add(var[:, :], mv[:, :, 1], LN_EPS).then_inc(var_done.sem, 1)
                sd_done.wait(dve, g + 1)
                dve.reciprocal(rstd[:, :], sd[:, :]).then_inc(rstd_done.sem, 1)
                rstd_done.wait(dve, g + 1)
                dve.scalar_tensor_tensor(nmr[:, :], mv[:, :, 0], -1.0, rstd[:, :], ALU.mult, ALU.mult)\
                   .then_inc(nmr_done.sem, 1)

            def front_split(g, b, q, chunks):
                for c in chunks:
                    tr_done.wait(dve, KC * g + c + 1)
                    lo_done.wait(dve, KC * g + c - 1)
                    dve.tensor_scalar(hf[:, c % 2], psT[c % 2][:, :], keep["modc"][:, b, CA, c:c + 1],
                                      keep["modc"][:, b, SA, c:c + 1], ALU.mult, ALU.add).then_inc(hf_done.sem, 1)
                for c in chunks:
                    hi_done.wait(dve, KC * g + c + 1)
                    dve.tensor_tensor(hT[q][:, 1, c], hf[:, c % 2], hT[q][:, 0, c].bitcast(F32),
                                      ALU.subtract).then_inc(lo_done.sem, 1)

            def tile(t, tt):
                k_mm.wait(dve, t + 1)
                er_done.wait(dve, t)
                dve.tensor_tensor(kb[:, :], psK[tt % 2][:, :], bkv[:, 0], ALU.add).then_inc(kb_done.sem, 1)
                v_mm.wait(dve, t + 1)
                v_lo.wait(dve, t)
                dve.tensor_tensor(vf[:, :], psV[:, :], bkv[:, 1], ALU.add).then_inc(vb_done.sem, 1)
                er_done.wait(dve, t + 1)
                k_lo.wait(dve, t)
                dve.tensor_tensor(kf[:, :], ek[:, :], rk[:, :], ALU.add).then_inc(k_done.sem, 1)
                v_hi.wait(dve, t + 1)
                kv_mm.wait(dve, t - 1)
                dve.tensor_tensor(vr[:, tt % 2, 1], vf[:, :], vr[:, tt % 2, 0].bitcast(F32),
                                  ALU.subtract).then_inc(v_lo.sem, 1)
                k_hi.wait(dve, t + 1)
                dve.tensor_tensor(kr[:, tt % 2, 1], kf[:, :], kr[:, tt % 2, 0].bitcast(F32),
                                  ALU.subtract).then_inc(k_lo.sem, 1)

            def sums(i):
                kv_mm.wait(dve, TPB * (i + 1))
                dve.tensor_copy(ksb[:, :], psS[:, :])
                for n in range(2):
                    pair = psKV[n][:, :].rearrange("p (h w d) -> p h w d", h=2, w=2)
                    dve.tensor_copy(kvs[:, n], pair[:, :, 0]).then_inc(sums_done.sem, 1)
                sums_done.wait(dve, 5 * i + 2)
                for n in range(2):
                    pair = psKV[n][:, :].rearrange("p (h w d) -> p h w d", h=2, w=2)
                    last = dve.tensor_tensor(keep["kvT"][:, i, 2 * n * P:2 * (n + 1) * P].rearrange("p (h d) -> p h d", h=2),
                                             kvs[:, n], pair[:, :, 1], ALU.add)
                last.then_inc(sums_done.sem, 1)
                ks_mm.wait(dve, i + 1)
                cols = psS[:, :].rearrange("p (h m) -> p h m", h=KVH)[:, :, 0:2]
                hi = keep["ks_hi"][:, i].rearrange("p (h m) -> p h m", m=2)
                lo = keep["ks_lo"][:, i].rearrange("p (h m) -> p h m", m=2)
                dve.tensor_scalar_mul(hi, cols, 1.0).then_inc(sums_done.sem, 1)
                sums_done.wait(dve, 5 * i + 4)
                dve.tensor_tensor(lo, cols, hi.bitcast(F32), ALU.subtract).then_inc(sums_done.sem, 1)

            for x in (hf_done, lo_done, kb_done, vb_done, k_done, k_lo, v_lo, sums_done, ag_done, nmr_done):
                x.start(dve)
            dve.wait_ge(bkv_in, 32)
            front_stats(0)
            front_split(0, 0, 0, (0, 1))
            front_split(0, 0, 0, (2, 3))

            def batch(i, last):
                for q in range(BB):
                    for j in range(TB):
                        tt = q * TB + j
                        tile(TPB * i + tt, tt)
                        ahead = not (last and q == BB - 1)
                        nq, ng = (q + 1) % BB, BB * i + q + 1
                        if ahead and j == 0:
                            front_stats(ng)
                        if ahead and j in (1, 2):
                            front_split(ng, i + (q + 1) // BB, nq, range(2 * (j - 1), 2 * j))
                sums(i)

            with dve.Fori(0, B - 1) as i:
                batch(i, False)
            batch(B - 1, True)

        @block.tensor
        def _(pe):
            def front_transpose(g, chunks):
                for c in chunks:
                    if c == 0:
                        z_done.wait(pe, TB * (g + 1))
                    hf_done.wait(pe, KC * g + c - 1)
                    for j in range(TB):
                        last = pe.transpose(psT[c % 2][:, j * P:(j + 1) * P], zt[:, j, c * P:(c + 1) * P],
                                            keep["ident"][:, :])
                    last.then_inc(tr_done.sem, 1)

            def tile(t, q, j):
                tt = q * TB + j
                tok = slice(j * P, (j + 1) * P)
                for n, (ps, free, done) in enumerate(((psK[tt % 2], kb_done, k_mm), (psV, vb_done, v_mm))):
                    free.wait(pe, t - 1 if n == 0 else t)
                    todo = [(a, w, c) for c in range(KC) for a, w in ((0, 0), (0, 1), (1, 0))]
                    for m, (a, w, c) in enumerate(todo):
                        wt = keep["wkv_lo" if w else "wkv_hi"]
                        last = pe.matmul(ps[:, :], hT[q][:, a, c, tok], wt[:, n, c],
                                         start=(m == 0), stop=(m == len(todo) - 1))
                    last.then_inc(done.sem, 1)

            def sums(t, tt):
                k_lo.wait(pe, t + 1)
                v_lo.wait(pe, t + 1)
                first, end = tt == 0, tt == TPB - 1
                k, v = kr[:, tt % 2], vr[:, tt % 2]
                for h in range(KVH):
                    at = slice(h * P, (h + 1) * P)
                    ps = psKV[h // 2][:, 2 * P * (h % 2):2 * P * (h % 2 + 1)]
                    pe.matmul(ps, v[:, 0, at], k[:, :, at], start=(first and h % 2 == 0), stop=False,
                              skip_group_check=True)
                    pe.matmul(ps[:, P:2 * P], v[:, 1, at], k[:, 0, at], start=False, stop=end,
                              skip_group_check=True)
                for a in range(2):
                    last = pe.matmul(psS[:, :], keep["ones"][:, :], k[:, a], start=(first and a == 0),
                                     stop=(end and a == 1), skip_group_check=True)
                last.then_inc(kv_mm.sem, 1)

            def key_columns(i):
                sums_done.wait(pe, 5 * i + 3)
                for h in range(KVH):
                    last = pe.transpose(psS[:, h * P:(h + 1) * P], ksb[:, h * P:(h + 1) * P], keep["ident"][:, :])
                last.then_inc(ks_mm.sem, 1)

            for x in (tr_done, kv_mm, v_mm):
                x.start(pe)
            front_transpose(0, range(KC))

            def batch(i, last):
                for q in range(BB):
                    for j in range(TB):
                        tt = q * TB + j
                        t = TPB * i + tt
                        if j == 0:
                            lo_done.wait(pe, KC * (BB * i + q + 1))
                        tile(t, q, j)
                        if tt == 1:
                            sums_done.wait(pe, 5 * i)
                        if tt >= 1:
                            sums(t - 1, tt - 1)
                        ahead = not (last and q == BB - 1)
                        if ahead and j in (1, 2):
                            front_transpose(BB * i + q + 1, range(2 * (j - 1), 2 * j))
                sums(TPB * i + TPB - 1, TPB - 1)
                key_columns(i)

            with pe.Fori(0, B - 1) as i:
                batch(i, False)
            batch(B - 1, True)


def queries(nc, io, keep):
    with Stage(nc, "q") as ctx:
        sem, count = ctx.sem, ctx.count

        def sb(name, shape, dt=F32):
            return ctx.enter_context(nc.sbuf_tensor(name, shape, dt))

        def psum(name, shape):
            return ctx.enter_context(nc.psum_tensor(name, shape, F32))

        STEPS = HEADS * BB
        WR = 2
        hT = [sb(f"qhT{q}", [P, 2, KC, BLK], F32R) for q in range(BB)]
        bq = sb("bq", [P, HEADS])
        gate = sb("gate", [P, D])
        kvb = sb("kvb", [P, D])
        wo = [sb(f"wo{n}", [P, D]) for n in range(WR)]
        w2f = sb("w2f", [P, D])
        w2 = [sb(f"w2_{n}", [P, 2, D + 2], F32R) for n in range(2)]
        bqn = sb("bqn", [P, HEADS])
        uq = sb("uq", [P, BLK])
        eq = sb("eq", [P, 2, BLK])
        rq = sb("rq", [P, 2, BLK])
        qf = sb("qf", [P, 2, BLK])
        qr = sb("qr", [P, 2, 2, BLK], F32R)
        nrm = sb("nrm", [P, 2, TB])
        rn = sb("rn", [P, 2, TB])
        xin = sb("xin", [P, BB, TB, D])
        acc = sb("acc", [P, BB, TB, D])
        st = sb("st2", [P, TPB, 6])
        spare = sb("spare2", [P, 1])
        mvb = sb("mvb", [P, TPB, 2])
        mv = sb("mv2", [P, B, TPB, 2])
        sd = sb("sd2", [P, B, TPB])
        HD = D // 2
        psQ = psum("psQ", [P, BLK])
        psO1 = psum("psO1", [P, TB, HD])
        psO2 = psum("psO2", [P, TB, D])
        psW = psum("psW", [P, D])

        bq_in, gate_in = sem("bq_in"), sem("gate_in")
        wo_in = [sem(f"wo_in{n}") for n in range(WR)]
        hT_in = [sem(f"hT_in{q}") for q in range(BB)]
        xin_in = sem("xin_in")
        acc_out = [sem(f"acc_out{q}") for q in range(BB)]
        acc_stored = count("acc_stored", BB)
        bn_done, ag_done, mv_done = count("bn_done2"), count("ag_done2", 1), count("mv_done2", 1)
        var_done, sd_done, rstd_done, nmr_done = sem("var2_done"), sem("sd2_done"), sem("rstd2_done"), sem("nmr2_done")
        kvb_done = count("kvb_done")
        w2_mm = count("w2_mm", WR)
        w2f_done, w2_hi, w2_lo = count("w2f_done", 1), count("w2_hi"), count("w2_lo", 1)
        q_mm = count("q_mm", BB)
        bqn_done = sem("bqn_done")
        u_done, r_done = count("u_done"), count("r_done", 1)
        er_done, qf_done = count("eqrq_done", 3), count("qf_done", 3)
        q_hi, q_lo = count("q_hi"), count("q_lo", 2)
        nrm_done, rn_done = count("nrm_done"), count("rn_done", 2)
        o_mm = count("o_mm", 2 * TB + 1)
        acc_done = count("acc_done", TB * STEPS)

        block = ctx.block()
        x_blocks = io["x"].rearrange("(g j p) d -> g p j d", j=TB, p=P)
        x1_blocks = io["x1"].rearrange("(g j p) d -> g p j d", j=TB, p=P)

        def batches(eng, slot):
            with eng.Fori(0, B - 1) as i:
                for s in range(STEPS):
                    slot(i, s, False)
            for s in range(STEPS):
                slot(B - 1, s, True)

        def later(i, s, n, last):
            if last and s + n >= STEPS:
                return []
            return [(i + (s + n) // STEPS, (s + n) % STEPS)]

        def next_head(i, s, last):
            return [(j, t // BB) for j, t in later(i, s, BB, last) if t % BB == 0]


        @block.sync
        def _(sp):
            def load_wo(i, h):
                w2_mm.wait(sp, HEADS * i + h - WR + 1)
                sp.dma_start(wo[h % WR][:, :], io["woT"][:, h]).then_inc(wo_in[h % WR], 16)

            def load_h(i, q):
                q_mm.wait(sp, STEPS * i - (BB - 1) + q)
                sp.dma_start(hT[q][:, :, :, :].bitcast(F32), io["hTs"][BB * i + q]).then_inc(hT_in[q], 16)

            sp.dma_start(bq[:, :], io["bq"]).then_inc(bq_in, 16)
            with sp.Fori(0, B) as i:
                w2f_done.wait(sp, HEADS * i)
                sp.dma_start(gate[:, :], io["modrows"][R_GA, i].partition_broadcast(P)).then_inc(gate_in, 16)
                for h in range(WR):
                    load_wo(i, h)
                for q in range(BB):
                    load_h(i, q)
                acc_done.wait(sp, TB * STEPS * i - TB * (STEPS - BB))
                for q in range(BB):
                    sp.dma_start(xin[:, q], x_blocks[BB * i + q]).then_inc(xin_in, 16)
                for h in range(WR, HEADS):
                    load_wo(i, h)

        @block.scalar
        def _(act):
            def w2_split(i, h):
                w2f_done.wait(act, HEADS * i + h + 1)
                o_mm.wait(act, TB * (STEPS * i + BB * (h - 1)))
                act.activation(w2[h % 2][:, 0, 0:D], w2f[:, :], ACT.Copy).then_inc(w2_hi.sem, 1)

            def exps(i, s):
                n, h = STEPS * i + s, s // BB
                q_mm.wait(act, n + 1)
                er_done.wait(act, n)
                qf_done.wait(act, n - 1)
                act.activation(uq[:, :], psQ[:, :], ACT.Relu, bias=bqn[:, h:h + 1], scale=-1.0)\
                   .then_inc(u_done.sem, 1)
                act.activation(rq[:, s % 2], psQ[:, :], ACT.Relu, bias=bq[:, h:h + 1]).then_inc(r_done.sem, 1)
                u_done.wait(act, n + 1)
                act.activation(eq[:, s % 2], uq[:, :], ACT.Exp, scale=-1.0).then_inc(er_done.sem, 1)

            def upper(i, s):
                n = STEPS * i + s
                qf_done.wait(act, n + 1)
                o_mm.wait(act, TB * (n - 1))
                act.activation(qr[:, s % 2, 0], qf[:, s % 2], ACT.Copy).then_inc(q_hi.sem, 1)

            for x in (r_done, er_done):
                x.start(act)
            act.wait_ge(bq_in, 16)
            act.mul(bqn[:, :], bq[:, :], -1.0).then_inc(bqn_done, 1)
            act.wait_ge(bqn_done, 1)
            def slot(i, s, last):
                for at in later(i, s, 1, last):
                    upper(*at)
                for at in later(i, s, 2, last):
                    exps(*at)
                for at in next_head(i, s, last):
                    w2_split(*at)

            exps(0, 0)
            w2_split(0, 0)
            upper(0, 0)
            exps(0, 1)
            batches(act, slot)
            act.wait_ge(var_done, 1)
            act.activation(sd[:, :, :], sd[:, :, :], ACT.Sqrt).then_inc(sd_done, 1)

        @block.vector
        def _(dve):
            def w2_gate(i, h):
                w2_mm.wait(dve, HEADS * i + h + 1)
                w2_lo.wait(dve, HEADS * i + h)
                dve.tensor_tensor(w2f[:, :], psW[:, :], gate[:, :], ALU.mult).then_inc(w2f_done.sem, 1)

            def w2_split(i, h):
                w2_hi.wait(dve, HEADS * i + h + 1)
                if h % GROUP < 2:
                    cols = slice(2 * (h // GROUP), 2 * (h // GROUP) + 2)
                    dve.tensor_scalar_mul(w2[h % 2][:, 0, D:D + 2], keep["ks_hi"][:, i, cols].bitcast(F32), 1.0)
                    dve.tensor_scalar_mul(w2[h % 2][:, 1, D:D + 2], keep["ks_lo"][:, i, cols].bitcast(F32), 1.0)
                dve.tensor_tensor(w2[h % 2][:, 1, 0:D], w2f[:, :], w2[h % 2][:, 0, 0:D].bitcast(F32),
                                  ALU.subtract).then_inc(w2_lo.sem, 1)

            def square(i, s):
                n = STEPS * i + s
                er_done.wait(dve, n + 1)
                q_lo.wait(dve, n - 1)
                dve.tensor_tensor(qf[:, s % 2], eq[:, s % 2], rq[:, s % 2], ALU.add)\
                   .then_inc(qf_done.sem, 1)

            def lower(i, s):
                n = STEPS * i + s
                q_hi.wait(dve, n + 1)
                dve.tensor_tensor(qr[:, s % 2, 1], qf[:, s % 2], qr[:, s % 2, 0].bitcast(F32),
                                  ALU.subtract).then_inc(q_lo.sem, 1)

            def norms(i, s):
                n = STEPS * i + s
                o_mm.wait(dve, TB * (n + 1))
                rn_done.wait(dve, n - 1)
                dve.tensor_scalar_add(nrm[:, s % 2], psO2[:, :, HD], NORM_EPS).then_inc(nrm_done.sem, 1)
                nrm_done.wait(dve, n + 1)
                acc_done.wait(dve, TB * (n - 1))
                dve.reciprocal(rn[:, s % 2], nrm[:, s % 2]).then_inc(rn_done.sem, 1)

            def add(i, s):
                n, q = STEPS * i + s, s % BB
                rn_done.wait(dve, n + 1)
                if s < BB:
                    acc_stored.wait(dve, BB * (i - 1) + q + 1)
                    dve.wait_ge(xin_in, 16 * BB * (i + 1))
                else:
                    acc_done.wait(dve, TB * (n - 1))
                base = xin if s < BB else acc
                for j in range(TB):
                    for half, ps in ((slice(0, HD), psO1[:, j]), (slice(HD, D), psO2[:, j, 0:HD])):
                        last = dve.scalar_tensor_tensor(acc[:, q, j, half], ps, rn[:, s % 2, j:j + 1],
                                                        base[:, q, j, half], ALU.mult, ALU.add)
                    last.then_inc(acc_done.sem, 1)

            def next_sums(i):
                w2_mm.wait(dve, HEADS * i)
                dve.tensor_scalar_mul(kvb[:, :], keep["kvT"][:, i], 1.0).then_inc(kvb_done.sem, 1)
                dve.wait_ge(gate_in, 16 * (i + 1))

            def stats(i, q):
                acc_done.wait(dve, TB * (STEPS * i + STEPS - BB + q + 1))
                ag_done.wait(dve, TPB * i)
                for j in range(TB):
                    dve.bn_stats(st[:, q * TB + j], acc[:, q, j]).then_inc(bn_done.sem, 1)

            def aggregate(i):
                mv_done.wait(dve, i)
                bn_done.wait(dve, TPB * (i + 1))
                dve.memset(spare[:, :], 0.0)
                for t in range(TPB):
                    dve.bn_aggr(mvb[:, t], st[:, t]).then_inc(ag_done.sem, 1)
                ag_done.wait(dve, TPB * (i + 1))
                dve.tensor_copy(mv[:, i], mvb[:, :, :]).then_inc(mv_done.sem, 1)

            for x in (ag_done, mv_done, w2f_done, w2_lo, qf_done, q_lo, rn_done, acc_done):
                x.start(dve)

            def slot(i, s, last):
                for at in later(i, s, 1, last):
                    lower(*at)
                if s == STEPS - BB - 1 and not last:
                    next_sums(i + 1)
                for at in next_head(i, s, last):
                    w2_gate(*at)
                for at in later(i, s, 2, last):
                    square(*at)
                for at in next_head(i, s, last):
                    w2_split(*at)
                norms(i, s)
                add(i, s)
                if s >= STEPS - BB:
                    stats(i, s - (STEPS - BB))
                if s == STEPS - 1:
                    aggregate(i)

            next_sums(0)
            w2_gate(0, 0)
            square(0, 0)
            w2_split(0, 0)
            lower(0, 0)
            square(0, 1)
            batches(dve, slot)
            mv_done.wait(dve, B)
            mean, var = mv[:, :, :, 0], mv[:, :, :, 1]
            dve.tensor_scalar_add(sd[:, :, :], var, LN_EPS).then_inc(var_done, 1)
            dve.wait_ge(sd_done, 1)
            dve.reciprocal(keep["rstd2"][:, :, :], sd[:, :, :]).then_inc(rstd_done, 1)
            dve.wait_ge(rstd_done, 1)
            dve.scalar_tensor_tensor(keep["nmr2"][:, :, :], mean, -1.0, keep["rstd2"][:, :, :], ALU.mult, ALU.mult)\
               .then_inc(nmr_done, 1)

        @block.tensor
        def _(pe):
            def query(i, s):
                n, h, q = STEPS * i + s, s // BB, s % BB
                if s < BB:
                    pe.wait_ge(hT_in[q], 16 * (i + 1))
                r_done.wait(pe, n)
                todo = [(w, a, c) for c in range(KC) for w, a in ((0, 0), (0, 1), (1, 0))]
                for m, (w, a, c) in enumerate(todo):
                    wt = keep["wq_lo" if w else "wq_hi"]
                    last = pe.matmul(psQ[:, :], wt[:, h, c], hT[q][:, a, c],
                                     start=(m == 0), stop=(m == len(todo) - 1))
                last.then_inc(q_mm.sem, 1)

            def weight(i, h):
                pe.wait_ge(wo_in[h % WR], 16 * (HEADS // WR * i + h // WR + 1))
                w2f_done.wait(pe, HEADS * i + h)
                g = h // GROUP
                pe.matmul(psW[:, :], kvb[:, g * P:(g + 1) * P], wo[h % WR][:, :], start=True, stop=True)\
                  .then_inc(w2_mm.sem, 1)

            def output(i, s):
                n, h = STEPS * i + s, s // BB
                q_lo.wait(pe, n + 1)
                w2_lo.wait(pe, HEADS * i + h + 1)
                for j in range(TB):
                    tok = slice(j * P, (j + 1) * P)
                    if j == 0:
                        acc_done.wait(pe, TB * (n - 1) + 2)
                    elif j == 1 or j == 3:
                        acc_done.wait(pe, TB * (n - 1) + j + 1)
                    elif j == 2:
                        acc_done.wait(pe, TB * n)
                    for half, ps in ((slice(0, HD), psO1[:, j]), (slice(HD, D + 2), psO2[:, j, 0:HD + 2])):
                        for m, (a, w) in enumerate(((0, 0), (0, 1), (1, 0))):
                            last = pe.matmul(ps, qr[:, s % 2, a, tok], w2[h % 2][:, w, half],
                                             start=(m == 0), stop=(m == 2))
                    last.then_inc(o_mm.sem, 1)

            for x in (w2_mm, q_mm, o_mm):
                x.start(pe)

            def slot(i, s, last):
                for j, h in next_head(i, s, last):
                    if h == 0:
                        kvb_done.wait(pe, j + 1)
                    weight(j, h)
                for at in later(i, s, 2, last):
                    query(*at)
                output(i, s)

            query(0, 0)
            kvb_done.wait(pe, 1)
            weight(0, 0)
            query(0, 1)
            batches(pe, slot)

        @block.gpsimd
        def _(pool):
            acc_stored.start(pool)
            with pool.Fori(0, B) as i:
                for q in range(BB):
                    acc_done.wait(pool, TB * (STEPS * i + STEPS - BB + q + 1))
                    pool.dma_start(x1_blocks[BB * i + q], acc[:, q]).then_inc(acc_out[q], 16)
                for q in range(BB):
                    pool.wait_ge(acc_out[q], 16 * (i + 1))
                    pool.sem_inc(acc_stored.sem, 1)


GU = 2 * FF
NF = len(FCH)
FPAD = NF * P
SLOTS = TOPK * TILES + EXPERTS


def shared_expert(nc, io, keep):
    with Stage(nc, "sh") as ctx:
        sem, count = ctx.sem, ctx.count

        def sb(name, shape, dt=F32):
            return ctx.enter_context(nc.sbuf_tensor(name, shape, dt))

        def psum(name, shape):
            return ctx.enter_context(nc.psum_tensor(name, shape, F32))

        AHEAD = 3
        XB = 4
        gu_raw = sb("gu_raw", [P, GU])
        gu = sb("gu", [P, 2, KC, GU], F32R)
        dn = sb("dn", [P, 2, NF, D], F32R)
        wr_raw = sb("wr_raw", [P, KC, EXPERTS])
        wr = sb("wr", [P, 2, KC, EXPERTS], F32R)
        rowsb = sb("rowsb", [P, 3, D])
        x1t = sb("x1t", [P, XB, D])
        h2t = sb("h2t", [P, 2, D])
        hTr = sb("hTr", [P, 2, 2, D], F32R)
        act_t = sb("act_t", [P, FPAD])
        aTr = sb("aTr", [P, 2, FPAD], F32R)
        yg = gu_raw[:, 0:D]
        psT = psum("psT_", [P, D])
        psL = psum("psL", [P, D])
        psG = psum("psG", [P, D])
        psU = psum("psU", [P, D])
        psA = psum("psA", [P, D])
        psY = [psum(f"psY{n}", [P, D]) for n in range(2)]

        gu_in = [sem(f"gu_in{c}") for c in range(KC)]
        dn_in = [sem(f"dn_in{c}") for c in range(NF)]
        wr_in = sem("wr_in")
        raw_hi, raw_lo, wr_hi, wr_lo = sem("raw_hi"), sem("raw_lo"), sem("wr_hi"), sem("wr_lo")
        pad_done = sem("pad_done")
        norm_rows_in, gate_in = sem("norm_rows_in"), sem("gate_in_")
        x_in = [sem(f"x1_in{n}") for n in range(XB)]
        h2_out = [sem(f"h2_out{n}") for n in range(2)]
        xs_out = [sem(f"xs_out{n}") for n in range(XB)]
        z_done, sc_done, h2_done = count("z2_done"), count("sc2_done", 1), count("h2_done", 1)
        t_mm, hi_done, lo_done = count("t_mm", 2), count("hi2_done"), count("lo2_done", 1)
        l_mm = count("l_mm")
        g_mm, u_mm = count("g_mm"), count("u_mm", 2)
        sil_done, a_done = count("sil_done", 1), count("a_done", 1)
        ta_mm, ahi_done, alo_done = count("ta_mm", 1), count("ahi_done"), count("alo_done", 1)
        y_mm = count("y_mm", 1)
        yg_done, xs_done = count("yg_done", 2), count("xs_done", 2)
        logits_done = sem("logits_done")

        x1_tiles = io["x1"].rearrange("(t p) d -> t p d", p=P)
        xs_tiles = io["xs"].rearrange("(t p) d -> t p d", p=P)
        h2_tiles = io["h2"].rearrange("(t p) d -> t p d", p=P)
        block = ctx.block()

        def slots(eng, step):
            with eng.Fori(0, B - 1) as i:
                for tt in range(TPB):
                    step(i, tt, False)
            for tt in range(TPB):
                step(B - 1, tt, True)

        def in_range(tt, ahead, last):
            return not last or tt + ahead < TPB


        @block.sync
        def _(sp):
            def load_x(i, tt):
                t = TPB * i + tt
                n = (tt + XB) % XB
                sp.wait_ge(xs_out[n], 16 * ((TPB // XB) * i + tt // XB + 1))
                sp.dma_start(x1t[:, n], x1_tiles[t]).then_inc(x_in[n], 16)

            def store_h2(i, tt):
                t = TPB * i + tt
                h2_done.wait(sp, t + 1)
                sp.dma_start(h2_tiles[t], h2t[:, tt % 2]).then_inc(h2_out[tt % 2], 16)

            def norm_rows(i):
                h2_done.wait(sp, TPB * i)
                for n, r in ((0, R_SB), (1, R_CB)):
                    sp.dma_start(rowsb[:, n], io["modrows"][r, i].partition_broadcast(P)).then_inc(norm_rows_in, 16)

            def step(i, tt, last):
                if tt == 0:
                    xs_done.wait(sp, TPB * i)
                    sp.dma_start(rowsb[:, 2], io["modrows"][R_GB, i].partition_broadcast(P)).then_inc(gate_in, 16)
                if tt + AHEAD == TPB and not last:
                    norm_rows(i + 1)
                if in_range(tt, AHEAD, last):
                    store_h2(i, tt + AHEAD)
                xs_done.wait(sp, TPB * i + tt + 1)
                sp.dma_start(xs_tiles[TPB * i + tt], x1t[:, tt % XB]).then_inc(xs_out[tt % XB], 16)
                if in_range(tt, XB, last):
                    load_x(i, tt + XB)

            for n in range(XB):
                sp.sem_inc(xs_out[n], 16)
            for n in range(2):
                sp.sem_inc(h2_out[n], 16)
            norm_rows(0)
            for n in range(XB):
                load_x(0, n)
            sp.dma_start(wr_raw[:, :, :], io["wr"]).then_inc(wr_in, 16)
            for c in range(KC):
                if c:
                    sp.wait_ge(raw_lo, c)
                sp.dma_start(gu_raw[:, :], io["gu_s"][:, c]).then_inc(gu_in[c], 16)
            for c in range(NF):
                sp.wait_ge(raw_lo, KC + c)
                sp.dma_start(gu_raw[0:FCH[c], 0:D], io["dn_s"][c * P:c * P + FCH[c]]).then_inc(dn_in[c], 16)
            for t in range(AHEAD):
                store_h2(0, t)
            slots(sp, step)
            for n in range(XB):
                sp.wait_ge(xs_out[n], 16 * (TILES // XB + 1))
            for n in range(2):
                sp.wait_ge(h2_out[n], 16 * (TILES // 2 + 1))

        @block.gpsimd
        def _(pool):
            for e in range(EXPERTS):
                pool.dma_start(keep["gu_e"][:, e], io["gu_e"][e]).then_inc(keep["we_in"][e], 16)
                for c in range(NF):
                    pool.dma_start(keep["dn_e"][0:FCH[c], e, c], io["dn_e"][e, c * P:c * P + FCH[c]])\
                        .then_inc(keep["we_in"][e], 16)

        @block.scalar
        def _(act):
            def norm(i, tt):
                t = TPB * i + tt
                act.wait_ge(x_in[tt % XB], 16 * ((TPB // XB) * i + tt // XB + 1))
                t_mm.wait(act, t - 1)
                act.wait_ge(h2_out[tt % 2], 16 * (TPB // 2 * i + tt // 2 + 1) )
                act.activation(h2t[:, tt % 2], x1t[:, tt % XB], ACT.Identity, bias=keep["nmr2"][:, i, tt:tt + 1],
                               scale=keep["rstd2"][:, i, tt:tt + 1]).then_inc(z_done.sem, 1)

            def upper(i, tt):
                t = TPB * i + tt
                t_mm.wait(act, t + 1)
                u_mm.wait(act, t - 1)
                act.activation(hTr[:, tt % 2, 0], psT[:, :], ACT.Copy).then_inc(hi_done.sem, 1)

            def silu(i, tt):
                t = TPB * i + tt
                g_mm.wait(act, t + 1)
                ta_mm.wait(act, t)
                act.activation(act_t[:, 0:FF], psG[:, 0:FF], ACT.Silu).then_inc(sil_done.sem, 1)

            def upper_a(i, tt):
                t = TPB * i + tt
                ta_mm.wait(act, t + 1)
                y_mm.wait(act, t)
                act.activation(aTr[:, 0], psA[:, 0:FPAD], ACT.Copy).then_inc(ahi_done.sem, 1)

            def step(i, tt, last):
                upper_a(i, tt)
                if in_range(tt, 2, last):
                    upper(*ahead(i, tt, 2))
                if in_range(tt, AHEAD, last):
                    norm(*ahead(i, tt, AHEAD))
                if in_range(tt, 1, last):
                    silu(*ahead(i, tt, 1))

            sil_done.start(act)
            act.wait_ge(pad_done, 1)
            act.wait_ge(wr_in, 16)
            act.activation(wr[:, 0], wr_raw[:, :, :], ACT.Copy).then_inc(wr_hi, 1)
            for c in range(KC):
                act.wait_ge(gu_in[c], 16)
                act.activation(gu[:, 0, c], gu_raw[:, :], ACT.Copy).then_inc(raw_hi, 1)
            for c in range(NF):
                act.wait_ge(dn_in[c], 16)
                act.activation(dn[0:FCH[c], 0, c], gu_raw[0:FCH[c], 0:D], ACT.Copy).then_inc(raw_hi, 1)
            norm(0, 0)
            norm(0, 1)
            upper(0, 0)
            norm(0, 2)
            upper(0, 1)
            silu(0, 0)
            slots(act, step)

        @block.vector
        def _(dve):
            def modulate(i, tt):
                t = TPB * i + tt
                z_done.wait(dve, t + 1)
                if tt == 0:
                    dve.wait_ge(norm_rows_in, 32 * (i + 1))
                dve.tensor_tensor(h2t[:, tt % 2], h2t[:, tt % 2], rowsb[:, 1], ALU.mult).then_inc(sc_done.sem, 1)
                sc_done.wait(dve, t + 1)
                dve.tensor_tensor(h2t[:, tt % 2], h2t[:, tt % 2], rowsb[:, 0], ALU.add).then_inc(h2_done.sem, 1)

            def lower(i, tt):
                hi_done.wait(dve, TPB * i + tt + 1)
                dve.tensor_tensor(hTr[:, tt % 2, 1], psT[:, :], hTr[:, tt % 2, 0].bitcast(F32), ALU.subtract)\
                   .then_inc(lo_done.sem, 1)

            def gated(i, tt):
                t = TPB * i + tt
                sil_done.wait(dve, t + 1)
                u_mm.wait(dve, t + 1)
                dve.tensor_tensor(act_t[:, 0:FF], act_t[:, 0:FF], psU[:, 0:FF], ALU.mult).then_inc(a_done.sem, 1)

            def lower_a(i, tt):
                ahi_done.wait(dve, TPB * i + tt + 1)
                dve.tensor_tensor(aTr[:, 1], psA[:, 0:FPAD], aTr[:, 0].bitcast(F32), ALU.subtract)\
                   .then_inc(alo_done.sem, 1)

            def add(i, tt):
                t = TPB * i + tt
                y_mm.wait(dve, t + 1)
                xs_done.wait(dve, t)
                if tt == 0:
                    dve.wait_ge(gate_in, 16 * (i + 1))
                dve.tensor_tensor(yg, psY[tt % 2][:, :], rowsb[:, 2], ALU.mult).then_inc(yg_done.sem, 1)
                yg_done.wait(dve, t + 1)
                dve.tensor_tensor(x1t[:, tt % XB], yg, x1t[:, tt % XB], ALU.add).then_inc(xs_done.sem, 1)

            def step(i, tt, last):
                lower_a(i, tt)
                if in_range(tt, 2, last):
                    lower(*ahead(i, tt, 2))
                if in_range(tt, AHEAD, last):
                    modulate(*ahead(i, tt, AHEAD))
                if in_range(tt, 1, last):
                    gated(*ahead(i, tt, 1))
                add(i, tt)

            for x in (sc_done, h2_done, lo_done, a_done, alo_done, yg_done, xs_done):
                x.start(dve)
            dve.memset(act_t[:, :], 0.0).then_inc(pad_done, 1)
            dve.wait_ge(pad_done, 1)
            dve.wait_ge(wr_hi, 1)
            dve.tensor_tensor(wr[:, 1], wr_raw[:, :, :], wr[:, 0].bitcast(F32), ALU.subtract).then_inc(wr_lo, 1)
            for c in range(KC):
                dve.wait_ge(raw_hi, c + 1)
                dve.tensor_tensor(gu[:, 1, c], gu_raw[:, :], gu[:, 0, c].bitcast(F32), ALU.subtract).then_inc(raw_lo, 1)
            for c in range(NF):
                dve.wait_ge(raw_hi, KC + c + 1)
                f = FCH[c]
                dve.tensor_tensor(dn[0:f, 1, c], gu_raw[0:f, 0:D], dn[0:f, 0, c].bitcast(F32), ALU.subtract)\
                   .then_inc(raw_lo, 1)
            modulate(0, 0)
            modulate(0, 1)
            lower(0, 0)
            modulate(0, 2)
            lower(0, 1)
            gated(0, 0)
            slots(dve, step)
            l_mm.wait(dve, TILES)
            dve.tensor_copy(keep["logits"][:, :, :].rearrange("p t e -> p (t e)"), psL[:, 0:TILES * EXPERTS])\
               .then_inc(logits_done, 1)

        @block.tensor
        def _(pe):
            def transpose_h(i, tt):
                t = TPB * i + tt
                h2_done.wait(pe, t + 1)
                lo_done.wait(pe, t)
                for c in range(KC):
                    last = pe.transpose(psT[:, c * P:(c + 1) * P], h2t[:, tt % 2, c * P:(c + 1) * P], keep["ident"][:, :])
                last.then_inc(t_mm.sem, 1)

            def logits(i, tt):
                t = TPB * i + tt
                lo_done.wait(pe, t + 1)
                todo = [(a, w, c) for c in range(KC) for a, w in ((0, 0), (0, 1), (1, 0))]
                for m, (a, w, c) in enumerate(todo):
                    last = pe.matmul(psL[:, bass.ds(t * EXPERTS, EXPERTS)], hTr[:, tt % 2, a, c * P:(c + 1) * P],
                                     wr[:, w, c], start=(m == 0), stop=(m == len(todo) - 1))
                last.then_inc(l_mm.sem, 1)

            def gate_up(i, tt):
                t = TPB * i + tt
                lo_done.wait(pe, t + 1)
                todo = [(a, w, c) for c in range(KC) for a, w in ((0, 0), (0, 1), (1, 0))]
                for n, (ps, done) in enumerate(((psG, g_mm), (psU, u_mm))):
                    if n == 0:
                        sil_done.wait(pe, t)
                    else:
                        a_done.wait(pe, t)
                    for m, (a, w, c) in enumerate(todo):
                        last = pe.matmul(ps[:, 0:FF], hTr[:, tt % 2, a, c * P:(c + 1) * P],
                                         gu[:, w, c, n * FF:(n + 1) * FF], start=(m == 0), stop=(m == len(todo) - 1))
                    last.then_inc(done.sem, 1)

            def transpose_a(i, tt):
                t = TPB * i + tt
                a_done.wait(pe, t + 1)
                alo_done.wait(pe, t)
                for c in range(NF):
                    last = pe.transpose(psA[:, c * P:(c + 1) * P], act_t[:, c * P:(c + 1) * P], keep["ident"][:, :])
                last.then_inc(ta_mm.sem, 1)

            def down(i, tt):
                t = TPB * i + tt
                alo_done.wait(pe, t + 1)
                yg_done.wait(pe, t - 1)
                todo = [(a, w, c) for c in range(NF) for a, w in ((0, 0), (0, 1), (1, 0))]
                for m, (a, w, c) in enumerate(todo):
                    f = FCH[c]
                    last = pe.matmul(psY[tt % 2][:, :], aTr[0:f, a, c * P:(c + 1) * P], dn[0:f, w, c],
                                     start=(m == 0), stop=(m == len(todo) - 1))
                last.then_inc(y_mm.sem, 1)

            def step(i, tt, last):
                transpose_a(i, tt)
                if in_range(tt, 2, last):
                    transpose_h(*ahead(i, tt, 2))
                if in_range(tt, 1, last):
                    gate_up(*ahead(i, tt, 1))
                down(i, tt)
                if in_range(tt, 2, last):
                    logits(*ahead(i, tt, 2))

            for x in (t_mm, u_mm, ta_mm, y_mm):
                x.start(pe)
            pe.wait_ge(wr_lo, 1)
            transpose_h(0, 0)
            transpose_h(0, 1)
            logits(0, 0)
            logits(0, 1)
            pe.wait_ge(raw_lo, KC + NF)
            gate_up(0, 0)
            slots(pe, step)


def ahead(i, tt, n):
    return i + (tt + n) // TPB, (tt + n) % TPB


def route(nc, io, keep):
    with Stage(nc, "rt") as ctx:
        sem = ctx.sem

        def sb(name, shape, dt=F32):
            return ctx.enter_context(nc.sbuf_tensor(name, shape, dt))

        TE = TILES * EXPERTS
        PAIRS = TOPK * TILES
        RING = 4
        big = [P, TILES, EXPERTS]
        bias2 = sb("bias2", [P, 2, EXPERTS])
        bias = sb("bias", [P, EXPERTS])
        lg = sb("lg", big)
        pr = sb("pr", big)
        top = sb("top", [P, TOPK, TILES])
        key = sb("key", big)
        kmax = sb("kmax", [P, TILES])
        oh = [sb(f"oh{k}", big) for k in range(TOPK)]
        rev = sb("rev", [P, EXPERTS])
        den = sb("den_", [P, TILES])
        mask = sb("mask", big, F32R)
        tri_f = sb("tri_f", [P, P])
        tri = sb("tri", [P, P], F32R)
        all_f = sb("all_f", [P, P])
        all_r = sb("all_r", [P, P], F32R)
        scan = [sb(f"scan{n}", big) for n in range(2)]
        before = sb("before", big)
        n_i = sb("n_i", [P, EXPERTS], I32)
        t_i = sb("t_i", [P, EXPERTS], I32)
        tiles = sb("tiles", [P, EXPERTS])
        ends = [sb(f"ends{n}", [P, EXPERTS]) for n in range(2)]
        base = sb("base", [P, EXPERTS])
        place = sb("place", big)
        prod = sb("prod", big)
        slot = sb("slot", [P, TOPK, TILES])
        tile_i = sb("tile_i", [P, PAIRS], I32)
        row_i = sb("row_i", [P, PAIRS], I32)
        tile_f = sb("tile_f", [P, PAIRS])
        row_f = sb("row_f", [P, PAIRS])
        iota_r = sb("iota_r", [P, P])
        iota_s = sb("iota_s", [P, SLOTS])
        tok = sb("tok", [P, TILES])
        ge = sb("ge", [P, SLOTS, EXPERTS])
        emap = sb("emap", [P, SLOTS])
        oh_row = sb("oh_row", [P, RING, P], F32R)
        oh_tile = sb("oh_tile", [P, RING, SLOTS], F32R)
        psB = ctx.enter_context(nc.psum_tensor("psB", [P, D], F32))
        psT = ctx.enter_context(nc.psum_tensor("psTot", [P, D], F32))
        psI = ctx.enter_context(nc.psum_tensor("psI", [P, D], F32))

        bias_in = sem("bias_in")
        iotas, tri_set, tri_done = sem("iotas"), sem("tri_set"), sem("tri_done")
        d = sem("route_steps")
        lg_done, e_done = sem("lg_done"), sem("ex_done")
        mask_done, counts_mm = sem("mask_done"), sem("counts_mm")
        split_done = sem("split_done")
        row_done, tile_done = ctx.count("oh_row_done"), ctx.count("oh_tile_done")
        id_mm = ctx.count("id_mm", RING)
        ids_done = sem("ids_done")
        block = ctx.block()

        @block.sync
        def _(sp):
            for n, name in enumerate(("br", "rb")):
                sp.dma_start(bias2[:, n], io[name].partition_broadcast(P)).then_inc(bias_in, 16)

        @block.gpsimd
        def _(pool):
            f = dict(allow_small_or_imprecise_dtypes=True)
            pool.iota(iota_r[:, :], pattern=[[1, P]], base=0, channel_multiplier=0, **f).then_inc(iotas, 1)
            pool.iota(iota_s[:, :], pattern=[[1, SLOTS]], base=0, channel_multiplier=0, **f).then_inc(iotas, 1)
            pool.iota(tok[:, :], pattern=[[P, TILES]], base=0, channel_multiplier=1, **f).then_inc(iotas, 1)
            pool.iota(rev[:, :], pattern=[[-1, EXPERTS]], base=EXPERTS, channel_multiplier=0, **f).then_inc(iotas, 1)
            pool.memset(all_f[:, :], 1.0).then_inc(tri_set, 1)
            pool.wait_ge(tri_set, 1)
            pool.affine_select(out=tri_f[:, :], in_=all_f[:, :], compare_op=ALU.is_gt, fill=0.0, base=0,
                               pattern=[[1, P]], channel_multiplier=-1).then_inc(tri_done, 1)

        @block.scalar
        def _(act):
            act.wait_ge(lg_done, 1)
            act.activation(pr[:, :, :], lg[:, :, :], ACT.Exp, scale=-1.0).then_inc(e_done, 1)

        @block.vector
        def _(dve):
            at = [0]

            def then(ins):
                at[0] += 1
                ins.then_inc(d, 1)
                dve.wait_ge(d, at[0])

            def over_tiles(x):
                return x[:, :].unsqueeze(1).broadcast_to(tuple(big))

            def over_experts(x):
                return x.unsqueeze(2).broadcast_to(tuple(big))

            dve.wait_ge(bias_in, 32)
            dve.wait_ge(iotas, 4)
            dve.wait_ge(tri_done, 1)
            then(dve.tensor_copy(tri[:, :], tri_f[:, :]))
            then(dve.tensor_copy(all_r[:, :], all_f[:, :]))
            then(dve.tensor_copy(keep["tok2"][:, 0:TILES], tok[:, :]))
            then(dve.tensor_copy(keep["tok2"][:, TILES:PAIRS], tok[:, :]))
            then(dve.tensor_tensor(bias[:, :], bias2[:, 0], bias2[:, 1], ALU.add))
            dve.tensor_tensor(lg[:, :, :], keep["logits"][:, :, :], over_tiles(bias), ALU.add).then_inc(lg_done, 1)
            dve.wait_ge(e_done, 1)
            then(dve.tensor_scalar_add(pr[:, :, :], pr[:, :, :], 1.0))
            then(dve.reciprocal(pr[:, :, :], pr[:, :, :]))
            for k in range(TOPK):
                then(dve.reduce_max(top[:, k], pr[:, :, :], AX_X))
                then(dve.tensor_tensor(key[:, :, :], pr[:, :, :], over_experts(top[:, k]), ALU.is_equal))
                then(dve.tensor_tensor(key[:, :, :], key[:, :, :], over_tiles(rev), ALU.mult))
                then(dve.reduce_max(kmax[:, :], key[:, :, :], AX_X))
                then(dve.tensor_tensor(oh[k][:, :, :], key[:, :, :], over_experts(kmax[:, :]), ALU.is_equal))
                if k == 0:
                    then(dve.scalar_tensor_tensor(pr[:, :, :], oh[0][:, :, :], -2.0, pr[:, :, :], ALU.mult, ALU.add))
            dve.tensor_tensor(mask[:, :, :], oh[0][:, :, :], oh[1][:, :, :], ALU.add).then_inc(mask_done, 1)
            then(dve.tensor_tensor(den[:, :], top[:, 0], top[:, 1], ALU.add))
            then(dve.reciprocal(den[:, :], den[:, :]))
            for k in range(TOPK):
                then(dve.tensor_tensor(keep["w"][:, k], top[:, k], den[:, :], ALU.mult))
            dve.wait_ge(counts_mm, 1)
            then(dve.tensor_copy(scan[0][:, :, :].rearrange("p t e -> p (t e)"), psT[:, 0:TE]))
            then(dve.tensor_copy(before[:, :, :], scan[0][:, :, :]))
            n, step = 0, 1
            while step < TILES:
                a, b = scan[n], scan[1 - n]
                then(dve.tensor_tensor(b[:, step:], a[:, step:], a[:, :TILES - step], ALU.add))
                then(dve.tensor_copy(b[:, :step], a[:, :step]))
                n, step = 1 - n, 2 * step
            total = scan[n]
            then(dve.tensor_copy(n_i[:, :], total[:, TILES - 1]))
            then(dve.tensor_scalar(t_i[:, :], n_i[:, :], P.bit_length() - 1, None, ALU.arith_shift_right))
            then(dve.tensor_copy(tiles[:, :], t_i[:, :]))
            then(dve.tensor_scalar_add(tiles[:, :], tiles[:, :], 1.0))
            then(dve.tensor_copy(ends[0][:, :], tiles[:, :]))
            m, step = 0, 1
            while step < EXPERTS:
                a, b = ends[m], ends[1 - m]
                then(dve.tensor_tensor(b[:, step:], a[:, step:], a[:, :EXPERTS - step], ALU.add))
                then(dve.tensor_copy(b[:, :step], a[:, :step]))
                m, step = 1 - m, 2 * step
            end = ends[m]
            then(dve.tensor_tensor(base[:, :], end[:, :], tiles[:, :], ALU.subtract))
            then(dve.tensor_scalar_mul(base[:, :], base[:, :], float(P)))
            then(dve.tensor_tensor(before[:, :, :], total[:, :, :], before[:, :, :], ALU.subtract))
            then(dve.tensor_tensor(place[:, :, :], before[:, :, :], over_tiles(base), ALU.add))
            then(dve.tensor_tensor(place[:, :, :], place[:, :, :],
                                   psB[:, 0:TE].rearrange("p (t e) -> p t e", e=EXPERTS), ALU.add))
            for k in range(TOPK):
                then(dve.tensor_tensor(prod[:, :, :], place[:, :, :], oh[k][:, :, :], ALU.mult))
                then(dve.reduce_sum(slot[:, k], prod[:, :, :], AX_X))
            then(dve.tensor_copy(keep["slot_i"][:, :], slot[:, :, :].rearrange("p k t -> p (k t)")))
            then(dve.tensor_scalar(tile_i[:, :], keep["slot_i"][:, :], P.bit_length() - 1, None, ALU.arith_shift_right))
            then(dve.tensor_scalar(row_i[:, :], keep["slot_i"][:, :], P - 1, None, ALU.bitwise_and))
            dve.tensor_copy(tile_f[:, :], tile_i[:, :]).then_inc(split_done, 1)
            dve.tensor_copy(row_f[:, :], row_i[:, :]).then_inc(split_done, 1)
            dve.wait_ge(split_done, 2)
            wide = (P, SLOTS, EXPERTS)
            then(dve.tensor_tensor(ge[:, :, :], iota_s[:, :].unsqueeze(2).broadcast_to(wide),
                                   end[:, :].unsqueeze(1).broadcast_to(wide), ALU.is_ge))
            then(dve.reduce_sum(emap[:, :], ge[:, :, :], AX_X))
            then(dve.tensor_scalar_min(emap[:, :], emap[:, :], float(EXPERTS - 1)))
            then(dve.tensor_copy(keep["tile_expert"][:, :], emap[:, :]))
            with dve.Fori(0, PAIRS // RING) as i:
                for r in range(RING):
                    m = RING * i + r
                    id_mm.wait(dve, m - RING + 1)
                    dve.tensor_scalar(oh_row[:, r], iota_r[:, :], row_f[:, bass.ds(m, 1)], None, ALU.is_equal)\
                       .then_inc(row_done.sem, 1)
                    dve.tensor_scalar(oh_tile[:, r], iota_s[:, :], tile_f[:, bass.ds(m, 1)],
                                      keep["tok2"][:, bass.ds(m, 1)], ALU.is_equal, ALU.mult).then_inc(tile_done.sem, 1)
            id_mm.wait(dve, PAIRS)
            dve.tensor_copy(keep["ids"][:, :], psI[:, 0:SLOTS]).then_inc(ids_done, 1)

        @block.tensor
        def _(pe):
            id_mm.start(pe)
            pe.wait_ge(mask_done, 1)
            m = mask[:, :, :].rearrange("p t e -> p (t e)")
            pe.matmul(psB[:, 0:TE], tri[:, :], m, start=True, stop=True)
            pe.matmul(psT[:, 0:TE], all_r[:, :], m, start=True, stop=True).then_inc(counts_mm, 1)
            row_done.wait(pe, 1)
            tile_done.wait(pe, 1)
            pe.matmul(psI[:, 0:SLOTS], oh_row[:, 0], oh_tile[:, 0], start=True, stop=False, skip_group_check=True)\
              .then_inc(id_mm.sem, 1)
            for r in range(1, RING):
                row_done.wait(pe, r + 1)
                tile_done.wait(pe, r + 1)
                pe.matmul(psI[:, 0:SLOTS], oh_row[:, r], oh_tile[:, r], start=False, stop=False,
                          skip_group_check=True).then_inc(id_mm.sem, 1)
            with pe.Fori(1, PAIRS // RING) as i:
                for r in range(RING):
                    row_done.wait(pe, RING * i + r + 1)
                    tile_done.wait(pe, RING * i + r + 1)
                    pe.matmul(psI[:, 0:SLOTS], oh_row[:, r], oh_tile[:, r], start=False, stop=False,
                              skip_group_check=True).then_inc(id_mm.sem, 1)


def routed_experts(nc, io, keep):
    with Stage(nc, "re") as ctx:
        sem, count = ctx.sem, ctx.count

        def sb(name, shape, dt=F32):
            return ctx.enter_context(nc.sbuf_tensor(name, shape, dt))

        def psum(name, shape):
            return ctx.enter_context(nc.psum_tensor(name, shape, F32))

        U = 4
        idx = sb("idx", [P, U], I32)
        hg = sb("hg", [P, U, D])
        hgT = sb("hgT", [P, 2, D])
        sil = sb("sil2", [P, FF])
        act_t = sb("act_t2", [P, FPAD])
        aT = sb("aT", [P, FPAD])
        y = sb("y_t", [P, U, D])
        psT = psum("psT2", [P, D])
        psG = psum("psG2", [P, D])
        psU = psum("psU2", [P, D])
        psA = psum("psA2", [P, D])
        psY = [psum(f"psY2{n}", [P, D]) for n in range(2)]

        idx_done = count("idx_done", U)
        idx_seen = sem("idx_seen")
        g_in = [sem(f"g_in{n}") for n in range(U)]
        y_out = [sem(f"y_out{n}") for n in range(U)]
        pad_done = sem("pad_done2")
        t_mm, hgT_done = count("t_mm2", U), count("hgT_done", 1)
        g_mm, u_mm = count("g_mm2"), count("u_mm2", 2)
        sil_done, a_done = count("sil_done2", 1), count("a_done2", 1)
        ta_mm, aT_done = count("ta_mm2", 1), count("aT_done", 1)
        y_mm, y_done = count("y_mm2", 1), count("y_done", 2)
        block = ctx.block()
        y_tiles = io["y"].rearrange("(s p) d -> s p d", p=P)

        def slots(eng, step):
            with eng.Fori(0, SLOTS // U - 1) as i:
                for r in range(U):
                    step(i, r, False)
            for r in range(U):
                step(SLOTS // U - 1, r, True)

        def in_range(r, n, last):
            return not last or r + n < U

        def on(i, r, n):
            return i + (r + n) // U, (r + n) % U

        @block.sync
        def _(sp):
            for n in range(U):
                sp.sem_inc(y_out[n], 16)
            with sp.Fori(0, SLOTS // U) as i:
                for r in range(U):
                    y_done.wait(sp, U * i + r + 1)
                    sp.dma_start(y_tiles[U * i + r], y[:, r]).then_inc(y_out[r], 16)
            for n in range(U):
                sp.wait_ge(y_out[n], 16 * (SLOTS // U + 1))

        @block.gpsimd
        def _(pool):
            idx_done.start(pool)
            with pool.Fori(0, SLOTS // U) as i:
                for r in range(U):
                    s = U * i + r
                    t_mm.wait(pool, s - U + 1)
                    pool.tensor_copy(idx[:, r:r + 1], keep["ids"][:, bass.ds(s, 1)]).then_inc(idx_done.sem, 1)
                    idx_done.wait(pool, s + 1)
                    pool.sem_inc(idx_seen, 1)
                    pool.indirect_dma_start(out=hg[:, r], out_offset=None, in_=io["h2"],
                                            in_offset=bass.IndirectOffsetOnAxis(ap=idx[:, r:r + 1].bitcast(U32), axis=0))\
                        .then_inc(g_in[r], 16)

        @block.scalar
        def _(act):
            def copy_h(i, r):
                s = U * i + r
                t_mm.wait(act, s + 1)
                u_mm.wait(act, s - 1)
                act.activation(hgT[:, r % 2], psT[:, :], ACT.Copy).then_inc(hgT_done.sem, 1)

            def silu(i, r):
                s = U * i + r
                g_mm.wait(act, s + 1)
                a_done.wait(act, s)
                act.activation(sil[:, :], psG[:, 0:FF], ACT.Silu).then_inc(sil_done.sem, 1)

            def copy_y(i, r):
                s = U * i + r
                y_mm.wait(act, s + 1)
                act.wait_ge(y_out[r], 16 * (i + 1))
                act.activation(y[:, r], psY[r % 2][:, :], ACT.Copy).then_inc(y_done.sem, 1)

            def step(i, r, last):
                if in_range(r, 2, last):
                    copy_h(*on(i, r, 2))
                if in_range(r, 1, last):
                    silu(*on(i, r, 1))
                copy_y(i, r)

            for x in (hgT_done, sil_done, y_done):
                x.start(act)
            copy_h(0, 0)
            copy_h(0, 1)
            silu(0, 0)
            slots(act, step)

        @block.vector
        def _(dve):
            def gated(i, r):
                s = U * i + r
                sil_done.wait(dve, s + 1)
                u_mm.wait(dve, s + 1)
                ta_mm.wait(dve, s)
                dve.tensor_tensor(act_t[:, 0:FF], sil[:, :], psU[:, 0:FF], ALU.mult).then_inc(a_done.sem, 1)

            def copy_a(i, r):
                s = U * i + r
                ta_mm.wait(dve, s + 1)
                y_mm.wait(dve, s)
                dve.tensor_copy(aT[:, :], psA[:, 0:FPAD]).then_inc(aT_done.sem, 1)

            def step(i, r, last):
                copy_a(i, r)
                if in_range(r, 1, last):
                    gated(*on(i, r, 1))

            for x in (a_done, aT_done):
                x.start(dve)
            dve.memset(act_t[:, :], 0.0).then_inc(pad_done, 1)
            dve.wait_ge(pad_done, 1)
            gated(0, 0)
            slots(dve, step)

        @block.tensor
        def _(pe):
            def transpose_h(i, r):
                s = U * i + r
                pe.wait_ge(g_in[r], 16 * (i + 1))
                hgT_done.wait(pe, s)
                for c in range(KC):
                    last = pe.transpose(psT[:, c * P:(c + 1) * P], hg[:, r, c * P:(c + 1) * P], keep["ident"][:, :])
                last.then_inc(t_mm.sem, 1)

            def gate_up(i, r, e):
                s = U * i + r
                hgT_done.wait(pe, s + 1)
                for n, (ps, done, free) in enumerate(((psG, g_mm, sil_done), (psU, u_mm, a_done))):
                    free.wait(pe, s)
                    for c in range(KC):
                        last = pe.matmul(ps[:, 0:FF], hgT[:, r % 2, c * P:(c + 1) * P],
                                         keep["gu_e"][:, e, c, n * FF:(n + 1) * FF],
                                         start=(c == 0), stop=(c == KC - 1))
                    last.then_inc(done.sem, 1)

            def transpose_a(i, r):
                s = U * i + r
                a_done.wait(pe, s + 1)
                aT_done.wait(pe, s)
                for c in range(NF):
                    last = pe.transpose(psA[:, c * P:(c + 1) * P], act_t[:, c * P:(c + 1) * P], keep["ident"][:, :])
                last.then_inc(ta_mm.sem, 1)

            def down(i, r, e):
                s = U * i + r
                aT_done.wait(pe, s + 1)
                y_done.wait(pe, s - 1)
                for c in range(NF):
                    f = FCH[c]
                    last = pe.matmul(psY[r % 2][:, :], aT[0:f, c * P:(c + 1) * P], keep["dn_e"][0:f, e, c],
                                     start=(c == 0), stop=(c == NF - 1))
                last.then_inc(y_mm.sem, 1)

            def expert(i, r):
                return pe.value_load(keep["tile_expert"][0:1, bass.ds(U * i + r, 1)], min_val=0, max_val=EXPERTS - 1)

            def step(i, r, last):
                transpose_a(i, r)
                if in_range(r, 2, last):
                    transpose_h(*on(i, r, 2))
                if in_range(r, 1, last):
                    gate_up(*on(i, r, 1), expert(*on(i, r, 1)))
                down(i, r, expert(i, r))

            for x in (t_mm, u_mm, ta_mm, y_mm):
                x.start(pe)
            for e in range(EXPERTS):
                pe.wait_ge(keep["we_in"][e], 16 * (1 + NF))
            transpose_h(0, 0)
            transpose_h(0, 1)
            gate_up(0, 0, expert(0, 0))
            slots(pe, step)


def combine(nc, io, keep):
    with Stage(nc, "cb") as ctx:
        sem, count = ctx.sem, ctx.count

        def sb(name, shape, dt=F32):
            return ctx.enter_context(nc.sbuf_tensor(name, shape, dt))

        U = 4
        gate = sb("gate_", [P, 2, D])
        idx = sb("idx_", [P, U, TOPK], I32)
        yk = sb("yk", [P, U, TOPK, D])
        xs = sb("xs_t", [P, U, D])
        t1 = sb("t1", [P, 2, D])
        t2 = sb("t2", [P, 2, D])
        t3 = sb("t3", [P, 2, D])
        gate_in = [sem(f"gatec_in{n}") for n in range(2)]
        idx_done = count("idxc_done")
        idx_seen = sem("idxc_seen")
        y_in = [sem(f"y_in{n}") for n in range(U)]
        xs_in = [sem(f"xs_in{n}") for n in range(U)]
        out_done = [sem(f"out_done{n}") for n in range(U)]
        t1_done, t2_done, t3_done = count("t1_done"), count("t2_done", U), count("t3_done", 2)
        sum_done = count("sum_done", TPB + 1)
        xs_tiles = io["xs"].rearrange("(t p) d -> t p d", p=P)
        out_tiles = io["out"].rearrange("(t p) d -> t p d", p=P)
        block = ctx.block()

        @block.sync
        def _(sp):
            def load(i, tt):
                sp.wait_ge(out_done[tt % U], 16 * ((TPB // U) * i + tt // U + 1))
                sp.dma_start(xs[:, tt % U], xs_tiles[TPB * i + tt]).then_inc(xs_in[tt % U], 16)

            def store(i, tt):
                sum_done.wait(sp, TPB * i + tt + 1)
                sp.dma_start(out_tiles[TPB * i + tt], xs[:, tt % U]).then_inc(out_done[tt % U], 16)

            for n in range(U):
                sp.sem_inc(out_done[n], 16)
            for n in range(U - 1):
                load(0, n)

            def batch(i, last):
                for tt in range(TPB):
                    if not last or tt + U - 1 < TPB:
                        load(i, tt + U - 1)
                    store(i, tt)

            with sp.Fori(0, B - 1) as i:
                batch(i, False)
            batch(B - 1, True)
            for n in range(U):
                sp.wait_ge(out_done[n], 16 * (TILES // U + 1))

        @block.gpsimd
        def _(pool):
            with pool.Fori(0, TILES // U) as i:
                for r in range(U):
                    t = U * i + r
                    t2_done.wait(pool, t - U + 1)
                    for k in range(TOPK):
                        pool.tensor_copy(idx[:, r, k:k + 1], keep["slot_i"][:, bass.ds(k * TILES + t, 1)])\
                            .then_inc(idx_done.sem, 1)
                    idx_done.wait(pool, TOPK * (t + 1))
                    pool.sem_inc(idx_seen, 1)
                    for k in range(TOPK):
                        pool.indirect_dma_start(out=yk[:, r, k], out_offset=None, in_=io["y"],
                                                in_offset=bass.IndirectOffsetOnAxis(
                                                    ap=idx[:, r, k:k + 1].bitcast(U32), axis=0)).then_inc(y_in[r], 16)

        @block.scalar
        def _(act):
            with act.Fori(0, B // 2) as i:
                for q in range(2):
                    sum_done.wait(act, TPB * (2 * i + q - 1))
                    act.dma_start(gate[:, q], io["modrows"][R_GB, 2 * i + q].partition_broadcast(P)).then_inc(gate_in[q], 16)
                    for tt in range(TPB):
                        t = TPB * (2 * i + q) + tt
                        act.wait_ge(y_in[tt % U], 16 * TOPK * ((TPB // U) * (2 * i + q) + tt // U + 1))
                        t2_done.wait(act, t - 1)
                        act.activation(t1[:, tt % 2], yk[:, tt % U, 0], ACT.Copy,
                                       scale=keep["w"][:, 0, bass.ds(t, 1)]).then_inc(t1_done.sem, 1)

        @block.vector
        def _(dve):
            for x in (t2_done, t3_done, sum_done):
                x.start(dve)
            with dve.Fori(0, B // 2) as i:
                for q in range(2):
                    dve.wait_ge(gate_in[q], 16 * (i + 1))
                    for tt in range(TPB):
                        t = TPB * (2 * i + q) + tt
                        t1_done.wait(dve, t + 1)
                        t3_done.wait(dve, t - 1)
                        dve.scalar_tensor_tensor(t2[:, tt % 2], yk[:, tt % U, 1], keep["w"][:, 1, bass.ds(t, 1)],
                                                 t1[:, tt % 2], ALU.mult, ALU.add).then_inc(t2_done.sem, 1)
                        t2_done.wait(dve, t + 1)
                        sum_done.wait(dve, t - 1)
                        dve.tensor_tensor(t3[:, tt % 2], t2[:, tt % 2], gate[:, q], ALU.mult).then_inc(t3_done.sem, 1)
                        t3_done.wait(dve, t + 1)
                        dve.wait_ge(xs_in[tt % U], 16 * ((TPB // U) * (2 * i + q) + tt // U + 1))
                        dve.tensor_tensor(xs[:, tt % U], t3[:, tt % 2], xs[:, tt % U], ALU.add).then_inc(sum_done.sem, 1)


def block_program(nc, io):
    with ExitStack() as ctx:
        def sb(name, shape, dt=F32):
            return ctx.enter_context(nc.sbuf_tensor(name, shape, dt))

        keep = {
            "ident": sb("ident", [P, P]),
            "ones": sb("ones", [P, P], F32R),
            "rstd2": sb("rstd2", [P, B, TPB]),
            "nmr2": sb("nmr2", [P, B, TPB]),
            "logits": sb("logits", [P, TILES, EXPERTS]),
            "w": sb("w", [P, TOPK, TILES]),
            "slot_i": sb("slot_i", [P, TOPK * TILES], I32),
            "tok2": sb("tok2", [P, TOPK * TILES]),
            "ids": sb("ids", [P, SLOTS], I32),
            "tile_expert": sb("tile_expert", [P, SLOTS], I32),
        }
        with ExitStack() as attn:
            def ab(name, shape, dt=F32):
                return attn.enter_context(nc.sbuf_tensor(name, shape, dt))

            keep["modc"] = ab("modc", [P, B, 2, KC])
            keep["kvT"] = ab("kvT", [P, B, D])
            keep["ks_hi"] = ab("ks_hi", [P, B, 2 * KVH], F32R)
            keep["ks_lo"] = ab("ks_lo", [P, B, 2 * KVH], F32R)
            keep["wq_hi"] = ab("wq_hi", [P, HEADS, KC, P], F32R)
            keep["wq_lo"] = ab("wq_lo", [P, HEADS, KC, P], F32R)
            with ExitStack() as kv:
                keep["wkv_hi"] = kv.enter_context(nc.sbuf_tensor("wkv_hi", [P, 2, KC, D], F32R))
                keep["wkv_lo"] = kv.enter_context(nc.sbuf_tensor("wkv_lo", [P, 2, KC, D], F32R))
                setup(nc, io, keep)
                keys_values(nc, io, keep)
            queries(nc, io, keep)
        with ExitStack() as ffn:
            def fb(name, shape, dt=F32):
                return ffn.enter_context(nc.sbuf_tensor(name, shape, dt))

            keep["gu_e"] = fb("gu_e", [P, EXPERTS, KC, GU])
            keep["dn_e"] = fb("dn_e", [P, EXPERTS, NF, D])
            keep["we_in"] = [ctx.enter_context(nc.semaphore(f"we_in{e}")) for e in range(EXPERTS)]
            shared_expert(nc, io, keep)
            route(nc, io, keep)
            routed_experts(nc, io, keep)
        combine(nc, io, keep)


def chunked(w):
    k, n = w.shape
    return w.reshape(k // P, P, n).transpose(1, 0, 2)


def kernel(**inputs):
    import concourse.bacc as bacc
    from concourse.bass_utils import run_bass_kernel_spmd

    a = {k.split("_", 1)[1]: np.asarray(v) for k, v in inputs.items()}
    laid_out = {
        "x": a["attn_hidden_states"].reshape(TOK, D),
        "wqT": chunked(a["attn_Wq"].T).reshape(P, KC, HEADS, P).transpose(0, 2, 1, 3),
        "bq": a["attn_bq"].reshape(HEADS, P).T,
        "wkvT": np.stack([chunked(a["attn_Wk"].T), chunked(a["attn_Wv"].T)], 1),
        "bk": a["attn_bk"],
        "bv": a["attn_bv"],
        "woT": a["attn_Wo"].T.reshape(HEADS, P, D).transpose(1, 0, 2),
        "cT": chunked(a["c"].T).reshape(P, KC * B),
        "wmod": chunked(a["wmod"]).reshape(P, KC, 3, 2 * D).transpose(0, 2, 1, 3),
        "wr": chunked(a["ffn_Wr"]),
        "br": a["ffn_br"],
        "rb": a["ffn_rb"],
        "gu_s": chunked(np.concatenate([a["ffn_Wg_s"], a["ffn_Wu_s"]], 1)),
        "dn_s": a["ffn_Wd_s"],
        "gu_e": np.stack([chunked(w) for w in np.concatenate([a["ffn_Wg"], a["ffn_Wu"]], 2)]),
        "dn_e": a["ffn_Wd"],
    }
    laid_out = {k: np.ascontiguousarray(v) for k, v in laid_out.items()}
    nc = bacc.Bacc("TRN2", target_bir_lowering=False, num_devices=1)
    io = {k: nc.dram_tensor(f"in_{k}", v.shape, F32, kind="ExternalInput").ap() for k, v in laid_out.items()}
    out = nc.dram_tensor("out", (TOK, D), F32, kind="ExternalOutput").ap()
    io["out"] = out
    for name, rows in (("x1", TOK), ("h2", TOK), ("xs", TOK), ("y", SLOTS * P)):
        io[name] = nc.dram_tensor(f"dram_{name}", (rows, D), F32, kind="Internal").ap()
    io["modrows"] = nc.dram_tensor("modrows", (len(ROWS), B, D), F32, kind="Internal").ap()
    io["hTs"] = nc.dram_tensor("hTs", (B * BB, P, 2, KC, BLK), F32, kind="Internal").ap()
    block_program(nc, io)
    r = run_bass_kernel_spmd(nc, [{f"in_{k}": v for k, v in laid_out.items()}], core_ids=[0])
    return r.results[0]["out"].reshape(B, S, D)
```

```python
from contextlib import ExitStack

import numpy as np

import concourse.bass as bass
from concourse import mybir

F32 = mybir.dt.float32
F32R = mybir.dt.float32r
I32 = mybir.dt.int32
U32 = mybir.dt.uint32
ALU = mybir.AluOpType
ACT = mybir.ActivationFunctionType
AX_X = mybir.AxisListType.X

P = 128
B, S, D = 4, 1024, 512
HEADS, KVH = 16, 4
GROUP = HEADS // KVH
KC = D // P
BLK = 512
TB = BLK // P
BB = S // BLK
TPB = S // P
TOK = B * S
TILES = TOK // P
EXPERTS, TOPK, FF = 8, 2, 352
FCH = [P, P, FF - 2 * P]
LN_EPS, NORM_EPS = 1e-5, 1e-6
MAG = 0.25
SA, CA, GA, SB, CB, GB = range(6)
ROWS = [GA, SB, CB, GB]
R_GA, R_SB, R_CB, R_GB = range(4)


class Count:

    def __init__(self, sem, head):
        self.sem = sem
        self.head = head

    def start(self, eng):
        eng.sem_inc(self.sem, self.head)

    def wait(self, eng, n):
        eng.wait_ge(self.sem, n + self.head)


class Stage(ExitStack):

    def __init__(self, nc, name):
        super().__init__()
        self.nc, self.name, self.sems = nc, name, []

    def sem(self, name):
        self.sems.append(self.enter_context(self.nc.semaphore(f"{self.name}_{name}")))
        return self.sems[-1]

    def count(self, name, head=0):
        return Count(self.sem(name), head)

    def clear(self):
        with self.nc.Block() as block:
            @block.gpsimd
            def _(pool):
                for s in self.sems:
                    pool.sem_clear(s)

    def block(self):
        self.callback(self.clear)
        return self.enter_context(self.nc.Block())


def setup(nc, io, keep):
    with Stage(nc, "set") as ctx:
        sem = ctx.sem

        def sb(name, shape, dt=F32):
            return ctx.enter_context(nc.sbuf_tensor(name, shape, dt))

        wkv_raw = sb("wkv_raw", [P, 2, KC, D])
        wmod = sb("wmod", [P, 3, KC, 2 * D])
        cT = sb("cT", [P, KC * B])
        den = sb("den", [P, KC * B])
        sc = sb("sc", [P, KC, B])
        rows = sb("rows", [B, len(ROWS), D])
        gabs = sb("gabs", [B, 2, D])
        mag = sb("mag", [B, 2, D])
        sgn = sb("sgn", [B, 2, D])
        ones_f = sb("ones_f", [P, P])
        psR = ctx.enter_context(nc.psum_tensor("psR", [P, 4, D], F32))
        psC = ctx.enter_context(nc.psum_tensor("psC", [P, D], F32))

        c_in = sem("c_in")
        wmod_in = [sem(f"wmod_in{n}") for n in range(3)]
        wkv_in = [sem(f"wkv_in{n}") for n in range(2)]
        e_done, den_done, rec_done, sc_done = sem("e_done"), sem("den_done"), sem("rec_done"), sem("sc_done")
        ident_zero, ident_done = sem("ident_zero"), sem("ident_done")
        ones_set, ones_done = sem("ones_set"), sem("ones_done")
        rows_mm, cols_mm = sem("rows_mm"), sem("cols_mm")
        abs_done, mag_done, sgn_done, rows_done = sem("abs_done"), sem("mag_done"), sem("sgn_done"), sem("rows_done")
        cols_done = sem("cols_done")
        hi_done, lo_done = sem("hi_done"), sem("lo_done")
        rows_out = sem("rows_out")
        block = ctx.block()

        @block.sync
        def _(sp):
            sp.dma_start(cT[:, :], io["cT"]).then_inc(c_in, 16)
            for n in range(2):
                sp.dma_start(wkv_raw[:, n], io["wkvT"][:, n]).then_inc(wkv_in[n], 16)
            for n in range(3):
                sp.dma_start(wmod[:, n], io["wmod"][:, n]).then_inc(wmod_in[n], 16)
            sp.wait_ge(rows_done, 4)
            sp.dma_start(io["modrows"].rearrange("v b d -> b v d"), rows[:, :, :]).then_inc(rows_out, 16)
            sp.wait_ge(rows_out, 16)

        @block.gpsimd
        def _(pool):
            pool.memset(keep["ident"][:, :], 0.0).then_inc(ident_zero, 1)
            pool.wait_ge(ident_zero, 1)
            pool.affine_select(out=keep["ident"][:, :], in_=keep["ident"][:, :], compare_op=ALU.not_equal, fill=1.0,
                               base=0, pattern=[[-1, P]], channel_multiplier=1).then_inc(ident_done, 1)

        @block.scalar
        def _(act):
            act.wait_ge(c_in, 16)
            act.activation(den[:, :], cT[:, :], ACT.Exp, scale=-1.0).then_inc(e_done, 1)
            for n in range(2):
                act.wait_ge(wkv_in[n], 16)
                act.activation(keep["wkv_hi"][:, n], wkv_raw[:, n], ACT.Copy).then_inc(hi_done, 1)
            act.wait_ge(rows_mm, 4)
            for n, v in enumerate((R_GA, R_GB)):
                act.activation(gabs[:, n], psR[0:B, v], ACT.Abs).then_inc(abs_done, 1)

        @block.vector
        def _(dve):
            dve.memset(ones_f[:, :], 1.0).then_inc(ones_set, 1)
            dve.wait_ge(ones_set, 1)
            dve.tensor_copy(keep["ones"][:, :], ones_f[:, :]).then_inc(ones_done, 1)
            dve.wait_ge(e_done, 1)
            dve.tensor_scalar_add(den[:, :], den[:, :], 1.0).then_inc(den_done, 1)
            dve.wait_ge(den_done, 1)
            dve.reciprocal(den[:, :], den[:, :]).then_inc(rec_done, 1)
            dve.wait_ge(rec_done, 1)
            dve.tensor_tensor(sc[:, :, :].rearrange("p c b -> p (c b)"), cT[:, :], den[:, :], ALU.mult).then_inc(sc_done, 1)
            for n in range(2):
                dve.wait_ge(hi_done, n + 1)
                dve.tensor_tensor(keep["wkv_lo"][:, n], wkv_raw[:, n], keep["wkv_hi"][:, n].bitcast(F32),
                                  ALU.subtract).then_inc(lo_done, 1)
            dve.wait_ge(cols_mm, 2)
            cols = psC[:, 0:2 * KC * B].rearrange("p (v n b) -> p b v n", v=2, n=KC)
            dve.tensor_copy(keep["modc"][:, :, SA], cols[:, :, SA]).then_inc(cols_done, 1)
            dve.tensor_scalar_add(keep["modc"][:, :, CA], cols[:, :, CA], 1.0).then_inc(cols_done, 1)
            dve.wait_ge(rows_mm, 4)
            dve.tensor_copy(rows[:, R_SB], psR[0:B, R_SB]).then_inc(rows_done, 1)
            dve.tensor_scalar_add(rows[:, R_CB], psR[0:B, R_CB], 1.0).then_inc(rows_done, 1)
            for n, v in enumerate((R_GA, R_GB)):
                dve.wait_ge(abs_done, n + 1)
                dve.tensor_scalar_max(mag[:, n], gabs[:, n], MAG).then_inc(mag_done, 1)
                dve.tensor_scalar(sgn[:, n], psR[0:B, v], 0.0, 2.0, ALU.is_ge, ALU.mult).then_inc(sgn_done, 1)
                dve.wait_ge(mag_done, n + 1)
                dve.wait_ge(sgn_done, n + 1)
                dve.scalar_tensor_tensor(rows[:, v], sgn[:, n], -1.0, mag[:, n], ALU.add, ALU.mult).then_inc(rows_done, 1)

        @block.tensor
        def _(pe):
            pe.wait_ge(sc_done, 1)
            pe.wait_ge(wmod_in[0], 16)
            for v in (SA, CA):
                for n in range(KC):
                    at = (v * KC + n) * B
                    for c in range(KC):
                        last = pe.matmul(psC[:, at:at + B], wmod[:, 0, c, v * D + n * P:v * D + (n + 1) * P],
                                         sc[:, c, :], start=(c == 0), stop=(c == KC - 1))
                last.then_inc(cols_mm, 1)
            for r, v in enumerate(ROWS):
                pe.wait_ge(wmod_in[v // 2], 16)
                for c in range(KC):
                    last = pe.matmul(psR[0:B, r], sc[:, c, :], wmod[:, v // 2, c, (v % 2) * D:(v % 2 + 1) * D],
                                     start=(c == 0), stop=(c == KC - 1))
                last.then_inc(rows_mm, 1)


def keys_values(nc, io, keep):
    with Stage(nc, "kv") as ctx:
        sem, count = ctx.sem, ctx.count

        def sb(name, shape, dt=F32):
            return ctx.enter_context(nc.sbuf_tensor(name, shape, dt))

        def psum(name, shape):
            return ctx.enter_context(nc.psum_tensor(name, shape, F32))

        QW = 4
        hT = [sb(f"hT{q}", [P, 2, KC, BLK], F32R) for q in range(BB)]
        xt = sb("xt", [P, TB, D])
        zt = sb("zt", [P, TB, D])
        st = sb("st", [P, TB, 6])
        mv = sb("mv", [P, TB, 2])
        spare = sb("spare", [P, 1])
        var = sb("var", [P, TB])
        sd = sb("sd", [P, TB])
        rstd = sb("rstd", [P, TB])
        nmr = sb("nmr", [P, TB])
        hf = sb("hf", [P, 2, BLK])
        bkv = sb("bkv", [P, 2, D])
        kb = sb("kb", [P, D])
        uk = sb("uk", [P, D])
        ek = sb("ek", [P, D])
        rk = sb("rk", [P, D])
        kf = sb("kf", [P, D])
        vf = sb("vf", [P, D])
        kvs = sb("kvs", [P, 2, 2, P])
        ksb = sb("ksb", [P, D])
        kr = sb("kr", [P, 2, 2, D], F32R)
        vr = sb("vr", [P, 2, 2, D], F32R)
        wq_raw = sb("wq_raw", [P, QW, KC, P])
        psT = [psum(f"psT{n}", [P, BLK]) for n in range(2)]
        psK = [psum(f"psK{n}", [P, D]) for n in range(2)]
        psV = psum("psV", [P, D])
        psKV = [psum(f"psKV{n}", [P, D]) for n in range(2)]
        psS = psum("psS", [P, D])

        bkv_in, x_in, wq_in = sem("bkv_in"), sem("x_in"), sem("wq_in")
        hT_out = [sem(f"hT_out{q}") for q in range(BB)]
        x_used = count("x_used", 1)
        bn_done, ag_done, var_done = count("bn_done"), count("ag_done", 1), count("var_done")
        sd_done, rstd_done, nmr_done = count("sd_done"), count("rstd_done"), count("nmr_done", 1)
        z_done = count("z_done")
        tr_done = count("tr_done", KC)
        hf_done = count("hf_done", 2)
        hi_done = count("h_hi_done")
        lo_done = count("h_lo_done", 2)
        k_mm, v_mm = count("k_mm"), count("v_mm", TB + 1)
        kb_done = count("kb_done", 2)
        vb_done = count("vb_done", 2)
        u_done = count("u_done")
        er_done = count("er_done", 1)
        k_done = count("k_done", 1)
        k_hi, k_lo = count("k_hi"), count("k_lo", 1)
        v_hi, v_lo = count("v_hi"), count("v_lo", 1)
        kv_mm = count("kv_mm", 2)
        sums_done = count("sums_done", 5)
        ks_mm = count("ks_mm")
        wqh_done, wql_done = count("wqh_done"), count("wql_done", 1)

        block = ctx.block()
        x_blocks = io["x"].rearrange("(g j p) d -> g p j d", j=TB, p=P)


        @block.sync
        def _(sp):
            def load_x(g):
                x_used.wait(sp, g)
                sp.dma_start(xt[:, :, :], x_blocks[g]).then_inc(x_in, 16)

            def store_h(i, q):
                lo_done.wait(sp, KC * (BB * i + q + 1))
                sp.dma_start(io["hTs"][BB * i + q], hT[q][:, :, :, :].bitcast(F32)).then_inc(hT_out[q], 16)

            for n, name in enumerate(("bk", "bv")):
                sp.dma_start(bkv[:, n], io[name].partition_broadcast(P)).then_inc(bkv_in, 16)
            for q in range(BB):
                sp.sem_inc(hT_out[q], 16)
            load_x(0)
            load_x(1)
            with sp.Fori(0, B - 1) as i:
                store_h(i, 0)
                load_x(BB * i + 2)
                store_h(i, 1)
                load_x(BB * i + 3)
            store_h(B - 1, 0)
            store_h(B - 1, 1)
            for q in range(BB):
                sp.wait_ge(hT_out[q], 16 * (B + 1))

        @block.gpsimd
        def _(pool):
            wql_done.start(pool)
            for n in range(HEADS // QW):
                part = slice(QW * n, QW * (n + 1))
                wql_done.wait(pool, n)
                pool.dma_start(wq_raw[:, :, :, :], io["wqT"][:, part]).then_inc(wq_in, 16)
                pool.wait_ge(wq_in, 16 * (n + 1))
                pool.tensor_copy(keep["wq_hi"][:, part], wq_raw[:, :, :, :]).then_inc(wqh_done.sem, 1)
                wqh_done.wait(pool, n + 1)
                pool.tensor_tensor(keep["wq_lo"][:, part], wq_raw[:, :, :, :], keep["wq_hi"][:, part].bitcast(F32),
                                   ALU.subtract).then_inc(wql_done.sem, 1)

        @block.scalar
        def _(act):
            def front_norm(g):
                var_done.wait(act, g + 1)
                act.activation(sd[:, :], var[:, :], ACT.Sqrt).then_inc(sd_done.sem, 1)
                nmr_done.wait(act, g + 1)
                tr_done.wait(act, KC * g)
                for j in range(TB):
                    done = act.activation(zt[:, j], xt[:, j], ACT.Identity, bias=nmr[:, j:j + 1],
                                          scale=rstd[:, j:j + 1]).then_inc(z_done.sem, 1)

            def front_free(g):
                z_done.wait(act, TB * (g + 1))
                act.sem_inc(x_used.sem, 1)

            def front_hi(g, q, chunks, out_wait):
                for c in chunks:
                    if c == 0:
                        act.wait_ge(hT_out[q], out_wait)
                        v_mm.wait(act, TB * g - TB)
                    hf_done.wait(act, KC * g + c + 1)
                    act.activation(hT[q][:, 0, c], hf[:, c % 2], ACT.Copy).then_inc(hi_done.sem, 1)

            def tile(t, tt):
                kb_done.wait(act, t + 1)
                k_done.wait(act, t)
                er_done.wait(act, t)
                act.activation(uk[:, :], kb[:, :], ACT.Relu, scale=-1.0).then_inc(u_done.sem, 1)
                act.activation(rk[:, :], kb[:, :], ACT.Relu)
                u_done.wait(act, t + 1)
                act.activation(ek[:, :], uk[:, :], ACT.Exp, scale=-1.0).then_inc(er_done.sem, 1)
                vb_done.wait(act, t + 1)
                kv_mm.wait(act, t - 1)
                act.activation(vr[:, tt % 2, 0], vf[:, :], ACT.Copy).then_inc(v_hi.sem, 1)
                k_done.wait(act, t + 1)
                act.activation(kr[:, tt % 2, 0], kf[:, :], ACT.Copy).then_inc(k_hi.sem, 1)

            x_used.start(act)
            er_done.start(act)
            front_norm(0)
            front_free(0)
            front_hi(0, 0, range(KC), 16)

            def batch(i, last):
                for q in range(BB):
                    for j in range(TB):
                        tt = q * TB + j
                        tile(TPB * i + tt, tt)
                        ahead = not (last and q == BB - 1)
                        nq, ng = (q + 1) % BB, BB * i + q + 1
                        if ahead and j == 0:
                            front_norm(ng)
                        if ahead and j == 1:
                            front_free(ng)
                        if ahead and j in (1, 2):
                            front_hi(ng, nq, range(2 * (j - 1), 2 * j), 16 * (i + 1 + (q + 1) // BB))

            with act.Fori(0, B - 1) as i:
                batch(i, False)
            batch(B - 1, True)

        @block.vector
        def _(dve):
            def front_stats(g):
                dve.wait_ge(x_in, 16 * (g + 1))
                ag_done.wait(dve, TB * g)
                for j in range(TB):
                    dve.bn_stats(st[:, j], xt[:, j]).then_inc(bn_done.sem, 1)
                bn_done.wait(dve, TB * (g + 1))
                nmr_done.wait(dve, g)
                dve.memset(spare[:, :], 0.0)
                for j in range(TB):
                    dve.bn_aggr(mv[:, j], st[:, j]).then_inc(ag_done.sem, 1)
                ag_done.wait(dve, TB * (g + 1))
                dve.tensor_scalar_add(var[:, :], mv[:, :, 1], LN_EPS).then_inc(var_done.sem, 1)
                sd_done.wait(dve, g + 1)
                dve.reciprocal(rstd[:, :], sd[:, :]).then_inc(rstd_done.sem, 1)
                rstd_done.wait(dve, g + 1)
                dve.scalar_tensor_tensor(nmr[:, :], mv[:, :, 0], -1.0, rstd[:, :], ALU.mult, ALU.mult)\
                   .then_inc(nmr_done.sem, 1)

            def front_split(g, b, q, chunks):
                for c in chunks:
                    tr_done.wait(dve, KC * g + c + 1)
                    lo_done.wait(dve, KC * g + c - 1)
                    dve.tensor_scalar(hf[:, c % 2], psT[c % 2][:, :], keep["modc"][:, b, CA, c:c + 1],
                                      keep["modc"][:, b, SA, c:c + 1], ALU.mult, ALU.add).then_inc(hf_done.sem, 1)
                for c in chunks:
                    hi_done.wait(dve, KC * g + c + 1)
                    dve.tensor_tensor(hT[q][:, 1, c], hf[:, c % 2], hT[q][:, 0, c].bitcast(F32),
                                      ALU.subtract).then_inc(lo_done.sem, 1)

            def tile(t, tt):
                k_mm.wait(dve, t + 1)
                er_done.wait(dve, t)
                dve.tensor_tensor(kb[:, :], psK[tt % 2][:, :], bkv[:, 0], ALU.add).then_inc(kb_done.sem, 1)
                v_mm.wait(dve, t + 1)
                v_lo.wait(dve, t)
                dve.tensor_tensor(vf[:, :], psV[:, :], bkv[:, 1], ALU.add).then_inc(vb_done.sem, 1)
                er_done.wait(dve, t + 1)
                k_lo.wait(dve, t)
                dve.tensor_tensor(kf[:, :], ek[:, :], rk[:, :], ALU.add).then_inc(k_done.sem, 1)
                v_hi.wait(dve, t + 1)
                kv_mm.wait(dve, t - 1)
                dve.tensor_tensor(vr[:, tt % 2, 1], vf[:, :], vr[:, tt % 2, 0].bitcast(F32),
                                  ALU.subtract).then_inc(v_lo.sem, 1)
                k_hi.wait(dve, t + 1)
                dve.tensor_tensor(kr[:, tt % 2, 1], kf[:, :], kr[:, tt % 2, 0].bitcast(F32),
                                  ALU.subtract).then_inc(k_lo.sem, 1)

            def sums(i):
                kv_mm.wait(dve, TPB * (i + 1))
                dve.tensor_copy(ksb[:, :], psS[:, :])
                for n in range(2):
                    pair = psKV[n][:, :].rearrange("p (h w d) -> p h w d", h=2, w=2)
                    dve.tensor_copy(kvs[:, n], pair[:, :, 0]).then_inc(sums_done.sem, 1)
                sums_done.wait(dve, 5 * i + 2)
                for n in range(2):
                    pair = psKV[n][:, :].rearrange("p (h w d) -> p h w d", h=2, w=2)
                    last = dve.tensor_tensor(keep["kvT"][:, i, 2 * n * P:2 * (n + 1) * P].rearrange("p (h d) -> p h d", h=2),
                                             kvs[:, n], pair[:, :, 1], ALU.add)
                last.then_inc(sums_done.sem, 1)
                ks_mm.wait(dve, i + 1)
                cols = psS[:, :].rearrange("p (h m) -> p h m", h=KVH)[:, :, 0:2]
                hi = keep["ks_hi"][:, i].rearrange("p (h m) -> p h m", m=2)
                lo = keep["ks_lo"][:, i].rearrange("p (h m) -> p h m", m=2)
                dve.tensor_scalar_mul(hi, cols, 1.0).then_inc(sums_done.sem, 1)
                sums_done.wait(dve, 5 * i + 4)
                dve.tensor_tensor(lo, cols, hi.bitcast(F32), ALU.subtract).then_inc(sums_done.sem, 1)

            for x in (hf_done, lo_done, kb_done, vb_done, k_done, k_lo, v_lo, sums_done, ag_done, nmr_done):
                x.start(dve)
            dve.wait_ge(bkv_in, 32)
            front_stats(0)
            front_split(0, 0, 0, (0, 1))
            front_split(0, 0, 0, (2, 3))

            def batch(i, last):
                for q in range(BB):
                    for j in range(TB):
                        tt = q * TB + j
                        tile(TPB * i + tt, tt)
                        ahead = not (last and q == BB - 1)
                        nq, ng = (q + 1) % BB, BB * i + q + 1
                        if ahead and j == 0:
                            front_stats(ng)
                        if ahead and j in (1, 2):
                            front_split(ng, i + (q + 1) // BB, nq, range(2 * (j - 1), 2 * j))
                sums(i)

            with dve.Fori(0, B - 1) as i:
                batch(i, False)
            batch(B - 1, True)

        @block.tensor
        def _(pe):
            def front_transpose(g, chunks):
                for c in chunks:
                    if c == 0:
                        z_done.wait(pe, TB * (g + 1))
                    hf_done.wait(pe, KC * g + c - 1)
                    for j in range(TB):
                        last = pe.transpose(psT[c % 2][:, j * P:(j + 1) * P], zt[:, j, c * P:(c + 1) * P],
                                            keep["ident"][:, :])
                    last.then_inc(tr_done.sem, 1)

            def tile(t, q, j):
                tt = q * TB + j
                tok = slice(j * P, (j + 1) * P)
                for n, (ps, free, done) in enumerate(((psK[tt % 2], kb_done, k_mm), (psV, vb_done, v_mm))):
                    free.wait(pe, t - 1 if n == 0 else t)
                    todo = [(a, w, c) for c in range(KC) for a, w in ((0, 0), (0, 1), (1, 0))]
                    for m, (a, w, c) in enumerate(todo):
                        wt = keep["wkv_lo" if w else "wkv_hi"]
                        last = pe.matmul(ps[:, :], hT[q][:, a, c, tok], wt[:, n, c],
                                         start=(m == 0), stop=(m == len(todo) - 1))
                    last.then_inc(done.sem, 1)

            def sums(t, tt):
                k_lo.wait(pe, t + 1)
                v_lo.wait(pe, t + 1)
                first, end = tt == 0, tt == TPB - 1
                k, v = kr[:, tt % 2], vr[:, tt % 2]
                for h in range(KVH):
                    at = slice(h * P, (h + 1) * P)
                    ps = psKV[h // 2][:, 2 * P * (h % 2):2 * P * (h % 2 + 1)]
                    pe.matmul(ps, v[:, 0, at], k[:, :, at], start=(first and h % 2 == 0), stop=False,
                              skip_group_check=True)
                    pe.matmul(ps[:, P:2 * P], v[:, 1, at], k[:, 0, at], start=False, stop=end,
                              skip_group_check=True)
                for a in range(2):
                    last = pe.matmul(psS[:, :], keep["ones"][:, :], k[:, a], start=(first and a == 0),
                                     stop=(end and a == 1), skip_group_check=True)
                last.then_inc(kv_mm.sem, 1)

            def key_columns(i):
                sums_done.wait(pe, 5 * i + 3)
                for h in range(KVH):
                    last = pe.transpose(psS[:, h * P:(h + 1) * P], ksb[:, h * P:(h + 1) * P], keep["ident"][:, :])
                last.then_inc(ks_mm.sem, 1)

            for x in (tr_done, kv_mm, v_mm):
                x.start(pe)
            front_transpose(0, range(KC))

            def batch(i, last):
                for q in range(BB):
                    for j in range(TB):
                        tt = q * TB + j
                        t = TPB * i + tt
                        if j == 0:
                            lo_done.wait(pe, KC * (BB * i + q + 1))
                        tile(t, q, j)
                        if tt == 1:
                            sums_done.wait(pe, 5 * i)
                        if tt >= 1:
                            sums(t - 1, tt - 1)
                        ahead = not (last and q == BB - 1)
                        if ahead and j in (1, 2):
                            front_transpose(BB * i + q + 1, range(2 * (j - 1), 2 * j))
                sums(TPB * i + TPB - 1, TPB - 1)
                key_columns(i)

            with pe.Fori(0, B - 1) as i:
                batch(i, False)
            batch(B - 1, True)


def queries(nc, io, keep):
    with Stage(nc, "q") as ctx:
        sem, count = ctx.sem, ctx.count

        def sb(name, shape, dt=F32):
            return ctx.enter_context(nc.sbuf_tensor(name, shape, dt))

        def psum(name, shape):
            return ctx.enter_context(nc.psum_tensor(name, shape, F32))

        STEPS = HEADS * BB
        WR = 2
        hT = [sb(f"qhT{q}", [P, 2, KC, BLK], F32R) for q in range(BB)]
        bq = sb("bq", [P, HEADS])
        gate = sb("gate", [P, D])
        kvb = sb("kvb", [P, D])
        wo = [sb(f"wo{n}", [P, D]) for n in range(WR)]
        w2f = sb("w2f", [P, D])
        w2 = [sb(f"w2_{n}", [P, 2, D + 2], F32R) for n in range(2)]
        bqn = sb("bqn", [P, HEADS])
        uq = sb("uq", [P, BLK])
        eq = sb("eq", [P, 2, BLK])
        rq = sb("rq", [P, 2, BLK])
        qf = sb("qf", [P, 2, BLK])
        qr = sb("qr", [P, 2, 2, BLK], F32R)
        nrm = sb("nrm", [P, 2, TB])
        rn = sb("rn", [P, 2, TB])
        xin = sb("xin", [P, BB, TB, D])
        acc = sb("acc", [P, BB, TB, D])
        st = sb("st2", [P, TPB, 6])
        spare = sb("spare2", [P, 1])
        mvb = sb("mvb", [P, TPB, 2])
        mv = sb("mv2", [P, B, TPB, 2])
        sd = sb("sd2", [P, B, TPB])
        HD = D // 2
        psQ = psum("psQ", [P, BLK])
        psO1 = psum("psO1", [P, TB, HD])
        psO2 = psum("psO2", [P, TB, D])
        psW = psum("psW", [P, D])

        bq_in, gate_in = sem("bq_in"), sem("gate_in")
        wo_in = [sem(f"wo_in{n}") for n in range(WR)]
        hT_in = [sem(f"hT_in{q}") for q in range(BB)]
        xin_in = sem("xin_in")
        acc_out = [sem(f"acc_out{q}") for q in range(BB)]
        acc_stored = count("acc_stored", BB)
        bn_done, ag_done, mv_done = count("bn_done2"), count("ag_done2", 1), count("mv_done2", 1)
        var_done, sd_done, rstd_done, nmr_done = sem("var2_done"), sem("sd2_done"), sem("rstd2_done"), sem("nmr2_done")
        kvb_done = count("kvb_done")
        w2_mm = count("w2_mm", WR)
        w2f_done, w2_hi, w2_lo = count("w2f_done", 1), count("w2_hi"), count("w2_lo", 1)
        q_mm = count("q_mm", BB)
        bqn_done = sem("bqn_done")
        u_done, r_done = count("u_done"), count("r_done", 1)
        er_done, qf_done = count("eqrq_done", 3), count("qf_done", 3)
        q_hi, q_lo = count("q_hi"), count("q_lo", 2)
        nrm_done, rn_done = count("nrm_done"), count("rn_done", 2)
        o_mm = count("o_mm", 2 * TB + 1)
        acc_done = count("acc_done", TB * STEPS)

        block = ctx.block()
        x_blocks = io["x"].rearrange("(g j p) d -> g p j d", j=TB, p=P)
        x1_blocks = io["x1"].rearrange("(g j p) d -> g p j d", j=TB, p=P)

        def batches(eng, slot):
            with eng.Fori(0, B - 1) as i:
                for s in range(STEPS):
                    slot(i, s, False)
            for s in range(STEPS):
                slot(B - 1, s, True)

        def later(i, s, n, last):
            if last and s + n >= STEPS:
                return []
            return [(i + (s + n) // STEPS, (s + n) % STEPS)]

        def next_head(i, s, last):
            return [(j, t // BB) for j, t in later(i, s, BB, last) if t % BB == 0]


        @block.sync
        def _(sp):
            def load_wo(i, h):
                w2_mm.wait(sp, HEADS * i + h - WR + 1)
                sp.dma_start(wo[h % WR][:, :], io["woT"][:, h]).then_inc(wo_in[h % WR], 16)

            def load_h(i, q):
                q_mm.wait(sp, STEPS * i - (BB - 1) + q)
                sp.dma_start(hT[q][:, :, :, :].bitcast(F32), io["hTs"][BB * i + q]).then_inc(hT_in[q], 16)

            sp.dma_start(bq[:, :], io["bq"]).then_inc(bq_in, 16)
            with sp.Fori(0, B) as i:
                w2f_done.wait(sp, HEADS * i)
                sp.dma_start(gate[:, :], io["modrows"][R_GA, i].partition_broadcast(P)).then_inc(gate_in, 16)
                for h in range(WR):
                    load_wo(i, h)
                for q in range(BB):
                    load_h(i, q)
                acc_done.wait(sp, TB * STEPS * i - TB * (STEPS - BB))
                for q in range(BB):
                    sp.dma_start(xin[:, q], x_blocks[BB * i + q]).then_inc(xin_in, 16)
                for h in range(WR, HEADS):
                    load_wo(i, h)

        @block.scalar
        def _(act):
            def w2_split(i, h):
                w2f_done.wait(act, HEADS * i + h + 1)
                o_mm.wait(act, TB * (STEPS * i + BB * (h - 1)))
                act.activation(w2[h % 2][:, 0, 0:D], w2f[:, :], ACT.Copy).then_inc(w2_hi.sem, 1)

            def exps(i, s):
                n, h = STEPS * i + s, s // BB
                q_mm.wait(act, n + 1)
                er_done.wait(act, n)
                qf_done.wait(act, n - 1)
                act.activation(uq[:, :], psQ[:, :], ACT.Relu, bias=bqn[:, h:h + 1], scale=-1.0)\
                   .then_inc(u_done.sem, 1)
                act.activation(rq[:, s % 2], psQ[:, :], ACT.Relu, bias=bq[:, h:h + 1]).then_inc(r_done.sem, 1)
                u_done.wait(act, n + 1)
                act.activation(eq[:, s % 2], uq[:, :], ACT.Exp, scale=-1.0).then_inc(er_done.sem, 1)

            def upper(i, s):
                n = STEPS * i + s
                qf_done.wait(act, n + 1)
                o_mm.wait(act, TB * (n - 1))
                act.activation(qr[:, s % 2, 0], qf[:, s % 2], ACT.Copy).then_inc(q_hi.sem, 1)

            for x in (r_done, er_done):
                x.start(act)
            act.wait_ge(bq_in, 16)
            act.mul(bqn[:, :], bq[:, :], -1.0).then_inc(bqn_done, 1)
            act.wait_ge(bqn_done, 1)
            def slot(i, s, last):
                for at in later(i, s, 1, last):
                    upper(*at)
                for at in later(i, s, 2, last):
                    exps(*at)
                for at in next_head(i, s, last):
                    w2_split(*at)

            exps(0, 0)
            w2_split(0, 0)
            upper(0, 0)
            exps(0, 1)
            batches(act, slot)
            act.wait_ge(var_done, 1)
            act.activation(sd[:, :, :], sd[:, :, :], ACT.Sqrt).then_inc(sd_done, 1)

        @block.vector
        def _(dve):
            def w2_gate(i, h):
                w2_mm.wait(dve, HEADS * i + h + 1)
                w2_lo.wait(dve, HEADS * i + h)
                dve.tensor_tensor(w2f[:, :], psW[:, :], gate[:, :], ALU.mult).then_inc(w2f_done.sem, 1)

            def w2_split(i, h):
                w2_hi.wait(dve, HEADS * i + h + 1)
                if h % GROUP < 2:
                    cols = slice(2 * (h // GROUP), 2 * (h // GROUP) + 2)
                    dve.tensor_scalar_mul(w2[h % 2][:, 0, D:D + 2], keep["ks_hi"][:, i, cols].bitcast(F32), 1.0)
                    dve.tensor_scalar_mul(w2[h % 2][:, 1, D:D + 2], keep["ks_lo"][:, i, cols].bitcast(F32), 1.0)
                dve.tensor_tensor(w2[h % 2][:, 1, 0:D], w2f[:, :], w2[h % 2][:, 0, 0:D].bitcast(F32),
                                  ALU.subtract).then_inc(w2_lo.sem, 1)

            def square(i, s):
                n = STEPS * i + s
                er_done.wait(dve, n + 1)
                q_lo.wait(dve, n - 1)
                dve.tensor_tensor(qf[:, s % 2], eq[:, s % 2], rq[:, s % 2], ALU.add)\
                   .then_inc(qf_done.sem, 1)

            def lower(i, s):
                n = STEPS * i + s
                q_hi.wait(dve, n + 1)
                dve.tensor_tensor(qr[:, s % 2, 1], qf[:, s % 2], qr[:, s % 2, 0].bitcast(F32),
                                  ALU.subtract).then_inc(q_lo.sem, 1)

            def norms(i, s):
                n = STEPS * i + s
                o_mm.wait(dve, TB * (n + 1))
                rn_done.wait(dve, n - 1)
                dve.tensor_scalar_add(nrm[:, s % 2], psO2[:, :, HD], NORM_EPS).then_inc(nrm_done.sem, 1)
                nrm_done.wait(dve, n + 1)
                acc_done.wait(dve, TB * (n - 1))
                dve.reciprocal(rn[:, s % 2], nrm[:, s % 2]).then_inc(rn_done.sem, 1)

            def add(i, s):
                n, q = STEPS * i + s, s % BB
                rn_done.wait(dve, n + 1)
                if s < BB:
                    acc_stored.wait(dve, BB * (i - 1) + q + 1)
                    dve.wait_ge(xin_in, 16 * BB * (i + 1))
                else:
                    acc_done.wait(dve, TB * (n - 1))
                base = xin if s < BB else acc
                for j in range(TB):
                    for half, ps in ((slice(0, HD), psO1[:, j]), (slice(HD, D), psO2[:, j, 0:HD])):
                        last = dve.scalar_tensor_tensor(acc[:, q, j, half], ps, rn[:, s % 2, j:j + 1],
                                                        base[:, q, j, half], ALU.mult, ALU.add)
                    last.then_inc(acc_done.sem, 1)

            def next_sums(i):
                w2_mm.wait(dve, HEADS * i)
                dve.tensor_scalar_mul(kvb[:, :], keep["kvT"][:, i], 1.0).then_inc(kvb_done.sem, 1)
                dve.wait_ge(gate_in, 16 * (i + 1))

            def stats(i, q):
                acc_done.wait(dve, TB * (STEPS * i + STEPS - BB + q + 1))
                ag_done.wait(dve, TPB * i)
                for j in range(TB):
                    dve.bn_stats(st[:, q * TB + j], acc[:, q, j]).then_inc(bn_done.sem, 1)

            def aggregate(i):
                mv_done.wait(dve, i)
                bn_done.wait(dve, TPB * (i + 1))
                dve.memset(spare[:, :], 0.0)
                for t in range(TPB):
                    dve.bn_aggr(mvb[:, t], st[:, t]).then_inc(ag_done.sem, 1)
                ag_done.wait(dve, TPB * (i + 1))
                dve.tensor_copy(mv[:, i], mvb[:, :, :]).then_inc(mv_done.sem, 1)

            for x in (ag_done, mv_done, w2f_done, w2_lo, qf_done, q_lo, rn_done, acc_done):
                x.start(dve)

            def slot(i, s, last):
                for at in later(i, s, 1, last):
                    lower(*at)
                if s == STEPS - BB - 1 and not last:
                    next_sums(i + 1)
                for at in next_head(i, s, last):
                    w2_gate(*at)
                for at in later(i, s, 2, last):
                    square(*at)
                for at in next_head(i, s, last):
                    w2_split(*at)
                norms(i, s)
                add(i, s)
                if s >= STEPS - BB:
                    stats(i, s - (STEPS - BB))
                if s == STEPS - 1:
                    aggregate(i)

            next_sums(0)
            w2_gate(0, 0)
            square(0, 0)
            w2_split(0, 0)
            lower(0, 0)
            square(0, 1)
            batches(dve, slot)
            mv_done.wait(dve, B)
            mean, var = mv[:, :, :, 0], mv[:, :, :, 1]
            dve.tensor_scalar_add(sd[:, :, :], var, LN_EPS).then_inc(var_done, 1)
            dve.wait_ge(sd_done, 1)
            dve.reciprocal(keep["rstd2"][:, :, :], sd[:, :, :]).then_inc(rstd_done, 1)
            dve.wait_ge(rstd_done, 1)
            dve.scalar_tensor_tensor(keep["nmr2"][:, :, :], mean, -1.0, keep["rstd2"][:, :, :], ALU.mult, ALU.mult)\
               .then_inc(nmr_done, 1)

        @block.tensor
        def _(pe):
            def query(i, s):
                n, h, q = STEPS * i + s, s // BB, s % BB
                if s < BB:
                    pe.wait_ge(hT_in[q], 16 * (i + 1))
                r_done.wait(pe, n)
                todo = [(w, a, c) for c in range(KC) for w, a in ((0, 0), (0, 1), (1, 0))]
                for m, (w, a, c) in enumerate(todo):
                    wt = keep["wq_lo" if w else "wq_hi"]
                    last = pe.matmul(psQ[:, :], wt[:, h, c], hT[q][:, a, c],
                                     start=(m == 0), stop=(m == len(todo) - 1))
                last.then_inc(q_mm.sem, 1)

            def weight(i, h):
                pe.wait_ge(wo_in[h % WR], 16 * (HEADS // WR * i + h // WR + 1))
                w2f_done.wait(pe, HEADS * i + h)
                g = h // GROUP
                pe.matmul(psW[:, :], kvb[:, g * P:(g + 1) * P], wo[h % WR][:, :], start=True, stop=True)\
                  .then_inc(w2_mm.sem, 1)

            def output(i, s):
                n, h = STEPS * i + s, s // BB
                q_lo.wait(pe, n + 1)
                w2_lo.wait(pe, HEADS * i + h + 1)
                for j in range(TB):
                    tok = slice(j * P, (j + 1) * P)
                    if j == 0:
                        acc_done.wait(pe, TB * (n - 1) + 2)
                    elif j == 1 or j == 3:
                        acc_done.wait(pe, TB * (n - 1) + j + 1)
                    elif j == 2:
                        acc_done.wait(pe, TB * n)
                    for half, ps in ((slice(0, HD), psO1[:, j]), (slice(HD, D + 2), psO2[:, j, 0:HD + 2])):
                        for m, (a, w) in enumerate(((0, 0), (0, 1), (1, 0))):
                            last = pe.matmul(ps, qr[:, s % 2, a, tok], w2[h % 2][:, w, half],
                                             start=(m == 0), stop=(m == 2))
                    last.then_inc(o_mm.sem, 1)

            for x in (w2_mm, q_mm, o_mm):
                x.start(pe)

            def slot(i, s, last):
                for j, h in next_head(i, s, last):
                    if h == 0:
                        kvb_done.wait(pe, j + 1)
                    weight(j, h)
                for at in later(i, s, 2, last):
                    query(*at)
                output(i, s)

            query(0, 0)
            kvb_done.wait(pe, 1)
            weight(0, 0)
            query(0, 1)
            batches(pe, slot)

        @block.gpsimd
        def _(pool):
            acc_stored.start(pool)
            with pool.Fori(0, B) as i:
                for q in range(BB):
                    acc_done.wait(pool, TB * (STEPS * i + STEPS - BB + q + 1))
                    pool.dma_start(x1_blocks[BB * i + q], acc[:, q]).then_inc(acc_out[q], 16)
                for q in range(BB):
                    pool.wait_ge(acc_out[q], 16 * (i + 1))
                    pool.sem_inc(acc_stored.sem, 1)


GU = 2 * FF
GR = FF + EXPERTS
NF = len(FCH)
FPAD = NF * P
SLOTS = TOPK * TILES + EXPERTS
RAW_DMAS = 3


def split_products(chunks):
    return [(a, w, c) for c in range(chunks) for a, w in ((0, 0), (0, 1), (1, 0))]


def load_expert(pool, io, keep, e):
    pool.dma_start(keep["gu_raw"][:, :, :], io["gu_e"][e]).then_inc(keep["raw_in"], 16)
    pool.dma_start(keep["dn_raw"][:, 0:NF - 1], io["dn_e"][e, 0:(NF - 1) * P].rearrange("(c p) d -> p c d", p=P))\
        .then_inc(keep["raw_in"], 16)
    pool.dma_start(keep["dn_raw"][0:FCH[-1], NF - 1], io["dn_e"][e, (NF - 1) * P:FF]).then_inc(keep["raw_in"], 16)


def split_expert(pool, keep, buf, e):
    f = FCH[-1]
    pairs = [(keep["gu_raw"][:, :, :], keep["gu_x"][:, buf]),
             (keep["dn_raw"][:, 0:NF - 1], keep["dn_x"][:, buf, :, 0:NF - 1]),
             (keep["dn_raw"][0:f, NF - 1], keep["dn_x"][0:f, buf, :, NF - 1])]
    for raw, halves in pairs:
        pool.tensor_copy(halves[:, 0], raw).then_inc(keep["upper_done"], 1)
    pool.wait_ge(keep["upper_done"], len(pairs) * (e + 1))
    for raw, halves in pairs:
        pool.tensor_tensor(halves[:, 1], raw, halves[:, 0].bitcast(F32), ALU.subtract).then_inc(keep["split_done"], 1)


SPLIT_STEPS = 3


def shared_expert(nc, io, keep):
    with Stage(nc, "sh") as ctx:
        sem, count = ctx.sem, ctx.count

        def sb(name, shape, dt=F32):
            return ctx.enter_context(nc.sbuf_tensor(name, shape, dt))

        def psum(name, shape):
            return ctx.enter_context(nc.psum_tensor(name, shape, F32))

        AHEAD = 3
        XB = 4
        place = keep["act"][:, TILES // 2:].rearrange("p t f -> p (t f)")
        gu_raw = place[:, 0:KC * (GR + FF)].rearrange("p (c f) -> p c f", c=KC)
        dn_raw = place[:, KC * (GR + FF):KC * (GR + FF) + NF * D].rearrange("p (c d) -> p c d", c=NF)
        gu = sb("gu", [P, 2, KC, GR + FF], F32R)
        rowsb = sb("rowsb", [P, 2, D])
        x1t = sb("x1t", [P, XB, D])
        h2t = sb("h2t", [P, XB, D])
        hTr = sb("hTr", [P, 2, 2, D], F32R)
        sil = sb("sil", [P, 2, FF])
        psT = [psum(f"psT_{n}", [P, D]) for n in range(2)]
        psG = [psum(f"psG{n}", [P, D]) for n in range(2)]
        psU = [psum(f"psU{n}", [P, D]) for n in range(2)]

        gu_in = [sem(f"gu_in{c}") for c in range(KC)]
        dn_in = [sem(f"dn_in{c}") for c in range(NF)]
        raw_hi, raw_lo = sem("raw_hi"), sem("raw_lo")
        norm_rows_in = sem("norm_rows_in")
        x_in = [sem(f"x1_in{n}") for n in range(XB)]
        h2_out = [sem(f"h2_out{n}") for n in range(XB)]
        z_done, sc_done, h2_done = count("z2_done", XB), count("sc2_done", 1), count("h2_done", 1)
        t_mm, hi_done, lo_done = count("t_mm", XB), count("hi2_done", 1), count("lo2_done", 2)
        g_mm, u_mm = count("g_mm"), count("u_mm", 2)
        sil_done, a_done, lg_done = count("sil_done", 1), count("a_done", 2), count("lg_done", 2)

        x1_tiles = io["x1"].rearrange("(t p) d -> t p d", p=P)
        h2_tiles = io["h2"].rearrange("(t p) d -> t p d", p=P)
        block = ctx.block()

        def slots(eng, step):
            with eng.Fori(0, B - 1) as i:
                for tt in range(TPB):
                    step(i, tt, False)
            for tt in range(TPB):
                step(B - 1, tt, True)

        def in_range(tt, n, last):
            return not last or tt + n < TPB


        @block.sync
        def _(sp):
            def load_x(i, tt):
                t = TPB * i + tt
                z_done.wait(sp, t - XB + 1)
                sp.dma_start(x1t[:, tt % XB], x1_tiles[t]).then_inc(x_in[tt % XB], 16)

            def store_h2(i, tt):
                t = TPB * i + tt
                h2_done.wait(sp, t + 1)
                sp.dma_start(h2_tiles[t], h2t[:, tt % XB]).then_inc(h2_out[tt % XB], 16)

            def norm_rows(i):
                h2_done.wait(sp, TPB * i)
                for n, r in ((0, R_SB), (1, R_CB)):
                    sp.dma_start(rowsb[:, n], io["modrows"][r, i].partition_broadcast(P)).then_inc(norm_rows_in, 16)

            def step(i, tt, last):
                if in_range(tt, XB, last):
                    load_x(*ahead(i, tt, XB))
                if tt + AHEAD == TPB and not last:
                    norm_rows(i + 1)
                if in_range(tt, AHEAD, last):
                    store_h2(*ahead(i, tt, AHEAD))

            for n in range(XB):
                sp.sem_inc(h2_out[n], 16)
            norm_rows(0)
            load_x(0, 0)
            for c in range(KC):
                sp.dma_start(gu_raw[:, c], io["gu_s"][:, c]).then_inc(gu_in[c], 16)
            for n in range(1, XB):
                load_x(0, n)
            for c in range(NF):
                sp.dma_start(dn_raw[0:FCH[c], c], io["dn_s"][c * P:c * P + FCH[c]]).then_inc(dn_in[c], 16)
            for t in range(AHEAD):
                store_h2(0, t)
            slots(sp, step)
            for n in range(XB):
                sp.wait_ge(h2_out[n], 16 * (TILES // XB + 1))

        @block.gpsimd
        def _(pool):
            for n in dn_in:
                pool.wait_ge(n, 16)
            for e in range(2):
                load_expert(pool, io, keep, e)
                pool.wait_ge(keep["raw_in"], 16 * RAW_DMAS * (e + 1))
                split_expert(pool, keep, e, e)
                pool.wait_ge(keep["split_done"], SPLIT_STEPS * (e + 1))
            load_expert(pool, io, keep, 2)

        @block.scalar
        def _(act):
            def norm(i, tt):
                t = TPB * i + tt
                act.wait_ge(x_in[tt % XB], 16 * ((TPB // XB) * i + tt // XB + 1))
                t_mm.wait(act, t - XB + 1)
                act.wait_ge(h2_out[tt % XB], 16 * ((TPB // XB) * i + tt // XB + 1))
                act.activation(h2t[:, tt % XB], x1t[:, tt % XB], ACT.Identity, bias=keep["nmr2"][:, i, tt:tt + 1],
                               scale=keep["rstd2"][:, i, tt:tt + 1]).then_inc(z_done.sem, 1)

            def upper(i, tt):
                t = TPB * i + tt
                t_mm.wait(act, t + 1)
                u_mm.wait(act, t - 1)
                act.activation(hTr[:, tt % 2, 0], psT[tt % 2][:, :], ACT.Copy).then_inc(hi_done.sem, 1)

            def silu(i, tt):
                t = TPB * i + tt
                g_mm.wait(act, t + 1)
                a_done.wait(act, t - 1)
                act.activation(sil[:, tt % 2], psG[tt % 2][:, 0:FF], ACT.Silu).then_inc(sil_done.sem, 1)

            def step(i, tt, last):
                if in_range(tt, 1, last):
                    upper(*ahead(i, tt, 1))
                if in_range(tt, AHEAD, last):
                    norm(*ahead(i, tt, AHEAD))
                silu(i, tt)

            for x in (z_done, hi_done, sil_done):
                x.start(act)
            norm(0, 0)
            for c in range(KC):
                act.wait_ge(gu_in[c], 16)
                act.activation(gu[:, 0, c], gu_raw[:, c], ACT.Copy).then_inc(raw_hi, 1)
            for c in range(NF):
                act.wait_ge(dn_in[c], 16)
                act.activation(keep["dn"][0:FCH[c], 0, c], dn_raw[0:FCH[c], c], ACT.Copy).then_inc(raw_hi, 1)
            norm(0, 1)
            upper(0, 0)
            norm(0, 2)
            slots(act, step)

        @block.vector
        def _(dve):
            def modulate(i, tt):
                t = TPB * i + tt
                z_done.wait(dve, t + 1)
                if tt == 0:
                    dve.wait_ge(norm_rows_in, 32 * (i + 1))
                dve.tensor_tensor(h2t[:, tt % XB], h2t[:, tt % XB], rowsb[:, 1], ALU.mult).then_inc(sc_done.sem, 1)
                sc_done.wait(dve, t + 1)
                dve.tensor_tensor(h2t[:, tt % XB], h2t[:, tt % XB], rowsb[:, 0], ALU.add).then_inc(h2_done.sem, 1)

            def lower(i, tt):
                hi_done.wait(dve, TPB * i + tt + 1)
                dve.tensor_tensor(hTr[:, tt % 2, 1], psT[tt % 2][:, :], hTr[:, tt % 2, 0].bitcast(F32), ALU.subtract)\
                   .then_inc(lo_done.sem, 1)

            def gated(i, tt):
                t = TPB * i + tt
                sil_done.wait(dve, t + 1)
                dve.tensor_scalar_mul(keep["logits"][:, bass.ds(t, 1)], psG[tt % 2][:, FF:GR].unsqueeze(1), 1.0)\
                   .then_inc(lg_done.sem, 1)
                u_mm.wait(dve, t + 1)
                dve.tensor_tensor(keep["act"][:, bass.ds(t, 1)], sil[:, tt % 2].unsqueeze(1),
                                  psU[tt % 2][:, 0:FF].unsqueeze(1), ALU.mult).then_inc(a_done.sem, 1)

            def step(i, tt, last):
                if in_range(tt, 1, last):
                    lower(*ahead(i, tt, 1))
                if in_range(tt, AHEAD, last):
                    modulate(*ahead(i, tt, AHEAD))
                gated(i, tt)

            for x in (sc_done, h2_done, lo_done, a_done, lg_done):
                x.start(dve)
            modulate(0, 0)
            for c in range(KC):
                dve.wait_ge(raw_hi, c + 1)
                dve.tensor_tensor(gu[:, 1, c], gu_raw[:, c], gu[:, 0, c].bitcast(F32), ALU.subtract).then_inc(raw_lo, 1)
            for c in range(NF):
                dve.wait_ge(raw_hi, KC + c + 1)
                f = FCH[c]
                dve.tensor_tensor(keep["dn"][0:f, 1, c], dn_raw[0:f, c], keep["dn"][0:f, 0, c].bitcast(F32),
                                  ALU.subtract).then_inc(raw_lo, 1)
            modulate(0, 1)
            lower(0, 0)
            modulate(0, 2)
            slots(dve, step)

        @block.tensor
        def _(pe):
            def transpose_h(i, tt):
                t = TPB * i + tt
                h2_done.wait(pe, t + 1)
                lo_done.wait(pe, t - 1)
                for c in range(KC):
                    last = pe.transpose(psT[tt % 2][:, c * P:(c + 1) * P], h2t[:, tt % XB, c * P:(c + 1) * P],
                                        keep["ident"][:, :])
                last.then_inc(t_mm.sem, 1)

            def gate_up(i, tt):
                t = TPB * i + tt
                lo_done.wait(pe, t + 1)
                for ps, cols, free, done in ((psG[tt % 2], slice(0, GR), lg_done, g_mm),
                                             (psU[tt % 2], slice(GR, GR + FF), a_done, u_mm)):
                    free.wait(pe, t - 1)
                    todo = split_products(KC)
                    for m, (a, w, c) in enumerate(todo):
                        last = pe.matmul(ps[:, 0:cols.stop - cols.start], hTr[:, tt % 2, a, c * P:(c + 1) * P],
                                         gu[:, w, c, cols], start=(m == 0), stop=(m == len(todo) - 1))
                    last.then_inc(done.sem, 1)

            def step(i, tt, last):
                if in_range(tt, 1, last):
                    transpose_h(*ahead(i, tt, 1))
                gate_up(i, tt)

            for x in (t_mm, u_mm):
                x.start(pe)
            transpose_h(0, 0)
            pe.wait_ge(raw_lo, KC)
            slots(pe, step)


def ahead(i, tt, n):
    return i + (tt + n) // TPB, (tt + n) % TPB


def route(nc, io, keep):
    with Stage(nc, "rt") as ctx:
        sem = ctx.sem

        def sb(name, shape, dt=F32):
            return ctx.enter_context(nc.sbuf_tensor(name, shape, dt))

        TE = TILES * EXPERTS
        PAIRS = TOPK * TILES
        PART = 16
        big = [P, TILES, EXPERTS]
        bias2 = sb("bias2", [P, 2, EXPERTS])
        bias = sb("bias", [P, EXPERTS])
        lg = sb("lg", big)
        pr = sb("pr", big)
        top = sb("top", [P, TOPK, TILES])
        key = sb("key", big)
        kmax = sb("kmax", [P, TILES])
        oh = [sb(f"oh{k}", big) for k in range(TOPK)]
        rev = sb("rev", [P, EXPERTS])
        den = sb("den_", [P, TILES])
        mask = sb("mask", big, F32R)
        tri_f = sb("tri_f", [P, P])
        tri = sb("tri", [P, P], F32R)
        all_f = sb("all_f", [P, P])
        all_r = sb("all_r", [P, P], F32R)
        scan = [sb(f"scan{n}", big) for n in range(2)]
        before = sb("before", big)
        n_i = sb("n_i", [P, EXPERTS], I32)
        t_i = sb("t_i", [P, EXPERTS], I32)
        tiles = sb("tiles", [P, EXPERTS])
        ends = [sb(f"ends{n}", [P, EXPERTS]) for n in range(2)]
        base = sb("base", [P, EXPERTS])
        place = sb("place", big)
        prod = sb("prod", big)
        slot = sb("slot", [P, TOPK, TILES])
        tile_i = sb("tile_i", [P, PAIRS], I32)
        row_i = sb("row_i", [P, PAIRS], I32)
        tile_f = sb("tile_f", [P, PAIRS])
        row_f = sb("row_f", [P, PAIRS])
        iota_r = sb("iota_r", [P, P])
        iota_s = sb("iota_s", [P, SLOTS])
        tok = sb("tok", [P, TILES])
        ge = sb("ge", [P, SLOTS, EXPERTS])
        emap = sb("emap", [P, SLOTS])
        isnew = sb("isnew", [P, SLOTS])
        oh_row = sb("oh_row", [P, 2, PART, P], F32R)
        oh_tile = sb("oh_tile", [P, PART, SLOTS])
        tok_tile = sb("tok_tile", [P, 2, PART, SLOTS], F32R)
        psB = ctx.enter_context(nc.psum_tensor("psB", [P, D], F32))
        psT = ctx.enter_context(nc.psum_tensor("psTot", [P, D], F32))
        psI = ctx.enter_context(nc.psum_tensor("psI", [P, D], F32))

        bias_in = sem("bias_in")
        iotas, tri_set, tri_done = sem("iotas"), sem("tri_set"), sem("tri_done")
        d = sem("route_steps")
        lg_done, e_done = sem("lg_done"), sem("ex_done")
        mask_done, counts_mm = sem("mask_done"), sem("counts_mm")
        split_done = sem("split_done")
        row_done, tile_done, tok_done = sem("oh_row_done"), sem("oh_tile_done"), sem("tok_tile_done")
        id_mm = sem("id_mm")
        ids_done = sem("ids_done")
        block = ctx.block()

        @block.sync
        def _(sp):
            for n, name in enumerate(("br", "rb")):
                sp.dma_start(bias2[:, n], io[name].partition_broadcast(P)).then_inc(bias_in, 16)

        @block.gpsimd
        def _(pool):
            f = dict(allow_small_or_imprecise_dtypes=True)
            pool.iota(iota_r[:, :], pattern=[[1, P]], base=0, channel_multiplier=0, **f).then_inc(iotas, 1)
            pool.iota(iota_s[:, :], pattern=[[1, SLOTS]], base=0, channel_multiplier=0, **f).then_inc(iotas, 1)
            pool.iota(tok[:, :], pattern=[[P, TILES]], base=0, channel_multiplier=1, **f).then_inc(iotas, 1)
            pool.iota(rev[:, :], pattern=[[-1, EXPERTS]], base=EXPERTS, channel_multiplier=0, **f).then_inc(iotas, 1)
            pool.memset(all_f[:, :], 1.0).then_inc(tri_set, 1)
            pool.wait_ge(tri_set, 1)
            pool.affine_select(out=tri_f[:, :], in_=all_f[:, :], compare_op=ALU.is_gt, fill=0.0, base=0,
                               pattern=[[1, P]], channel_multiplier=-1).then_inc(tri_done, 1)
            for n in range(PAIRS // PART):
                pool.wait_ge(tile_done, n + 1)
                if n >= 2:
                    pool.wait_ge(id_mm, n - 1)
                pool.tensor_tensor(tok_tile[:, n % 2], oh_tile[:, :, :],
                                   keep["tok2"][:, n * PART:(n + 1) * PART].unsqueeze(2)
                                   .broadcast_to((P, PART, SLOTS)), ALU.mult).then_inc(tok_done, 1)

        @block.scalar
        def _(act):
            act.wait_ge(lg_done, 1)
            act.activation(pr[:, :, :], lg[:, :, :], ACT.Exp, scale=-1.0).then_inc(e_done, 1)

        @block.vector
        def _(dve):
            at = [0]

            def then(ins):
                at[0] += 1
                ins.then_inc(d, 1)
                dve.wait_ge(d, at[0])

            def over_tiles(x):
                return x[:, :].unsqueeze(1).broadcast_to(tuple(big))

            def over_experts(x):
                return x.unsqueeze(2).broadcast_to(tuple(big))

            then(dve.memset(isnew[:, :], 0.0))
            dve.wait_ge(bias_in, 32)
            dve.wait_ge(iotas, 4)
            dve.wait_ge(tri_done, 1)
            then(dve.tensor_copy(tri[:, :], tri_f[:, :]))
            then(dve.tensor_copy(all_r[:, :], all_f[:, :]))
            then(dve.tensor_copy(keep["tok2"][:, 0:TILES], tok[:, :]))
            then(dve.tensor_copy(keep["tok2"][:, TILES:PAIRS], tok[:, :]))
            then(dve.tensor_tensor(bias[:, :], bias2[:, 0], bias2[:, 1], ALU.add))
            dve.tensor_tensor(lg[:, :, :], keep["logits"][:, :, :], over_tiles(bias), ALU.add).then_inc(lg_done, 1)
            dve.wait_ge(e_done, 1)
            then(dve.tensor_scalar_add(pr[:, :, :], pr[:, :, :], 1.0))
            then(dve.reciprocal(pr[:, :, :], pr[:, :, :]))
            for k in range(TOPK):
                then(dve.reduce_max(top[:, k], pr[:, :, :], AX_X))
                then(dve.tensor_tensor(key[:, :, :], pr[:, :, :], over_experts(top[:, k]), ALU.is_equal))
                then(dve.tensor_tensor(key[:, :, :], key[:, :, :], over_tiles(rev), ALU.mult))
                then(dve.reduce_max(kmax[:, :], key[:, :, :], AX_X))
                then(dve.tensor_tensor(oh[k][:, :, :], key[:, :, :], over_experts(kmax[:, :]), ALU.is_equal))
                if k == 0:
                    then(dve.scalar_tensor_tensor(pr[:, :, :], oh[0][:, :, :], -2.0, pr[:, :, :], ALU.mult, ALU.add))
            dve.tensor_tensor(mask[:, :, :], oh[0][:, :, :], oh[1][:, :, :], ALU.add).then_inc(mask_done, 1)
            then(dve.tensor_tensor(den[:, :], top[:, 0], top[:, 1], ALU.add))
            then(dve.reciprocal(den[:, :], den[:, :]))
            for k in range(TOPK):
                then(dve.tensor_tensor(keep["w"][:, k], top[:, k], den[:, :], ALU.mult))
            dve.wait_ge(counts_mm, 1)
            then(dve.tensor_copy(scan[0][:, :, :].rearrange("p t e -> p (t e)"), psT[:, 0:TE]))
            then(dve.tensor_copy(before[:, :, :], scan[0][:, :, :]))
            n, step = 0, 1
            while step < TILES:
                a, b = scan[n], scan[1 - n]
                then(dve.tensor_tensor(b[:, step:], a[:, step:], a[:, :TILES - step], ALU.add))
                then(dve.tensor_copy(b[:, :step], a[:, :step]))
                n, step = 1 - n, 2 * step
            total = scan[n]
            then(dve.tensor_copy(n_i[:, :], total[:, TILES - 1]))
            then(dve.tensor_scalar(t_i[:, :], n_i[:, :], P.bit_length() - 1, None, ALU.arith_shift_right))
            then(dve.tensor_copy(tiles[:, :], t_i[:, :]))
            then(dve.tensor_scalar_add(tiles[:, :], tiles[:, :], 1.0))
            then(dve.tensor_copy(ends[0][:, :], tiles[:, :]))
            m, step = 0, 1
            while step < EXPERTS:
                a, b = ends[m], ends[1 - m]
                then(dve.tensor_tensor(b[:, step:], a[:, step:], a[:, :EXPERTS - step], ALU.add))
                then(dve.tensor_copy(b[:, :step], a[:, :step]))
                m, step = 1 - m, 2 * step
            end = ends[m]
            then(dve.tensor_tensor(base[:, :], end[:, :], tiles[:, :], ALU.subtract))
            then(dve.tensor_scalar_mul(base[:, :], base[:, :], float(P)))
            then(dve.tensor_tensor(before[:, :, :], total[:, :, :], before[:, :, :], ALU.subtract))
            then(dve.tensor_tensor(place[:, :, :], before[:, :, :], over_tiles(base), ALU.add))
            then(dve.tensor_tensor(place[:, :, :], place[:, :, :],
                                   psB[:, 0:TE].rearrange("p (t e) -> p t e", e=EXPERTS), ALU.add))
            for k in range(TOPK):
                then(dve.tensor_tensor(prod[:, :, :], place[:, :, :], oh[k][:, :, :], ALU.mult))
                then(dve.reduce_sum(slot[:, k], prod[:, :, :], AX_X))
            then(dve.tensor_copy(keep["slot_i"][:, :], slot[:, :, :].rearrange("p k t -> p (k t)")))
            then(dve.tensor_scalar(tile_i[:, :], keep["slot_i"][:, :], P.bit_length() - 1, None, ALU.arith_shift_right))
            then(dve.tensor_scalar(row_i[:, :], keep["slot_i"][:, :], P - 1, None, ALU.bitwise_and))
            dve.tensor_copy(tile_f[:, :], tile_i[:, :]).then_inc(split_done, 1)
            dve.tensor_copy(row_f[:, :], row_i[:, :]).then_inc(split_done, 1)
            dve.wait_ge(split_done, 2)
            wide = (P, SLOTS, EXPERTS)
            then(dve.tensor_tensor(ge[:, :, :], iota_s[:, :].unsqueeze(2).broadcast_to(wide),
                                   end[:, :].unsqueeze(1).broadcast_to(wide), ALU.is_ge))
            then(dve.reduce_sum(emap[:, :], ge[:, :, :], AX_X))
            then(dve.tensor_scalar_min(emap[:, :], emap[:, :], float(EXPERTS - 1)))
            then(dve.tensor_copy(keep["tile_expert"][:, :], emap[:, :]))
            then(dve.tensor_tensor(isnew[:, 1:], emap[:, 1:], emap[:, :SLOTS - 1], ALU.is_gt))
            then(dve.tensor_tensor(isnew[:, 1:], isnew[:, 1:], emap[:, 1:], ALU.mult))
            then(dve.scalar_tensor_tensor(isnew[:, 1:], isnew[:, 1:], float(EXPERTS - 1), isnew[:, 1:],
                                          ALU.is_lt, ALU.mult))
            then(dve.tensor_copy(keep["turn"][:, 1:], isnew[:, :]))
            then(dve.tensor_copy(keep["turn"][:, 0:1], isnew[:, 0:1]))
            for n in range(PAIRS // PART):
                part = slice(n * PART, (n + 1) * PART)
                wide = (P, PART, SLOTS)
                if n >= 1:
                    dve.wait_ge(tok_done, n)
                dve.tensor_tensor(oh_tile[:, :, :], iota_s[:, :].unsqueeze(1).broadcast_to(wide),
                                  tile_f[:, part].unsqueeze(2).broadcast_to(wide), ALU.is_equal).then_inc(tile_done, 1)
                if n >= 2:
                    dve.wait_ge(id_mm, n - 1)
                wide = (P, PART, P)
                dve.tensor_tensor(oh_row[:, n % 2], iota_r[:, :].unsqueeze(1).broadcast_to(wide),
                                  row_f[:, part].unsqueeze(2).broadcast_to(wide), ALU.is_equal).then_inc(row_done, 1)
            dve.wait_ge(id_mm, PAIRS // PART)
            dve.tensor_copy(keep["ids"][:, :], psI[:, 0:SLOTS]).then_inc(ids_done, 1)

        @block.tensor
        def _(pe):
            pe.wait_ge(mask_done, 1)
            m = mask[:, :, :].rearrange("p t e -> p (t e)")
            pe.matmul(psB[:, 0:TE], tri[:, :], m, start=True, stop=True)
            pe.matmul(psT[:, 0:TE], all_r[:, :], m, start=True, stop=True).then_inc(counts_mm, 1)
            for n in range(PAIRS // PART):
                pe.wait_ge(row_done, n + 1)
                pe.wait_ge(tok_done, n + 1)
                for m in range(PART):
                    last = pe.matmul(psI[:, 0:SLOTS], oh_row[:, n % 2, m], tok_tile[:, n % 2, m],
                                     start=(n == 0 and m == 0), stop=(n == PAIRS // PART - 1 and m == PART - 1))
                last.then_inc(id_mm, 1)


def routed_experts(nc, io, keep):
    with Stage(nc, "re") as ctx:
        sem, count = ctx.sem, ctx.count

        def sb(name, shape, dt=F32):
            return ctx.enter_context(nc.sbuf_tensor(name, shape, dt))

        def psum(name, shape):
            return ctx.enter_context(nc.psum_tensor(name, shape, F32))

        U = 8
        YB = 4
        LAG = U + 1
        idx = sb("idx", [P, U], I32)
        hg = sb("hg", [P, U, D])
        hgT = sb("hgT", [P, 2, 2, D], F32R)
        sil = sb("sil2", [P, FF])
        act_t = sb("act_t2", [P, FPAD])
        aT = sb("aT", [P, 2, FPAD], F32R)
        y = sb("y_t", [P, YB, D])
        psT = psum("psT2", [P, D])
        psG = psum("psG2", [P, D])
        psU = psum("psU2", [P, D])
        psA = psum("psA2", [P, D])
        psY = [psum(f"psY2{n}", [P, D]) for n in range(2)]

        idx_done = count("idx_done", U)
        idx_seen = sem("idx_seen")
        g_in = [sem(f"g_in{n}") for n in range(U)]
        y_out = [sem(f"y_out{n}") for n in range(YB)]
        pad_done = sem("pad_done2")
        t_mm, hi_done, lo_done = count("t_mm2", U), count("hgT_hi"), count("hgT_lo", 1)
        g_mm, u_mm = count("g_mm2"), count("u_mm2", 2)
        sil_done, a_done = count("sil_done2", 1), count("a_done2", 1)
        ta_mm, ahi_done, alo_done = count("ta_mm2", 1), count("ahi_done"), count("alo_done", 1)
        y_mm, y_done = count("y_mm2", 1), count("y_done", 2)
        block = ctx.block()
        y_tiles = io["y"].rearrange("(s p) d -> s p d", p=P)

        def slots(eng, step):
            with eng.Fori(0, SLOTS // U - 1) as i:
                for r in range(U):
                    step(i, r, False)
            for r in range(U):
                step(SLOTS // U - 1, r, True)

        def in_range(r, n, last):
            return not last or r + n < U

        def on(i, r, n):
            return i + (r + n) // U, (r + n) % U

        @block.sync
        def _(sp):
            for n in range(YB):
                sp.sem_inc(y_out[n], 16)
            with sp.Fori(0, SLOTS // YB) as i:
                for r in range(YB):
                    y_done.wait(sp, YB * i + r + 1)
                    sp.dma_start(y_tiles[YB * i + r], y[:, r]).then_inc(y_out[r], 16)
            for n in range(YB):
                sp.wait_ge(y_out[n], 16 * (SLOTS // YB + 1))

        @block.gpsimd
        def _(pool):
            def gather(s, r):
                t_mm.wait(pool, s - U + 1)
                pool.tensor_copy(idx[:, r:r + 1], keep["ids"][:, bass.ds(s, 1)]).then_inc(idx_done.sem, 1)
                idx_done.wait(pool, s + 1)
                pool.sem_inc(idx_seen, 1)
                pool.indirect_dma_start(out=hg[:, r], out_offset=None, in_=io["h2"],
                                        in_offset=bass.IndirectOffsetOnAxis(ap=idx[:, r:r + 1].bitcast(U32), axis=0))\
                    .then_inc(g_in[r], 16)

            def check(s, at):
                e = pool.value_load(keep["turn"][0:1, bass.ds(at, 1)], min_val=0, max_val=EXPERTS - 1)
                with pool.If(e > 0):
                    y_mm.wait(pool, s)
                    pool.wait_ge(keep["raw_in"], 16 * RAW_DMAS * (e + 2))
                    with pool.If(e % 2 == 0):
                        split_expert(pool, keep, 1, e + 1)
                    with pool.If(e % 2 == 1):
                        split_expert(pool, keep, 0, e + 1)
                    with pool.If(e < EXPERTS - 2):
                        early = pool.value_load(keep["turn"][0:1, bass.ds(at, 1)], min_val=1, max_val=EXPERTS - 3)
                        pool.wait_ge(keep["split_done"], SPLIT_STEPS * (e + 2))
                        load_expert(pool, io, keep, early + 2)

            idx_done.start(pool)
            for r in range(U):
                gather(r, r)
            with pool.Fori(1, SLOTS // U) as i:
                for r in range(U):
                    gather(U * i + r, r)
                    check(U * i + r - LAG, U * i + r - LAG + 1)
            with pool.Fori(SLOTS - LAG, SLOTS) as s:
                check(s, s + 1)

        @block.scalar
        def _(act):
            def upper(i, r):
                s = U * i + r
                t_mm.wait(act, s + 1)
                u_mm.wait(act, s - 1)
                act.activation(hgT[:, r % 2, 0], psT[:, :], ACT.Copy).then_inc(hi_done.sem, 1)

            def silu(i, r):
                s = U * i + r
                g_mm.wait(act, s + 1)
                a_done.wait(act, s)
                act.activation(sil[:, :], psG[:, 0:FF], ACT.Silu).then_inc(sil_done.sem, 1)

            def upper_a(i, r):
                s = U * i + r
                ta_mm.wait(act, s + 1)
                y_mm.wait(act, s)
                act.activation(aT[:, 0], psA[:, 0:FPAD], ACT.Copy).then_inc(ahi_done.sem, 1)

            def copy_y(i, r):
                s = U * i + r
                y_mm.wait(act, s + 1)
                act.wait_ge(y_out[r % YB], 16 * (U // YB * i + r // YB + 1))
                act.activation(y[:, r % YB], psY[r % 2][:, :], ACT.Copy).then_inc(y_done.sem, 1)

            def step(i, r, last):
                upper_a(i, r)
                if in_range(r, 2, last):
                    upper(*on(i, r, 2))
                if in_range(r, 1, last):
                    silu(*on(i, r, 1))
                copy_y(i, r)

            for x in (sil_done, y_done):
                x.start(act)
            act.wait_ge(pad_done, 1)
            upper(0, 0)
            upper(0, 1)
            silu(0, 0)
            slots(act, step)

        @block.vector
        def _(dve):
            def lower(i, r):
                s = U * i + r
                hi_done.wait(dve, s + 1)
                dve.tensor_tensor(hgT[:, r % 2, 1], psT[:, :], hgT[:, r % 2, 0].bitcast(F32), ALU.subtract)\
                   .then_inc(lo_done.sem, 1)

            def gated(i, r):
                s = U * i + r
                sil_done.wait(dve, s + 1)
                u_mm.wait(dve, s + 1)
                ta_mm.wait(dve, s)
                dve.tensor_tensor(act_t[:, 0:FF], sil[:, :], psU[:, 0:FF], ALU.mult).then_inc(a_done.sem, 1)

            def lower_a(i, r):
                ahi_done.wait(dve, U * i + r + 1)
                dve.tensor_tensor(aT[:, 1], psA[:, 0:FPAD], aT[:, 0].bitcast(F32), ALU.subtract)\
                   .then_inc(alo_done.sem, 1)

            def step(i, r, last):
                lower_a(i, r)
                if in_range(r, 2, last):
                    lower(*on(i, r, 2))
                if in_range(r, 1, last):
                    gated(*on(i, r, 1))

            for x in (lo_done, a_done, alo_done):
                x.start(dve)
            dve.memset(act_t[:, :], 0.0).then_inc(pad_done, 1)
            dve.wait_ge(pad_done, 1)
            lower(0, 0)
            lower(0, 1)
            gated(0, 0)
            slots(dve, step)

        @block.tensor
        def _(pe):
            def transpose_h(i, r):
                s = U * i + r
                pe.wait_ge(g_in[r], 16 * (i + 1))
                lo_done.wait(pe, s)
                for c in range(KC):
                    last = pe.transpose(psT[:, c * P:(c + 1) * P], hg[:, r, c * P:(c + 1) * P], keep["ident"][:, :])
                last.then_inc(t_mm.sem, 1)

            def expert(i, r):
                e = pe.value_load(keep["tile_expert"][0:1, bass.ds(U * i + r, 1)], min_val=0, max_val=EXPERTS - 1)
                return e, e % 2

            def gate_up(i, r):
                s = U * i + r
                e, buf = expert(i, r)
                pe.wait_ge(keep["split_done"], SPLIT_STEPS * (e + 1))
                lo_done.wait(pe, s + 1)
                for n, (ps, done, free) in enumerate(((psG, g_mm, sil_done), (psU, u_mm, a_done))):
                    free.wait(pe, s)
                    todo = split_products(KC)
                    for m, (a, w, c) in enumerate(todo):
                        last = pe.matmul(ps[:, 0:FF], hgT[:, r % 2, a, c * P:(c + 1) * P],
                                         keep["gu_x"][:, buf, w, c, n * FF:(n + 1) * FF],
                                         start=(m == 0), stop=(m == len(todo) - 1))
                    last.then_inc(done.sem, 1)

            def transpose_a(i, r):
                s = U * i + r
                a_done.wait(pe, s + 1)
                alo_done.wait(pe, s)
                for c in range(NF):
                    last = pe.transpose(psA[:, c * P:(c + 1) * P], act_t[:, c * P:(c + 1) * P], keep["ident"][:, :])
                last.then_inc(ta_mm.sem, 1)

            def down(i, r):
                s = U * i + r
                e, buf = expert(i, r)
                alo_done.wait(pe, s + 1)
                y_done.wait(pe, s - 1)
                todo = split_products(NF)
                for m, (a, w, c) in enumerate(todo):
                    f = FCH[c]
                    last = pe.matmul(psY[r % 2][:, :], aT[0:f, a, c * P:(c + 1) * P], keep["dn_x"][0:f, buf, w, c],
                                     start=(m == 0), stop=(m == len(todo) - 1))
                last.then_inc(y_mm.sem, 1)

            def step(i, r, last):
                transpose_a(i, r)
                if in_range(r, 2, last):
                    transpose_h(*on(i, r, 2))
                if in_range(r, 1, last):
                    gate_up(*on(i, r, 1))
                down(i, r)

            for x in (t_mm, u_mm, ta_mm, y_mm):
                x.start(pe)
            transpose_h(0, 0)
            transpose_h(0, 1)
            gate_up(0, 0)
            slots(pe, step)


def combine(nc, io, keep):
    with Stage(nc, "cb") as ctx:
        sem, count = ctx.sem, ctx.count

        def sb(name, shape, dt=F32):
            return ctx.enter_context(nc.sbuf_tensor(name, shape, dt))

        def psum(name, shape):
            return ctx.enter_context(nc.psum_tensor(name, shape, F32))

        U = 4
        gate = sb("gate_", [P, B, D])
        idx = sb("idx_", [P, U, TOPK], I32)
        yk = sb("yk", [P, U, TOPK, D])
        x1 = sb("x1_t", [P, U, D])
        act_t = sb("act_t3", [P, 2, FF])
        aT = sb("aT_", [P, 2, 2, FPAD], F32R)
        y0 = sb("y0", [P, 2, D])
        y01 = sb("y01", [P, 2, D])
        ysum = sb("ysum", [P, 2, D])
        ygate = sb("ygate", [P, 2, D])
        psA = [psum(f"psA3{n}", [P, D]) for n in range(2)]
        psY = [psum(f"psY3{n}", [P, D]) for n in range(2)]
        gate_in = sem("gatec_in")
        idx_done = count("idxc_done")
        idx_seen = sem("idxc_seen")
        pad_done = sem("pad_done3")
        y_in = [sem(f"y_in{n}") for n in range(U)]
        x1_in = [sem(f"x1c_in{n}") for n in range(U)]
        out_done = [sem(f"out_done{n}") for n in range(U)]
        act_here = count("act_here")
        ta_mm, ahi_done, alo_done = count("ta_mm3", 2), count("ahi3_done"), count("alo3_done", 2)
        y_mm = count("y_mm3", 2)
        y0_done, y01_done = count("y0_done"), count("y01_done", U)
        ysum_done, ygate_done = count("ysum_done", 2), count("ygate_done", 2)
        out_sum = count("out_sum", 2)
        x1_tiles = io["x1"].rearrange("(t p) d -> t p d", p=P)
        out_tiles = io["out"].rearrange("(t p) d -> t p d", p=P)
        block = ctx.block()

        def slots(eng, step):
            with eng.Fori(0, B - 1) as i:
                for tt in range(TPB):
                    step(i, tt, False)
            for tt in range(TPB):
                step(B - 1, tt, True)

        def in_range(tt, n, last):
            return not last or tt + n < TPB


        @block.sync
        def _(sp):
            def load(i, tt):
                sp.wait_ge(out_done[tt % U], 16 * ((TPB // U) * i + tt // U + 1))
                sp.dma_start(x1[:, tt % U], x1_tiles[TPB * i + tt]).then_inc(x1_in[tt % U], 16)

            def store(i, tt):
                out_sum.wait(sp, TPB * i + tt + 1)
                sp.dma_start(out_tiles[TPB * i + tt], x1[:, tt % U]).then_inc(out_done[tt % U], 16)

            def step(i, tt, last):
                if in_range(tt, U - 1, last):
                    load(*ahead(i, tt, U - 1))
                store(i, tt)

            for n in range(U):
                sp.sem_inc(out_done[n], 16)
            for b in range(B):
                sp.dma_start(gate[:, b], io["modrows"][R_GB, b].partition_broadcast(P)).then_inc(gate_in, 16)
            for n in range(U - 1):
                load(0, n)
            slots(sp, step)
            for n in range(U):
                sp.wait_ge(out_done[n], 16 * (TILES // U + 1))

        @block.gpsimd
        def _(pool):
            with pool.Fori(0, TILES // U) as i:
                for r in range(U):
                    t = U * i + r
                    y01_done.wait(pool, t - U + 1)
                    for k in range(TOPK):
                        pool.tensor_copy(idx[:, r, k:k + 1], keep["slot_i"][:, bass.ds(k * TILES + t, 1)])\
                            .then_inc(idx_done.sem, 1)
                    idx_done.wait(pool, TOPK * (t + 1))
                    pool.sem_inc(idx_seen, 1)
                    for k in range(TOPK):
                        pool.indirect_dma_start(out=yk[:, r, k], out_offset=None, in_=io["y"],
                                                in_offset=bass.IndirectOffsetOnAxis(
                                                    ap=idx[:, r, k:k + 1].bitcast(U32), axis=0)).then_inc(y_in[r], 16)

        @block.scalar
        def _(act):
            def place(i, tt):
                t = TPB * i + tt
                ta_mm.wait(act, t - 1)
                act.activation(act_t[:, tt % 2].unsqueeze(1), keep["act"][:, bass.ds(t, 1)], ACT.Copy)\
                   .then_inc(act_here.sem, 1)

            def upper_a(i, tt):
                t = TPB * i + tt
                ta_mm.wait(act, t + 1)
                y_mm.wait(act, t - 1)
                act.activation(aT[:, tt % 2, 0], psA[tt % 2][:, 0:FPAD], ACT.Copy).then_inc(ahi_done.sem, 1)

            def weigh(i, tt):
                t = TPB * i + tt
                act.wait_ge(y_in[tt % U], 16 * TOPK * ((TPB // U) * i + tt // U + 1))
                y01_done.wait(act, t - 1)
                act.activation(y0[:, tt % 2], yk[:, tt % U, 0], ACT.Copy,
                               scale=keep["w"][:, 0, bass.ds(t, 1)]).then_inc(y0_done.sem, 1)

            def step(i, tt, last):
                if in_range(tt, 2, last):
                    place(*ahead(i, tt, 2))
                if in_range(tt, 1, last):
                    upper_a(*ahead(i, tt, 1))
                    weigh(*ahead(i, tt, 1))

            act.wait_ge(pad_done, 2)
            place(0, 0)
            place(0, 1)
            upper_a(0, 0)
            weigh(0, 0)
            slots(act, step)

        @block.vector
        def _(dve):
            def lower_a(i, tt):
                ahi_done.wait(dve, TPB * i + tt + 1)
                dve.tensor_tensor(aT[:, tt % 2, 1], psA[tt % 2][:, 0:FPAD], aT[:, tt % 2, 0].bitcast(F32),
                                  ALU.subtract).then_inc(alo_done.sem, 1)

            def add_experts(i, tt):
                t = TPB * i + tt
                y0_done.wait(dve, t + 1)
                ysum_done.wait(dve, t - 1)
                dve.scalar_tensor_tensor(y01[:, tt % 2], yk[:, tt % U, 1], keep["w"][:, 1, bass.ds(t, 1)],
                                         y0[:, tt % 2], ALU.mult, ALU.add).then_inc(y01_done.sem, 1)

            def finish(i, tt):
                t = TPB * i + tt
                y01_done.wait(dve, t + 1)
                y_mm.wait(dve, t + 1)
                ygate_done.wait(dve, t - 1)
                dve.tensor_tensor(ysum[:, tt % 2], psY[tt % 2][:, :], y01[:, tt % 2], ALU.add).then_inc(ysum_done.sem, 1)
                ysum_done.wait(dve, t + 1)
                out_sum.wait(dve, t - 1)
                dve.tensor_tensor(ygate[:, tt % 2].unsqueeze(1), ysum[:, tt % 2].unsqueeze(1),
                                  gate[:, bass.ds(i, 1)], ALU.mult).then_inc(ygate_done.sem, 1)
                ygate_done.wait(dve, t + 1)
                dve.wait_ge(x1_in[tt % U], 16 * ((TPB // U) * i + tt // U + 1))
                dve.tensor_tensor(x1[:, tt % U], ygate[:, tt % 2], x1[:, tt % U], ALU.add).then_inc(out_sum.sem, 1)

            def step(i, tt, last):
                if in_range(tt, 1, last):
                    lower_a(*ahead(i, tt, 1))
                    add_experts(*ahead(i, tt, 1))
                finish(i, tt)

            for x in (alo_done, y01_done, ysum_done, ygate_done, out_sum):
                x.start(dve)
            for n in range(2):
                dve.memset(psA[n][:, 0:FPAD], 0.0).then_inc(pad_done, 1)
            dve.wait_ge(gate_in, 16 * B)
            lower_a(0, 0)
            add_experts(0, 0)
            slots(dve, step)

        @block.tensor
        def _(pe):
            def transpose_a(i, tt):
                t = TPB * i + tt
                act_here.wait(pe, t + 1)
                alo_done.wait(pe, t - 1)
                for c in range(NF):
                    f = FCH[c]
                    last = pe.transpose(psA[tt % 2][0:f, c * P:(c + 1) * P], act_t[:, tt % 2, c * P:c * P + f],
                                        keep["ident"][:, :])
                last.then_inc(ta_mm.sem, 1)

            def down(i, tt):
                t = TPB * i + tt
                alo_done.wait(pe, t + 1)
                ysum_done.wait(pe, t - 1)
                todo = split_products(NF)
                for m, (a, w, c) in enumerate(todo):
                    f = FCH[c]
                    last = pe.matmul(psY[tt % 2][:, :], aT[0:f, tt % 2, a, c * P:(c + 1) * P], keep["dn"][0:f, w, c],
                                     start=(m == 0), stop=(m == len(todo) - 1))
                last.then_inc(y_mm.sem, 1)

            def step(i, tt, last):
                if in_range(tt, 1, last):
                    transpose_a(*ahead(i, tt, 1))
                down(i, tt)

            for x in (ta_mm, y_mm):
                x.start(pe)
            pe.wait_ge(pad_done, 2)
            transpose_a(0, 0)
            slots(pe, step)


def block_program(nc, io):
    with ExitStack() as ctx:
        def sb(name, shape, dt=F32):
            return ctx.enter_context(nc.sbuf_tensor(name, shape, dt))

        keep = {
            "ident": sb("ident", [P, P]),
            "ones": sb("ones", [P, P], F32R),
            "rstd2": sb("rstd2", [P, B, TPB]),
            "nmr2": sb("nmr2", [P, B, TPB]),
            "logits": sb("logits", [P, TILES, EXPERTS]),
            "w": sb("w", [P, TOPK, TILES]),
            "slot_i": sb("slot_i", [P, TOPK * TILES], I32),
            "tok2": sb("tok2", [P, TOPK * TILES]),
            "ids": sb("ids", [P, SLOTS], I32),
            "tile_expert": sb("tile_expert", [P, SLOTS], I32),
            "turn": sb("turn", [P, SLOTS + 1], I32),
        }
        with ExitStack() as attn:
            def ab(name, shape, dt=F32):
                return attn.enter_context(nc.sbuf_tensor(name, shape, dt))

            keep["modc"] = ab("modc", [P, B, 2, KC])
            keep["kvT"] = ab("kvT", [P, B, D])
            keep["ks_hi"] = ab("ks_hi", [P, B, 2 * KVH], F32R)
            keep["ks_lo"] = ab("ks_lo", [P, B, 2 * KVH], F32R)
            keep["wq_hi"] = ab("wq_hi", [P, HEADS, KC, P], F32R)
            keep["wq_lo"] = ab("wq_lo", [P, HEADS, KC, P], F32R)
            with ExitStack() as kv:
                keep["wkv_hi"] = kv.enter_context(nc.sbuf_tensor("wkv_hi", [P, 2, KC, D], F32R))
                keep["wkv_lo"] = kv.enter_context(nc.sbuf_tensor("wkv_lo", [P, 2, KC, D], F32R))
                setup(nc, io, keep)
                keys_values(nc, io, keep)
            queries(nc, io, keep)
        def late(name, shape, dt=F32):
            keep[name] = sb(name, shape, dt)

        late("act", [P, TILES, FF])
        late("dn", [P, 2, NF, D], F32R)
        with ExitStack() as ffn:
            def fb(name, shape, dt=F32):
                keep[name] = ffn.enter_context(nc.sbuf_tensor(name, shape, dt))

            fb("gu_raw", [P, KC, GU])
            fb("dn_raw", [P, NF, D])
            fb("gu_x", [P, 2, 2, KC, GU], F32R)
            fb("dn_x", [P, 2, 2, NF, D], F32R)
            for name in ("raw_in", "upper_done", "split_done"):
                keep[name] = ctx.enter_context(nc.semaphore(name))
            shared_expert(nc, io, keep)
            route(nc, io, keep)
            routed_experts(nc, io, keep)
        combine(nc, io, keep)


def chunked(w):
    k, n = w.shape
    return w.reshape(k // P, P, n).transpose(1, 0, 2)


def kernel(**inputs):
    import concourse.bacc as bacc
    from concourse.bass_utils import run_bass_kernel_spmd

    a = {k.split("_", 1)[1]: np.asarray(v) for k, v in inputs.items()}
    laid_out = {
        "x": a["attn_hidden_states"].reshape(TOK, D),
        "wqT": chunked(a["attn_Wq"].T).reshape(P, KC, HEADS, P).transpose(0, 2, 1, 3),
        "bq": a["attn_bq"].reshape(HEADS, P).T,
        "wkvT": np.stack([chunked(a["attn_Wk"].T), chunked(a["attn_Wv"].T)], 1),
        "bk": a["attn_bk"],
        "bv": a["attn_bv"],
        "woT": a["attn_Wo"].T.reshape(HEADS, P, D).transpose(1, 0, 2),
        "cT": chunked(a["c"].T).reshape(P, KC * B),
        "wmod": chunked(a["wmod"]).reshape(P, KC, 3, 2 * D).transpose(0, 2, 1, 3),
        "br": a["ffn_br"],
        "rb": a["ffn_rb"],
        "gu_s": chunked(np.concatenate([a["ffn_Wg_s"], a["ffn_Wr"], a["ffn_Wu_s"]], 1)),
        "dn_s": a["ffn_Wd_s"],
        "gu_e": np.stack([chunked(w) for w in np.concatenate([a["ffn_Wg"], a["ffn_Wu"]], 2)]),
        "dn_e": a["ffn_Wd"],
    }
    laid_out = {k: np.ascontiguousarray(v) for k, v in laid_out.items()}
    nc = bacc.Bacc("TRN2", target_bir_lowering=False, num_devices=1)
    io = {k: nc.dram_tensor(f"in_{k}", v.shape, F32, kind="ExternalInput").ap() for k, v in laid_out.items()}
    out = nc.dram_tensor("out", (TOK, D), F32, kind="ExternalOutput").ap()
    io["out"] = out
    for name, rows in (("x1", TOK), ("h2", TOK), ("y", SLOTS * P)):
        io[name] = nc.dram_tensor(f"dram_{name}", (rows, D), F32, kind="Internal").ap()
    io["modrows"] = nc.dram_tensor("modrows", (len(ROWS), B, D), F32, kind="Internal").ap()
    io["hTs"] = nc.dram_tensor("hTs", (B * BB, P, 2, KC, BLK), F32, kind="Internal").ap()
    block_program(nc, io)
    r = run_bass_kernel_spmd(nc, [{f"in_{k}": v for k, v in laid_out.items()}], core_ids=[0])
    return r.results[0]["out"].reshape(B, S, D)
```

```python
from contextlib import ExitStack

import numpy as np

import concourse.bass as bass
from concourse import mybir

F32 = mybir.dt.float32
F32R = mybir.dt.float32r
I32 = mybir.dt.int32
U32 = mybir.dt.uint32
ALU = mybir.AluOpType
ACT = mybir.ActivationFunctionType
AX_X = mybir.AxisListType.X

P = 128
B, S, D = 4, 1024, 512
HEADS, KVH = 16, 4
GROUP = HEADS // KVH
KC = D // P
BLK = 512
TB = BLK // P
BB = S // BLK
TPB = S // P
TOK = B * S
TILES = TOK // P
EXPERTS, TOPK, FF = 8, 2, 352
FCH = [P, P, FF - 2 * P]
LN_EPS, NORM_EPS = 1e-5, 1e-6
MAG = 0.25
SA, CA, GA, SB, CB, GB = range(6)
ROWS = [GA, SB, CB, GB]
R_GA, R_SB, R_CB, R_GB = range(4)


class Count:

    def __init__(self, sem, head, done):
        self.sem = sem
        self.head = head
        self.done = done

    def start(self, eng):
        eng.sem_inc(self.sem, self.head + self.done)

    def wait(self, eng, n):
        eng.wait_ge(self.sem, n + self.head)


class Stage(ExitStack):

    def __init__(self, nc, keep, name):
        super().__init__()
        self.nc, self.keep, self.name = nc, keep, name
        self.sems, self.held = [], ExitStack()

    def sem(self, name):
        self.sems.append(self.held.enter_context(self.nc.semaphore(f"{self.name}_{name}")))
        return self.sems[-1]

    def count(self, name, head=0, done=0):
        return Count(self.sem(name), head, done)

    def clear_previous(self, pool):
        for s in self.keep["previous"].sems:
            pool.sem_clear(s)

    def leave(self):
        if "previous" in self.keep:
            self.keep["previous"].held.close()
        self.keep["previous"] = self

    def block(self):
        self.callback(self.leave)
        return self.enter_context(self.nc.Block())


def setup(nc, io, keep):
    with Stage(nc, keep, "set") as ctx:
        sem = ctx.sem

        def sb(name, shape, dt=F32):
            return ctx.enter_context(nc.sbuf_tensor(name, shape, dt))

        wkv_raw = sb("wkv_raw", [P, 2, KC, D])
        wmod = sb("wmod", [P, 3, KC, 2 * D])
        cT = sb("cT", [P, KC * B])
        den = sb("den", [P, KC * B])
        sc = sb("sc", [P, KC, B])
        rows = sb("rows", [B, len(ROWS), D])
        first = sb("first", [B, 2, D])
        gabs = sb("gabs", [B, 2, D])
        mag, sgn = gabs, first
        ones_f = sb("ones_f", [P, P])
        ps1 = ctx.enter_context(nc.psum_tensor("ps1", [P, 2, D], F32))
        psR = ctx.enter_context(nc.psum_tensor("psR", [P, 4, D], F32))
        psC = ctx.enter_context(nc.psum_tensor("psC", [P, D], F32))

        c_in = sem("c_in")
        wmod_in = [sem(f"wmod_in{n}") for n in range(3)]
        wkv_in = [sem(f"wkv_in{n}") for n in range(2)]
        e_done, den_done, rec_done, sc_done = sem("e_done"), sem("den_done"), sem("rec_done"), sem("sc_done")
        ident_zero, ident_done = sem("ident_zero"), sem("ident_done")
        ones_set, ones_done = sem("ones_set"), sem("ones_done")
        rows_mm, cols_mm = sem("rows_mm"), sem("cols_mm")
        abs_done, mag_done, sgn_done, rows_done = sem("abs_done"), sem("mag_done"), sem("sgn_done"), sem("rows_done")
        first_mm, first_done, cols_done = sem("first_mm"), sem("first_done"), sem("cols_done")
        x_in, bn_done, ag_done, var_done = sem("x0_in"), sem("bn0_done"), sem("ag0_done"), sem("var0_done")
        sd_done, rstd_done, nmr_done, z_done = sem("sd0_done"), sem("rstd0_done"), sem("nmr0_done"), sem("z0_done")
        xt, zt, st, mv, var, sd, rstd, nmr = keep["front"]
        hi_done, lo_done = sem("hi_done"), sem("lo_done")
        rows_out = sem("rows_out")
        block = ctx.block()

        @block.sync
        def _(sp):
            sp.dma_start(cT[:, :], io["cT"]).then_inc(c_in, 16)
            sp.dma_start(wmod[:, 0], io["wmod"][:, 0]).then_inc(wmod_in[0], 16)
            sp.dma_start(xt[:, :, :], io["x"][0:BLK].rearrange("(j p) d -> p j d", p=P)).then_inc(x_in, 16)
            sp.dma_start(wmod[:, 1], io["wmod"][:, 1]).then_inc(wmod_in[1], 16)
            sp.dma_start(wmod[:, 2], io["wmod"][:, 2]).then_inc(wmod_in[2], 16)
            for n in range(2):
                sp.dma_start(wkv_raw[:, n], io["wkvT"][:, n]).then_inc(wkv_in[n], 16)
            sp.wait_ge(rows_done, 4)
            sp.dma_start(io["modrows"].rearrange("v b d -> b v d"), rows[:, :, :]).then_inc(rows_out, 16)
            sp.wait_ge(rows_out, 16)

        @block.gpsimd
        def _(pool):
            pool.memset(keep["ident"][:, :], 0.0).then_inc(ident_zero, 1)
            pool.wait_ge(ident_zero, 1)
            pool.affine_select(out=keep["ident"][:, :], in_=keep["ident"][:, :], compare_op=ALU.not_equal, fill=1.0,
                               base=0, pattern=[[-1, P]], channel_multiplier=1).then_inc(ident_done, 1)

        @block.scalar
        def _(act):
            act.wait_ge(c_in, 16)
            act.activation(den[:, :], cT[:, :], ACT.Exp, scale=-1.0).then_inc(e_done, 1)
            act.wait_ge(var_done, 1)
            act.activation(sd[:, :], var[:, :], ACT.Sqrt).then_inc(sd_done, 1)
            act.wait_ge(nmr_done, 1)
            for j in range(TB):
                act.activation(zt[:, j], xt[:, j], ACT.Identity, bias=nmr[:, j:j + 1],
                               scale=rstd[:, j:j + 1]).then_inc(z_done, 1)
            for n in range(2):
                act.wait_ge(wkv_in[n], 16)
                act.activation(keep["wkv_hi"][:, n], wkv_raw[:, n], ACT.Copy).then_inc(hi_done, 1)
            act.wait_ge(rows_mm, 4)
            for n, v in enumerate((R_GA, R_GB)):
                act.activation(gabs[:, n], psR[0:B, v], ACT.Abs).then_inc(abs_done, 1)

        @block.vector
        def _(dve):
            dve.memset(ones_f[:, :], 1.0).then_inc(ones_set, 1)
            dve.wait_ge(ones_set, 1)
            dve.tensor_copy(keep["ones"][:, :], ones_f[:, :]).then_inc(ones_done, 1)
            dve.wait_ge(e_done, 1)
            dve.tensor_scalar_add(den[:, :], den[:, :], 1.0).then_inc(den_done, 1)
            dve.wait_ge(den_done, 1)
            dve.reciprocal(den[:, :], den[:, :]).then_inc(rec_done, 1)
            dve.wait_ge(rec_done, 1)
            dve.tensor_tensor(sc[:, :, :].rearrange("p c b -> p (c b)"), cT[:, :], den[:, :], ALU.mult).then_inc(sc_done, 1)
            for v in (SA, CA):
                dve.wait_ge(first_mm, v + 1)
                dve.tensor_scalar_add(first[:, v], ps1[0:B, v], float(v == CA)).then_inc(first_done, 1)
            dve.wait_ge(cols_mm, 1)
            cols = psC[:, 0:2 * KC * B].rearrange("p (v n b) -> p b v n", v=2, n=KC)
            dve.tensor_copy(keep["modc"][:, :, :, :], cols).then_inc(cols_done, 1)
            dve.wait_ge(x_in, 16)
            for j in range(TB):
                dve.bn_stats(st[:, j], xt[:, j]).then_inc(bn_done, 1)
            dve.wait_ge(bn_done, TB)
            for j in range(TB):
                dve.bn_aggr(mv[:, j], st[:, j]).then_inc(ag_done, 1)
            dve.wait_ge(ag_done, TB)
            dve.tensor_scalar_add(var[:, :], mv[:, :, 1], LN_EPS).then_inc(var_done, 1)
            dve.wait_ge(sd_done, 1)
            dve.reciprocal(rstd[:, :], sd[:, :]).then_inc(rstd_done, 1)
            dve.wait_ge(rstd_done, 1)
            dve.scalar_tensor_tensor(nmr[:, :], mv[:, :, 0], -1.0, rstd[:, :], ALU.mult, ALU.mult).then_inc(nmr_done, 1)
            for n in range(2):
                dve.wait_ge(hi_done, n + 1)
                dve.tensor_tensor(keep["wkv_lo"][:, n], wkv_raw[:, n], keep["wkv_hi"][:, n].bitcast(F32),
                                  ALU.subtract).then_inc(lo_done, 1)
            dve.wait_ge(rows_mm, 4)
            dve.tensor_copy(rows[:, R_SB], psR[0:B, R_SB]).then_inc(rows_done, 1)
            dve.tensor_scalar_add(rows[:, R_CB], psR[0:B, R_CB], 1.0).then_inc(rows_done, 1)
            for n, v in enumerate((R_GA, R_GB)):
                dve.wait_ge(abs_done, n + 1)
                dve.tensor_scalar_max(mag[:, n], gabs[:, n], MAG).then_inc(mag_done, 1)
                dve.tensor_scalar(sgn[:, n], psR[0:B, v], 0.0, 2.0, ALU.is_ge, ALU.mult).then_inc(sgn_done, 1)
                dve.wait_ge(mag_done, n + 1)
                dve.wait_ge(sgn_done, n + 1)
                dve.scalar_tensor_tensor(rows[:, v], sgn[:, n], -1.0, mag[:, n], ALU.add, ALU.mult).then_inc(rows_done, 1)

        @block.tensor
        def _(pe):
            pe.wait_ge(sc_done, 1)
            pe.wait_ge(wmod_in[0], 16)
            for v in (SA, CA):
                for c in range(KC):
                    last = pe.matmul(ps1[0:B, v], sc[:, c, :], wmod[:, 0, c, v * D:(v + 1) * D],
                                     start=(c == 0), stop=(c == KC - 1))
                last.then_inc(first_mm, 1)
            pe.wait_ge(ident_done, 1)
            for v in (SA, CA):
                pe.wait_ge(first_done, v + 1)
                for n in range(KC):
                    at = (v * KC + n) * B
                    last = pe.transpose(psC[:, at:at + B], first[:, v, n * P:(n + 1) * P], keep["ident"][0:B, 0:B])
            last.then_inc(cols_mm, 1)
            for r, v in enumerate(ROWS):
                pe.wait_ge(wmod_in[v // 2], 16)
                for c in range(KC):
                    last = pe.matmul(psR[0:B, r], sc[:, c, :], wmod[:, v // 2, c, (v % 2) * D:(v % 2 + 1) * D],
                                     start=(c == 0), stop=(c == KC - 1))
                last.then_inc(rows_mm, 1)


def keys_values(nc, io, keep):
    with Stage(nc, keep, "kv") as ctx:
        sem, count = ctx.sem, ctx.count

        def sb(name, shape, dt=F32):
            return ctx.enter_context(nc.sbuf_tensor(name, shape, dt))

        def psum(name, shape):
            return ctx.enter_context(nc.psum_tensor(name, shape, F32))

        QW = 2
        hT = [sb(f"hT{q}", [P, 2, KC, BLK], F32R) for q in range(BB)]
        xt, zt, st, mv, var, sd, rstd, nmr = keep["front"]
        spare = sb("spare", [P, 1])
        hf = sb("hf", [P, 2, BLK])
        bkv = sb("bkv", [P, 2, D])
        kb = sb("kb", [P, D])
        uk = sb("uk", [P, D])
        ek = sb("ek", [P, D])
        rk = sb("rk", [P, D])
        kf = sb("kf", [P, D])
        vf = sb("vf", [P, D])
        kvs = sb("kvs", [P, 2, 2, P])
        ksb = sb("ksb", [P, B, D])
        kr = sb("kr", [P, 2, 2, D], F32R)
        vr = sb("vr", [P, 2, 2, D], F32R)
        wq_raw = sb("wq_raw", [P, QW, KC, P])
        psT = [psum(f"psT{n}", [P, BLK]) for n in range(2)]
        psK = [psum(f"psK{n}", [P, D]) for n in range(2)]
        psV = psum("psV", [P, D])
        psKV = [psum(f"psKV{n}", [P, D]) for n in range(2)]
        psS = psum("psS", [P, D])

        bkv_in, x_in, wq_in = sem("bkv_in"), sem("x_in"), sem("wq_in")
        hT_out = [sem(f"hT_out{q}") for q in range(BB)]
        x_used = count("x_used", 1, 1)
        bn_done, ag_done, var_done = count("bn_done", 0, TB), count("ag_done", 1, TB), count("var_done", 0, 1)
        sd_done, rstd_done, nmr_done = count("sd_done", 0, 1), count("rstd_done", 0, 1), count("nmr_done", 1, 1)
        z_done = count("z_done", 0, TB)
        tr_done = count("tr_done", KC)
        hf_done = count("hf_done", 2)
        hi_done = count("h_hi_done")
        lo_done = count("h_lo_done", 2)
        k_mm, v_mm = count("k_mm"), count("v_mm", TB + 1)
        kb_done = count("kb_done", 2)
        vb_done = count("vb_done", 2)
        u_done = count("u_done")
        er_done = count("er_done", 1)
        k_done = count("k_done", 1)
        k_hi, k_lo = count("k_hi"), count("k_lo", 1)
        v_hi, v_lo = count("v_hi"), count("v_lo", 1)
        kv_mm = count("kv_mm", 2)
        SUMS = 4
        sums_done = count("sums_done", SUMS)
        ks_mm, ks_hi_done, ks_lo_done = sem("ks_mm"), sem("ks_hi_done"), sem("ks_lo_done")
        wqh_done, wql_done = count("wqh_done"), count("wql_done", 1)

        block = ctx.block()
        x_blocks = io["x"].rearrange("(g j p) d -> g p j d", j=TB, p=P)

        def slots(eng, slot):
            with eng.Fori(0, B - 1) as i:
                for tt in range(TPB):
                    slot(i, tt, False)
            for tt in range(TPB):
                slot(B - 1, tt, True)


        @block.sync
        def _(sp):
            def load_x(g):
                x_used.wait(sp, g)
                sp.dma_start(xt[:, :, :], x_blocks[g]).then_inc(x_in, 16)

            def store_h(i, q):
                lo_done.wait(sp, KC * (BB * i + q + 1))
                sp.dma_start(io["hTs"][BB * i + q], hT[q][:, :, :, :].bitcast(F32)).then_inc(hT_out[q], 16)

            for n, name in enumerate(("bk", "bv")):
                sp.dma_start(bkv[:, n], io[name].partition_broadcast(P)).then_inc(bkv_in, 16)
            for q in range(BB):
                sp.sem_inc(hT_out[q], 16)
            load_x(1)
            with sp.Fori(0, B - 1) as i:
                store_h(i, 0)
                load_x(BB * i + 2)
                store_h(i, 1)
                load_x(BB * i + 3)
            store_h(B - 1, 0)
            store_h(B - 1, 1)
            for q in range(BB):
                sp.wait_ge(hT_out[q], 16 * (B + 1))

        @block.gpsimd
        def _(pool):
            ctx.clear_previous(pool)
            wql_done.start(pool)
            for n in range(HEADS // QW):
                part = slice(QW * n, QW * (n + 1))
                wql_done.wait(pool, n)
                pool.dma_start(wq_raw[:, :, :, :], io["wqT"][:, part]).then_inc(wq_in, 16)
                pool.wait_ge(wq_in, 16 * (n + 1))
                pool.tensor_copy(keep["wq_hi"][:, part], wq_raw[:, :, :, :]).then_inc(wqh_done.sem, 1)
                wqh_done.wait(pool, n + 1)
                pool.tensor_tensor(keep["wq_lo"][:, part], wq_raw[:, :, :, :], keep["wq_hi"][:, part].bitcast(F32),
                                   ALU.subtract).then_inc(wql_done.sem, 1)

        @block.scalar
        def _(act):
            def front_deviation(g):
                var_done.wait(act, g + 1)
                act.activation(sd[:, :], var[:, :], ACT.Sqrt).then_inc(sd_done.sem, 1)

            def front_norm(g):
                nmr_done.wait(act, g + 1)
                tr_done.wait(act, KC * g)
                for j in range(TB):
                    done = act.activation(zt[:, j], xt[:, j], ACT.Identity, bias=nmr[:, j:j + 1],
                                          scale=rstd[:, j:j + 1]).then_inc(z_done.sem, 1)

            def front_free(g):
                z_done.wait(act, TB * (g + 1))
                act.sem_inc(x_used.sem, 1)

            def front_hi(g, q, chunks, out_wait):
                for c in chunks:
                    if c == 0:
                        act.wait_ge(hT_out[q], out_wait)
                        v_mm.wait(act, TB * g - TB)
                    hf_done.wait(act, KC * g + c + 1)
                    act.activation(hT[q][:, 0, c], hf[:, c % 2], ACT.Copy).then_inc(hi_done.sem, 1)

            def tile(i, tt, last):
                t = TPB * i + tt
                kb_done.wait(act, t + 1)
                k_done.wait(act, t)
                er_done.wait(act, t)
                act.activation(uk[:, :], kb[:, :], ACT.Relu, scale=-1.0).then_inc(u_done.sem, 1)
                act.activation(rk[:, :], kb[:, :], ACT.Relu)
                u_done.wait(act, t + 1)
                act.activation(ek[:, :], uk[:, :], ACT.Exp, scale=-1.0).then_inc(er_done.sem, 1)
                vb_done.wait(act, t + 1)
                kv_mm.wait(act, t - 1)
                act.activation(vr[:, tt % 2, 0], vf[:, :], ACT.Copy).then_inc(v_hi.sem, 1)
                k_done.wait(act, t + 1)
                act.activation(kr[:, tt % 2, 0], kf[:, :], ACT.Copy).then_inc(k_hi.sem, 1)

                q, j = tt // TB, tt % TB
                nq, ng = (q + 1) % BB, BB * i + q + 1
                if not last or q < BB - 1:
                    if j == 0:
                        front_norm(ng)
                        front_free(ng)
                    if j in (1, 2):
                        front_hi(ng, nq, range(2 * (j - 1), 2 * j), 16 * (i + 1 + (q + 1) // BB))
                if not last and j == TB - 1:
                    front_deviation(ng + 1)

            def slot(i, tt, last):
                if not last or tt + 1 < TPB:
                    tile(*ahead(i, tt, 1), last)

            for x in (x_used, sd_done, z_done, er_done):
                x.start(act)
            front_hi(0, 0, range(KC), 16)
            front_deviation(1)
            tile(0, 0, False)
            slots(act, slot)

        @block.vector
        def _(dve):
            def front_stats(g):
                dve.wait_ge(x_in, 16 * g)
                ag_done.wait(dve, TB * g)
                for j in range(TB):
                    dve.bn_stats(st[:, j], xt[:, j]).then_inc(bn_done.sem, 1)
                bn_done.wait(dve, TB * (g + 1))
                nmr_done.wait(dve, g)
                dve.memset(spare[:, :], 0.0)
                for j in range(TB):
                    dve.bn_aggr(mv[:, j], st[:, j]).then_inc(ag_done.sem, 1)
                ag_done.wait(dve, TB * (g + 1))
                dve.tensor_scalar_add(var[:, :], mv[:, :, 1], LN_EPS).then_inc(var_done.sem, 1)
                sd_done.wait(dve, g + 1)
                dve.reciprocal(rstd[:, :], sd[:, :]).then_inc(rstd_done.sem, 1)
                rstd_done.wait(dve, g + 1)
                dve.scalar_tensor_tensor(nmr[:, :], mv[:, :, 0], -1.0, rstd[:, :], ALU.mult, ALU.mult)\
                   .then_inc(nmr_done.sem, 1)

            def front_split(g, b, q, chunks):
                for c in chunks:
                    tr_done.wait(dve, KC * g + c + 1)
                    lo_done.wait(dve, KC * g + c - 1)
                    dve.tensor_scalar(hf[:, c % 2], psT[c % 2][:, :], keep["modc"][:, b, CA, c:c + 1],
                                      keep["modc"][:, b, SA, c:c + 1], ALU.mult, ALU.add).then_inc(hf_done.sem, 1)
                for c in chunks:
                    hi_done.wait(dve, KC * g + c + 1)
                    dve.tensor_tensor(hT[q][:, 1, c], hf[:, c % 2], hT[q][:, 0, c].bitcast(F32),
                                      ALU.subtract).then_inc(lo_done.sem, 1)

            def sums(i):
                kv_mm.wait(dve, TPB * (i + 1))
                for n in range(2):
                    pair = psKV[n][:, :].rearrange("p (h w d) -> p h w d", h=2, w=2)
                    dve.tensor_copy(kvs[:, n], pair[:, :, 0]).then_inc(sums_done.sem, 1)
                dve.tensor_copy(ksb[:, bass.ds(i, 1)], psS[:, :].unsqueeze(1)).then_inc(sums_done.sem, 1)
                sums_done.wait(dve, SUMS * i + SUMS - 1)
                for n in range(2):
                    pair = psKV[n][:, :].rearrange("p (h w d) -> p h w d", h=2, w=2)
                    last = dve.tensor_tensor(keep["kvT"][:, i, 2 * n * P:2 * (n + 1) * P].rearrange("p (h d) -> p h d", h=2),
                                             kvs[:, n], pair[:, :, 1], ALU.add)
                last.then_inc(sums_done.sem, 1)

            def tile(i, tt, last, end_of=None):
                t = TPB * i + tt
                k_mm.wait(dve, t + 1)
                er_done.wait(dve, t)
                dve.tensor_tensor(kb[:, :], psK[tt % 2][:, :], bkv[:, 0], ALU.add).then_inc(kb_done.sem, 1)
                v_mm.wait(dve, t + 1)
                v_lo.wait(dve, t)
                dve.tensor_tensor(vf[:, :], psV[:, :], bkv[:, 1], ALU.add).then_inc(vb_done.sem, 1)
                if end_of is not None:
                    sums(end_of)
                er_done.wait(dve, t + 1)
                k_lo.wait(dve, t)
                dve.tensor_tensor(kf[:, :], ek[:, :], rk[:, :], ALU.add).then_inc(k_done.sem, 1)
                v_hi.wait(dve, t + 1)
                kv_mm.wait(dve, t - 1)
                dve.tensor_tensor(vr[:, tt % 2, 1], vf[:, :], vr[:, tt % 2, 0].bitcast(F32),
                                  ALU.subtract).then_inc(v_lo.sem, 1)
                k_hi.wait(dve, t + 1)
                dve.tensor_tensor(kr[:, tt % 2, 1], kf[:, :], kr[:, tt % 2, 0].bitcast(F32),
                                  ALU.subtract).then_inc(k_lo.sem, 1)

                q, j = tt // TB, tt % TB
                if (not last or q < BB - 1) and j in (1, 2):
                    front_split(BB * i + q + 1, i + (q + 1) // BB, (q + 1) % BB, range(2 * (j - 1), 2 * j))
                if not last and j == TB - 1:
                    front_stats(BB * i + q + 2)

            for x in (hf_done, lo_done, kb_done, vb_done, k_done, k_lo, v_lo, sums_done, bn_done, ag_done, var_done,
                      rstd_done, nmr_done):
                x.start(dve)
            dve.wait_ge(bkv_in, 32)
            front_split(0, 0, 0, (0, 1))
            front_split(0, 0, 0, (2, 3))
            front_stats(1)

            def slot(i, tt, last):
                if not last or tt + 1 < TPB:
                    tile(*ahead(i, tt, 1), last, i if tt == TPB - 1 else None)

            tile(0, 0, False)
            slots(dve, slot)
            sums(B - 1)
            dve.wait_ge(ks_mm, 1)
            hi, lo = (keep[name][:, :, :].rearrange("p b k -> p (b k)") for name in ("ks_hi", "ks_lo"))
            dve.tensor_copy(hi, psS[:, 0:2 * B * KVH]).then_inc(ks_hi_done, 1)
            dve.wait_ge(ks_hi_done, 1)
            dve.tensor_tensor(lo, psS[:, 0:2 * B * KVH], hi.bitcast(F32), ALU.subtract).then_inc(ks_lo_done, 1)

        @block.tensor
        def _(pe):
            def front_transpose(g, chunks):
                for c in chunks:
                    if c == 0:
                        z_done.wait(pe, TB * (g + 1))
                    hf_done.wait(pe, KC * g + c - 1)
                    for j in range(TB):
                        last = pe.transpose(psT[c % 2][:, j * P:(j + 1) * P], zt[:, j, c * P:(c + 1) * P],
                                            keep["ident"][:, :])
                    last.then_inc(tr_done.sem, 1)

            def tile(i, tt, last):
                t = TPB * i + tt
                q, j = tt // TB, tt % TB
                if j == 0:
                    lo_done.wait(pe, KC * (BB * i + q + 1))
                tok = slice(j * P, (j + 1) * P)
                for n, (ps, free, done) in enumerate(((psK[tt % 2], kb_done, k_mm), (psV, vb_done, v_mm))):
                    free.wait(pe, t - 1 if n == 0 else t)
                    todo = [(a, w, c) for c in range(KC) for a, w in ((0, 0), (0, 1), (1, 0))]
                    for m, (a, w, c) in enumerate(todo):
                        wt = keep["wkv_lo" if w else "wkv_hi"]
                        last = pe.matmul(ps[:, :], hT[q][:, a, c, tok], wt[:, n, c],
                                         start=(m == 0), stop=(m == len(todo) - 1))
                    last.then_inc(done.sem, 1)

            def front(i, tt, last):
                q, j = tt // TB, tt % TB
                if (not last or q < BB - 1) and j in (1, 2):
                    front_transpose(BB * i + q + 1, range(2 * (j - 1), 2 * j))

            def sums(i, tt):
                t = TPB * i + tt
                if tt == 0:
                    sums_done.wait(pe, SUMS * i)
                k_lo.wait(pe, t + 1)
                v_lo.wait(pe, t + 1)
                first, end = tt == 0, tt == TPB - 1
                k, v = kr[:, tt % 2], vr[:, tt % 2]
                for h in range(KVH):
                    at = slice(h * P, (h + 1) * P)
                    ps = psKV[h // 2][:, 2 * P * (h % 2):2 * P * (h % 2 + 1)]
                    pe.matmul(ps, v[:, 0, at], k[:, :, at], start=(first and h % 2 == 0), stop=False,
                              skip_group_check=True)
                    pe.matmul(ps[:, P:2 * P], v[:, 1, at], k[:, 0, at], start=False, stop=end,
                              skip_group_check=True)
                for a in range(2):
                    last = pe.matmul(psS[:, :], keep["ones"][:, :], k[:, a], start=(first and a == 0),
                                     stop=(end and a == 1), skip_group_check=True)
                last.then_inc(kv_mm.sem, 1)

            def slot(i, tt, last):
                ahead_too = not last or tt + 1 < TPB
                if ahead_too:
                    tile(*ahead(i, tt, 1), last)
                sums(i, tt)
                if ahead_too:
                    front(*ahead(i, tt, 1), last)

            for x in (tr_done, kv_mm, v_mm):
                x.start(pe)
            front_transpose(0, range(KC))
            tile(0, 0, False)
            slots(pe, slot)
            sums_done.wait(pe, SUMS * B)
            for b in range(B):
                for h in range(KVH):
                    at = 2 * (KVH * b + h)
                    last = pe.transpose(psS[:, at:at + 2], ksb[0:2, b, h * P:(h + 1) * P], keep["ident"][0:2, 0:2])
            last.then_inc(ks_mm, 1)




def queries(nc, io, keep):
    with Stage(nc, keep, "q") as ctx:
        sem, count = ctx.sem, ctx.count

        def sb(name, shape, dt=F32):
            return ctx.enter_context(nc.sbuf_tensor(name, shape, dt))

        def psum(name, shape):
            return ctx.enter_context(nc.psum_tensor(name, shape, F32))

        STEPS = HEADS * BB
        WR = 2
        hT = [sb(f"qhT{q}", [P, 2, KC, BLK], F32R) for q in range(BB)]
        bq = sb("bq", [P, HEADS])
        gate = sb("gate", [P, D])
        kvb = sb("kvb", [P, 2, D], F32R)
        wo = [sb(f"wo{n}", [P, D]) for n in range(WR)]
        wor = [sb(f"wor{n}", [P, 2, D], F32R) for n in range(2)]
        w2f = sb("w2f", [P, D])
        w2 = [sb(f"w2_{n}", [P, 2, D + 2], F32R) for n in range(2)]
        bqn = sb("bqn", [P, HEADS])
        uq = sb("uq", [P, BLK])
        eq = sb("eq", [P, 2, BLK])
        rq = sb("rq", [P, 2, BLK])
        qf = sb("qf", [P, 2, BLK])
        qr = sb("qr", [P, 2, 2, BLK], F32R)
        nrm = sb("nrm", [P, 2, TB])
        rn = sb("rn", [P, 2, TB])
        xin = sb("xin", [P, BB, TB, D])
        acc = sb("acc", [P, BB, TB, D])
        st = sb("st2", [P, TPB, 6])
        spare = sb("spare2", [P, 1])
        mvb = sb("mvb", [P, TPB, 2])
        mv = sb("mv2", [P, B, TPB, 2])
        sd = sb("sd2", [P, B, TPB])
        HD = D // 2
        psQ = psum("psQ", [P, BLK])
        psO1 = psum("psO1", [P, TB, HD])
        psO2 = psum("psO2", [P, TB, D])
        psW = psum("psW", [P, D])

        bq_in, gate_in = sem("bq_in"), sem("gate_in")
        wo_in = [sem(f"wo_in{n}") for n in range(WR)]
        hT_in = [[sem(f"hT_in{q}_{n}") for n in range(2)] for q in range(BB)]
        xin_in = sem("xin_in")
        acc_out = [sem(f"acc_out{q}") for q in range(BB)]
        bn_done, ag_done, mv_done = count("bn_done2", TPB), count("ag_done2", 1), count("mv_done2", 1)
        var_done, sd_done, rstd_done, nmr_done = sem("var2_done"), sem("sd2_done"), sem("rstd2_done"), sem("nmr2_done")
        kvb_done = count("kvb_done")
        w2_mm = count("w2_mm", 2)
        wo_hi, wo_lo = count("wo_hi"), count("wo_lo", WR)
        w2f_done, w2_hi, w2_lo = count("w2f_done", 1), count("w2_hi"), count("w2_lo", 1)
        q_mm = count("q_mm", BB)
        bqn_done = sem("bqn_done")
        u_done, r_done = count("u_done"), count("r_done", 1)
        er_done, qf_done = count("eqrq_done", 3), count("qf_done", 3)
        q_hi, q_lo = count("q_hi"), count("q_lo", 2)
        nrm_done, rn_done = count("nrm_done"), count("rn_done", 2)
        o_mm = count("o_mm", 2 * TB + 1)
        acc_done = count("acc_done", TB * STEPS)

        block = ctx.block()
        x_blocks = io["x"].rearrange("(g j p) d -> g p j d", j=TB, p=P)
        x1_blocks = io["x1"].rearrange("(g j p) d -> g p j d", j=TB, p=P)

        def batches(eng, slot):
            with eng.Fori(0, B - 1) as i:
                for s in range(STEPS):
                    slot(i, s, False)
            for s in range(STEPS):
                slot(B - 1, s, True)

        def later(i, s, n, last):
            if last and s + n >= STEPS:
                return []
            return [(i + (s + n) // STEPS, (s + n) % STEPS)]

        def next_head(i, s, last, n=1):
            return [(j, t // BB) for j, t in later(i, s, n * BB, last) if t % BB == 0]


        @block.sync
        def _(sp):
            def load_wo(i, h):
                wo_lo.wait(sp, HEADS * i + h - WR + 1)
                sp.dma_start(wo[h % WR][:, :], io["woT"][:, h]).then_inc(wo_in[h % WR], 16)

            def load_h(i, q):
                q_mm.wait(sp, STEPS * i - (BB - 1) + q)
                for n in range(2):
                    part = slice(n * KC // 2, (n + 1) * KC // 2)
                    sp.dma_start(hT[q][:, :, part].bitcast(F32), io["hTs"][BB * i + q, :, :, part])\
                      .then_inc(hT_in[q][n], 16)

            sp.dma_start(bq[:, :], io["bq"]).then_inc(bq_in, 16)

            def begin(i):
                for h in range(WR):
                    load_wo(i, h)
                w2f_done.wait(sp, HEADS * i)
                sp.dma_start(gate[:, :], io["modrows"][R_GA, i].partition_broadcast(P)).then_inc(gate_in, 16)
                for q in range(BB):
                    load_h(i, q)
                acc_done.wait(sp, TB * STEPS * i - TB * (STEPS - BB))
                for q in range(BB):
                    sp.dma_start(xin[:, q], x_blocks[BB * i + q]).then_inc(xin_in, 16)

            def store(i):
                for q in range(BB):
                    acc_done.wait(sp, TB * (STEPS * i + STEPS - BB + q + 1))
                    sp.dma_start(x1_blocks[BB * i + q], acc[:, q]).then_inc(acc_out[q], 16)

            for q in range(BB):
                sp.sem_inc(acc_out[q], 16)
            begin(0)
            for h in range(WR, HEADS):
                load_wo(0, h)
            with sp.Fori(1, B) as i:
                begin(i)
                store(i - 1)
                for h in range(WR, HEADS):
                    load_wo(i, h)
            store(B - 1)
            for q in range(BB):
                sp.wait_ge(acc_out[q], 16 * (B + 1))

        @block.scalar
        def _(act):
            def w2_split(i, h):
                w2f_done.wait(act, HEADS * i + h + 1)
                o_mm.wait(act, TB * (STEPS * i + BB * (h - 1)))
                act.activation(w2[h % 2][:, 0, 0:D], w2f[:, :], ACT.Copy).then_inc(w2_hi.sem, 1)

            def wo_upper(i, h):
                act.wait_ge(wo_in[h % WR], 16 * (HEADS // WR * i + h // WR + 1))
                w2_mm.wait(act, HEADS * i + h - 1)
                act.activation(wor[h % 2][:, 0], wo[h % WR][:, :], ACT.Copy).then_inc(wo_hi.sem, 1)

            def exps(i, s):
                n, h = STEPS * i + s, s // BB
                q_mm.wait(act, n + 1)
                er_done.wait(act, n)
                qf_done.wait(act, n - 1)
                act.activation(uq[:, :], psQ[:, :], ACT.Relu, bias=bqn[:, h:h + 1], scale=-1.0)\
                   .then_inc(u_done.sem, 1)
                act.activation(rq[:, s % 2], psQ[:, :], ACT.Relu, bias=bq[:, h:h + 1]).then_inc(r_done.sem, 1)
                u_done.wait(act, n + 1)
                act.activation(eq[:, s % 2], uq[:, :], ACT.Exp, scale=-1.0).then_inc(er_done.sem, 1)

            def upper(i, s):
                n = STEPS * i + s
                qf_done.wait(act, n + 1)
                o_mm.wait(act, TB * (n - 1))
                act.activation(qr[:, s % 2, 0], qf[:, s % 2], ACT.Copy).then_inc(q_hi.sem, 1)

            for x in (r_done, er_done):
                x.start(act)
            act.wait_ge(bq_in, 16)
            act.mul(bqn[:, :], bq[:, :], -1.0).then_inc(bqn_done, 1)
            act.wait_ge(bqn_done, 1)
            def slot(i, s, last):
                for at in later(i, s, 1, last):
                    upper(*at)
                for at in later(i, s, 2, last):
                    exps(*at)
                for at in next_head(i, s, last):
                    w2_split(*at)
                for at in next_head(i, s, last, 2):
                    wo_upper(*at)

            wo_upper(0, 0)
            exps(0, 0)
            w2_split(0, 0)
            wo_upper(0, 1)
            upper(0, 0)
            exps(0, 1)
            batches(act, slot)
            act.wait_ge(var_done, 1)
            act.activation(sd[:, :, :], sd[:, :, :], ACT.Sqrt).then_inc(sd_done, 1)

        @block.vector
        def _(dve):
            def w2_gate(i, h):
                w2_mm.wait(dve, HEADS * i + h + 1)
                w2_lo.wait(dve, HEADS * i + h)
                if h % GROUP < 2:
                    cols = slice(2 * (h // GROUP), 2 * (h // GROUP) + 2)
                    for part, name in enumerate(("ks_hi", "ks_lo")):
                        dve.tensor_scalar_mul(w2[h % 2][:, part, D:D + 2], keep[name][:, i, cols].bitcast(F32), 1.0)
                dve.tensor_tensor(w2f[:, :], psW[:, :], gate[:, :], ALU.mult).then_inc(w2f_done.sem, 1)

            def square(i, s):
                n = STEPS * i + s
                er_done.wait(dve, n + 1)
                q_lo.wait(dve, n - 1)
                dve.tensor_tensor(qf[:, s % 2], eq[:, s % 2], rq[:, s % 2], ALU.add)\
                   .then_inc(qf_done.sem, 1)

            def norms(i, s):
                n = STEPS * i + s
                o_mm.wait(dve, TB * (n + 1))
                rn_done.wait(dve, n - 1)
                dve.tensor_scalar_add(nrm[:, s % 2], psO2[:, :, HD], NORM_EPS).then_inc(nrm_done.sem, 1)
                nrm_done.wait(dve, n + 1)
                acc_done.wait(dve, TB * (n - 1))
                dve.reciprocal(rn[:, s % 2], nrm[:, s % 2]).then_inc(rn_done.sem, 1)

            def add(i, s):
                n, q = STEPS * i + s, s % BB
                rn_done.wait(dve, n + 1)
                if s < BB:
                    dve.wait_ge(acc_out[q], 16 * (i + 1))
                    bn_done.wait(dve, TPB * (i - 1) + TB * (q + 1))
                    dve.wait_ge(xin_in, 16 * BB * (i + 1))
                else:
                    acc_done.wait(dve, TB * (n - 1))
                base = xin if s < BB else acc
                for j in range(TB):
                    for half, ps in ((slice(0, HD), psO1[:, j]), (slice(HD, D), psO2[:, j, 0:HD])):
                        last = dve.scalar_tensor_tensor(acc[:, q, j, half], ps, rn[:, s % 2, j:j + 1],
                                                        base[:, q, j, half], ALU.mult, ALU.add)
                    last.then_inc(acc_done.sem, 1)

            def next_sums(i):
                w2_mm.wait(dve, HEADS * i)
                dve.tensor_scalar_mul(kvb[:, 0], keep["kvT"][:, i], 1.0).then_inc(kvb_done.sem, 1)
                kvb_done.wait(dve, 2 * i + 1)
                dve.tensor_tensor(kvb[:, 1], keep["kvT"][:, i], kvb[:, 0].bitcast(F32), ALU.subtract)\
                   .then_inc(kvb_done.sem, 1)
                dve.wait_ge(gate_in, 16 * (i + 1))

            def stats(i, part):
                q = part // 2
                acc_done.wait(dve, TB * (STEPS * i + STEPS - BB + q + 1))
                ag_done.wait(dve, TPB * i)
                for j in range(part % 2 * TB // 2, (part % 2 + 1) * TB // 2):
                    dve.bn_stats(st[:, q * TB + j], acc[:, q, j]).then_inc(bn_done.sem, 1)

            def aggregate(i):
                mv_done.wait(dve, i)
                bn_done.wait(dve, TPB * (i + 1))
                dve.memset(spare[:, :], 0.0)
                for t in range(TPB):
                    dve.bn_aggr(mvb[:, t], st[:, t]).then_inc(ag_done.sem, 1)
                ag_done.wait(dve, TPB * (i + 1))
                dve.tensor_copy(mv[:, i], mvb[:, :, :]).then_inc(mv_done.sem, 1)

            for x in (bn_done, ag_done, mv_done, w2f_done, qf_done, rn_done, acc_done):
                x.start(dve)

            def slot(i, s, last, stats_of=None):
                if s == STEPS - BB - 1 and not last:
                    next_sums(i + 1)
                for at in next_head(i, s, last):
                    w2_gate(*at)
                for at in later(i, s, 2, last):
                    square(*at)
                if stats_of is not None:
                    stats(stats_of, BB + s)
                norms(i, s)
                add(i, s)
                if s >= STEPS - BB:
                    stats(i, s - (STEPS - BB))
                if stats_of is not None and s == BB - 1:
                    aggregate(stats_of)

            next_sums(0)
            w2_gate(0, 0)
            square(0, 0)
            square(0, 1)
            for s in range(BB):
                slot(0, s, False)
            with dve.Fori(0, B - 1) as i:
                for s in range(BB, STEPS):
                    slot(i, s, False)
                for s in range(BB):
                    slot(i + 1, s, False, i)
            for s in range(BB, STEPS):
                slot(B - 1, s, True)
            for part in range(BB, 2 * BB):
                stats(B - 1, part)
            aggregate(B - 1)
            mv_done.wait(dve, B)
            mean, var = mv[:, :, :, 0], mv[:, :, :, 1]
            dve.tensor_scalar_add(sd[:, :, :], var, LN_EPS).then_inc(var_done, 1)
            dve.wait_ge(sd_done, 1)
            dve.reciprocal(keep["rstd2"][:, :, :], sd[:, :, :]).then_inc(rstd_done, 1)
            dve.wait_ge(rstd_done, 1)
            dve.scalar_tensor_tensor(keep["nmr2"][:, :, :], mean, -1.0, keep["rstd2"][:, :, :], ALU.mult, ALU.mult)\
               .then_inc(nmr_done, 1)

        @block.tensor
        def _(pe):
            def query(i, s):
                n, h, q = STEPS * i + s, s // BB, s % BB
                r_done.wait(pe, n)
                todo = [(w, a, c) for c in range(KC) for w, a in ((0, 0), (0, 1), (1, 0))]
                for m, (w, a, c) in enumerate(todo):
                    if s < BB and m % (len(todo) // 2) == 0:
                        pe.wait_ge(hT_in[q][2 * m // len(todo)], 16 * (i + 1))
                    wt = keep["wq_lo" if w else "wq_hi"]
                    last = pe.matmul(psQ[:, :], wt[:, h, c], hT[q][:, a, c],
                                     start=(m == 0), stop=(m == len(todo) - 1))
                last.then_inc(q_mm.sem, 1)

            def weight(i, h):
                wo_lo.wait(pe, HEADS * i + h + 1)
                w2f_done.wait(pe, HEADS * i + h)
                g = h // GROUP
                for m, (a, w) in enumerate(((0, 0), (0, 1), (1, 0))):
                    last = pe.matmul(psW[:, :], kvb[:, a, g * P:(g + 1) * P], wor[h % 2][:, w],
                                     start=(m == 0), stop=(m == 2))
                last.then_inc(w2_mm.sem, 1)

            def output(i, s):
                n, h = STEPS * i + s, s // BB
                q_lo.wait(pe, n + 1)
                w2_lo.wait(pe, HEADS * i + h + 1)
                for j in range(TB):
                    tok = slice(j * P, (j + 1) * P)
                    if j == 0:
                        acc_done.wait(pe, TB * (n - 1) + 2)
                    elif j == 1 or j == 3:
                        acc_done.wait(pe, TB * (n - 1) + j + 1)
                    elif j == 2:
                        acc_done.wait(pe, TB * n)
                    for half, ps in ((slice(0, HD), psO1[:, j]), (slice(HD, D + 2), psO2[:, j, 0:HD + 2])):
                        for m, (a, w) in enumerate(((0, 0), (0, 1), (1, 0))):
                            last = pe.matmul(ps, qr[:, s % 2, a, tok], w2[h % 2][:, w, half],
                                             start=(m == 0), stop=(m == 2))
                    last.then_inc(o_mm.sem, 1)

            for x in (w2_mm, q_mm, o_mm):
                x.start(pe)

            def slot(i, s, last):
                for j, h in next_head(i, s, last):
                    if h == 0:
                        kvb_done.wait(pe, 2 * (j + 1))
                    weight(j, h)
                for at in later(i, s, 2, last):
                    query(*at)
                output(i, s)

            query(0, 0)
            kvb_done.wait(pe, 2)
            weight(0, 0)
            query(0, 1)
            batches(pe, slot)

        @block.gpsimd
        def _(pool):
            def w2_split(i, h):
                w2_hi.wait(pool, HEADS * i + h + 1)
                pool.tensor_tensor(w2[h % 2][:, 1, 0:D], w2f[:, :], w2[h % 2][:, 0, 0:D].bitcast(F32),
                                   ALU.subtract).then_inc(w2_lo.sem, 1)

            def wo_lower(i, h):
                wo_hi.wait(pool, HEADS * i + h + 1)
                pool.tensor_tensor(wor[h % 2][:, 1], wo[h % WR][:, :], wor[h % 2][:, 0].bitcast(F32),
                                   ALU.subtract).then_inc(wo_lo.sem, 1)

            def lower(i, s):
                n = STEPS * i + s
                q_hi.wait(pool, n + 1)
                pool.tensor_tensor(qr[:, s % 2, 1], qf[:, s % 2], qr[:, s % 2, 0].bitcast(F32),
                                   ALU.subtract).then_inc(q_lo.sem, 1)

            def slot(i, s, last):
                for at in later(i, s, 1, last):
                    lower(*at)
                for at in next_head(i, s, last):
                    w2_split(*at)
                for at in next_head(i, s, last, 2):
                    wo_lower(*at)

            for x in (wo_lo, w2_lo, q_lo):
                x.start(pool)
            wo_lower(0, 0)
            ctx.clear_previous(pool)
            w2_split(0, 0)
            wo_lower(0, 1)
            lower(0, 0)
            batches(pool, slot)


GU = 2 * FF
GR = FF + EXPERTS
NF = len(FCH)
FPAD = NF * P
SLOTS = TOPK * TILES + EXPERTS
RAW_DMAS = 3


def split_products(chunks):
    return [(a, w, c) for c in range(chunks) for a, w in ((0, 0), (0, 1), (1, 0))]


def load_expert(pool, io, keep, e):
    pool.dma_start(keep["gu_raw"][:, :, :], io["gu_e"][e]).then_inc(keep["raw_in"], 16)
    pool.dma_start(keep["dn_raw"][:, 0:NF - 1], io["dn_e"][e, 0:(NF - 1) * P].rearrange("(c p) d -> p c d", p=P))\
        .then_inc(keep["raw_in"], 16)
    pool.dma_start(keep["dn_raw"][0:FCH[-1], NF - 1], io["dn_e"][e, (NF - 1) * P:FF]).then_inc(keep["raw_in"], 16)


def split_expert(pool, keep, buf, e):
    f = FCH[-1]
    pairs = [(keep["gu_raw"][:, :, :], keep["gu_x"][:, buf]),
             (keep["dn_raw"][:, 0:NF - 1], keep["dn_x"][:, buf, :, 0:NF - 1]),
             (keep["dn_raw"][0:f, NF - 1], keep["dn_x"][0:f, buf, :, NF - 1])]
    for raw, halves in pairs:
        pool.tensor_copy(halves[:, 0], raw).then_inc(keep["upper_done"], 1)
    pool.wait_ge(keep["upper_done"], len(pairs) * (e + 1))
    for raw, halves in pairs:
        pool.tensor_tensor(halves[:, 1], raw, halves[:, 0].bitcast(F32), ALU.subtract).then_inc(keep["split_done"], 1)


SPLIT_STEPS = 3


def shared_expert(nc, io, keep):
    with Stage(nc, keep, "sh") as ctx:
        sem, count = ctx.sem, ctx.count

        def sb(name, shape, dt=F32):
            return ctx.enter_context(nc.sbuf_tensor(name, shape, dt))

        def psum(name, shape):
            return ctx.enter_context(nc.psum_tensor(name, shape, F32))

        AHEAD = 3
        XB = 4
        place = keep["act"][:, TILES // 2:].rearrange("p t f -> p (t f)")
        gu_raw = place[:, 0:KC * (GR + FF)].rearrange("p (c f) -> p c f", c=KC)
        dn_raw = place[:, KC * (GR + FF):KC * (GR + FF) + NF * D].rearrange("p (c d) -> p c d", c=NF)
        gu = sb("gu", [P, 2, KC, GR + FF], F32R)
        rowsb = sb("rowsb", [P, 2, D])
        x1t = sb("x1t", [P, XB, D])
        h2t = sb("h2t", [P, XB, D])
        hTr = sb("hTr", [P, 2, 2, D], F32R)
        sil = sb("sil", [P, 2, FF])
        psT = [psum(f"psT_{n}", [P, D]) for n in range(2)]
        psG = [psum(f"psG{n}", [P, D]) for n in range(2)]
        psU = [psum(f"psU{n}", [P, D]) for n in range(2)]

        gu_in = [sem(f"gu_in{c}") for c in range(KC)]
        dn_in = [sem(f"dn_in{c}") for c in range(NF)]
        raw_hi, raw_lo = sem("raw_hi"), sem("raw_lo")
        norm_rows_in = sem("norm_rows_in")
        x_in = [sem(f"x1_in{n}") for n in range(XB)]
        h2_out = [sem(f"h2_out{n}") for n in range(XB)]
        z_done, sc_done, h2_done = count("z2_done", XB), count("sc2_done", 1), count("h2_done", 1)
        t_mm, hi_done, lo_done = count("t_mm", XB), count("hi2_done", 1), count("lo2_done", 2)
        g_mm, u_mm = count("g_mm"), count("u_mm", 2)
        sil_done, a_done, lg_done = count("sil_done", 1), count("a_done", 2), count("lg_done", 2)

        x1_tiles = io["x1"].rearrange("(t p) d -> t p d", p=P)
        h2_tiles = io["h2"].rearrange("(t p) d -> t p d", p=P)
        block = ctx.block()

        def slots(eng, step):
            with eng.Fori(0, B - 1) as i:
                for tt in range(TPB):
                    step(i, tt, False)
            for tt in range(TPB):
                step(B - 1, tt, True)

        def in_range(tt, n, last):
            return not last or tt + n < TPB


        @block.sync
        def _(sp):
            def load_x(i, tt):
                t = TPB * i + tt
                z_done.wait(sp, t - XB + 1)
                sp.dma_start(x1t[:, tt % XB], x1_tiles[t]).then_inc(x_in[tt % XB], 16)

            def store_h2(i, tt):
                t = TPB * i + tt
                h2_done.wait(sp, t + 1)
                sp.dma_start(h2_tiles[t], h2t[:, tt % XB]).then_inc(h2_out[tt % XB], 16)

            def norm_rows(i):
                h2_done.wait(sp, TPB * i)
                for n, r in ((0, R_SB), (1, R_CB)):
                    sp.dma_start(rowsb[:, n], io["modrows"][r, i].partition_broadcast(P)).then_inc(norm_rows_in, 16)

            def step(i, tt, last):
                if in_range(tt, XB, last):
                    load_x(*ahead(i, tt, XB))
                if tt + AHEAD == TPB and not last:
                    norm_rows(i + 1)
                if in_range(tt, AHEAD, last):
                    store_h2(*ahead(i, tt, AHEAD))

            for n in range(XB):
                sp.sem_inc(h2_out[n], 16)
            norm_rows(0)
            load_x(0, 0)
            for c in range(KC):
                sp.dma_start(gu_raw[:, c], io["gu_s"][:, c]).then_inc(gu_in[c], 16)
            for n in range(1, XB):
                load_x(0, n)
            for c in range(NF):
                sp.dma_start(dn_raw[0:FCH[c], c], io["dn_s"][c * P:c * P + FCH[c]]).then_inc(dn_in[c], 16)
            for t in range(AHEAD):
                store_h2(0, t)
            slots(sp, step)
            for n in range(XB):
                sp.wait_ge(h2_out[n], 16 * (TILES // XB + 1))

        @block.gpsimd
        def _(pool):
            ctx.clear_previous(pool)
            for n in dn_in:
                pool.wait_ge(n, 16)
            for e in range(2):
                load_expert(pool, io, keep, e)
                pool.wait_ge(keep["raw_in"], 16 * RAW_DMAS * (e + 1))
                split_expert(pool, keep, e, e)
                pool.wait_ge(keep["split_done"], SPLIT_STEPS * (e + 1))
            load_expert(pool, io, keep, 2)

        @block.scalar
        def _(act):
            def norm(i, tt):
                t = TPB * i + tt
                act.wait_ge(x_in[tt % XB], 16 * ((TPB // XB) * i + tt // XB + 1))
                t_mm.wait(act, t - XB + 1)
                act.wait_ge(h2_out[tt % XB], 16 * ((TPB // XB) * i + tt // XB + 1))
                act.activation(h2t[:, tt % XB], x1t[:, tt % XB], ACT.Identity, bias=keep["nmr2"][:, i, tt:tt + 1],
                               scale=keep["rstd2"][:, i, tt:tt + 1]).then_inc(z_done.sem, 1)

            def upper(i, tt):
                t = TPB * i + tt
                t_mm.wait(act, t + 1)
                u_mm.wait(act, t - 1)
                act.activation(hTr[:, tt % 2, 0], psT[tt % 2][:, :], ACT.Copy).then_inc(hi_done.sem, 1)

            def silu(i, tt):
                t = TPB * i + tt
                g_mm.wait(act, t + 1)
                a_done.wait(act, t - 1)
                act.activation(sil[:, tt % 2], psG[tt % 2][:, 0:FF], ACT.Silu).then_inc(sil_done.sem, 1)

            def step(i, tt, last):
                if in_range(tt, 1, last):
                    upper(*ahead(i, tt, 1))
                if in_range(tt, AHEAD, last):
                    norm(*ahead(i, tt, AHEAD))
                silu(i, tt)

            for x in (z_done, hi_done, sil_done):
                x.start(act)
            norm(0, 0)
            for c in range(KC):
                act.wait_ge(gu_in[c], 16)
                act.activation(gu[:, 0, c], gu_raw[:, c], ACT.Copy).then_inc(raw_hi, 1)
            upper(0, 0)
            norm(0, 1)
            norm(0, 2)
            for c in range(NF):
                act.wait_ge(dn_in[c], 16)
                act.activation(keep["dn"][0:FCH[c], 0, c], dn_raw[0:FCH[c], c], ACT.Copy).then_inc(raw_hi, 1)
            slots(act, step)

        @block.vector
        def _(dve):
            def modulate(i, tt):
                t = TPB * i + tt
                z_done.wait(dve, t + 1)
                if tt == 0:
                    dve.wait_ge(norm_rows_in, 32 * (i + 1))
                dve.tensor_tensor(h2t[:, tt % XB], h2t[:, tt % XB], rowsb[:, 1], ALU.mult).then_inc(sc_done.sem, 1)
                sc_done.wait(dve, t + 1)
                dve.tensor_tensor(h2t[:, tt % XB], h2t[:, tt % XB], rowsb[:, 0], ALU.add).then_inc(h2_done.sem, 1)

            def lower(i, tt):
                hi_done.wait(dve, TPB * i + tt + 1)
                dve.tensor_tensor(hTr[:, tt % 2, 1], psT[tt % 2][:, :], hTr[:, tt % 2, 0].bitcast(F32), ALU.subtract)\
                   .then_inc(lo_done.sem, 1)

            def gated(i, tt):
                t = TPB * i + tt
                sil_done.wait(dve, t + 1)
                dve.tensor_scalar_mul(keep["logits"][:, bass.ds(t, 1)], psG[tt % 2][:, FF:GR].unsqueeze(1), 1.0)\
                   .then_inc(lg_done.sem, 1)
                u_mm.wait(dve, t + 1)
                dve.tensor_tensor(keep["act"][:, bass.ds(t, 1)], sil[:, tt % 2].unsqueeze(1),
                                  psU[tt % 2][:, 0:FF].unsqueeze(1), ALU.mult).then_inc(a_done.sem, 1)

            def step(i, tt, last):
                if in_range(tt, 1, last):
                    lower(*ahead(i, tt, 1))
                if in_range(tt, AHEAD, last):
                    modulate(*ahead(i, tt, AHEAD))
                gated(i, tt)

            for x in (sc_done, h2_done, lo_done, a_done, lg_done):
                x.start(dve)
            modulate(0, 0)
            for c in range(KC):
                dve.wait_ge(raw_hi, c + 1)
                dve.tensor_tensor(gu[:, 1, c], gu_raw[:, c], gu[:, 0, c].bitcast(F32), ALU.subtract).then_inc(raw_lo, 1)
            lower(0, 0)
            modulate(0, 1)
            modulate(0, 2)
            for c in range(NF):
                dve.wait_ge(raw_hi, KC + c + 1)
                f = FCH[c]
                dve.tensor_tensor(keep["dn"][0:f, 1, c], dn_raw[0:f, c], keep["dn"][0:f, 0, c].bitcast(F32),
                                  ALU.subtract).then_inc(raw_lo, 1)
            slots(dve, step)

        @block.tensor
        def _(pe):
            def transpose_h(i, tt):
                t = TPB * i + tt
                h2_done.wait(pe, t + 1)
                lo_done.wait(pe, t - 1)
                for c in range(KC):
                    last = pe.transpose(psT[tt % 2][:, c * P:(c + 1) * P], h2t[:, tt % XB, c * P:(c + 1) * P],
                                        keep["ident"][:, :])
                last.then_inc(t_mm.sem, 1)

            def gate_up(i, tt):
                t = TPB * i + tt
                lo_done.wait(pe, t + 1)
                for ps, cols, free, done in ((psG[tt % 2], slice(0, GR), lg_done, g_mm),
                                             (psU[tt % 2], slice(GR, GR + FF), a_done, u_mm)):
                    free.wait(pe, t - 1)
                    todo = split_products(KC)
                    for m, (a, w, c) in enumerate(todo):
                        last = pe.matmul(ps[:, 0:cols.stop - cols.start], hTr[:, tt % 2, a, c * P:(c + 1) * P],
                                         gu[:, w, c, cols], start=(m == 0), stop=(m == len(todo) - 1))
                    last.then_inc(done.sem, 1)

            def step(i, tt, last):
                if in_range(tt, 1, last):
                    transpose_h(*ahead(i, tt, 1))
                gate_up(i, tt)

            for x in (t_mm, u_mm):
                x.start(pe)
            transpose_h(0, 0)
            pe.wait_ge(raw_lo, KC)
            slots(pe, step)


def ahead(i, tt, n):
    return i + (tt + n) // TPB, (tt + n) % TPB


def route(nc, io, keep):
    with Stage(nc, keep, "rt") as ctx:
        sem = ctx.sem

        def sb(name, shape, dt=F32):
            return ctx.enter_context(nc.sbuf_tensor(name, shape, dt))

        TE = TILES * EXPERTS
        PAIRS = TOPK * TILES
        PART = 16
        big = [P, TILES, EXPERTS]
        bias2 = sb("bias2", [P, 2, EXPERTS])
        bias = sb("bias", [P, EXPERTS])
        lg = sb("lg", big)
        pr = sb("pr", big)
        top = sb("top", [P, TOPK, TILES])
        key = sb("key", big)
        kmax = sb("kmax", [P, TILES])
        oh = [sb(f"oh{k}", big) for k in range(TOPK)]
        rev = sb("rev", [P, EXPERTS])
        den = sb("den_", [P, TILES])
        mask = sb("mask", big, F32R)
        tri_f = sb("tri_f", [P, P])
        tri = sb("tri", [P, P], F32R)
        all_f = sb("all_f", [P, P])
        all_r = sb("all_r", [P, P], F32R)
        scan = [sb(f"scan{n}", big) for n in range(2)]
        before = sb("before", big)
        n_i = sb("n_i", [P, EXPERTS], I32)
        t_i = sb("t_i", [P, EXPERTS], I32)
        tiles = sb("tiles", [P, EXPERTS])
        ends = [sb(f"ends{n}", [P, EXPERTS]) for n in range(2)]
        base = sb("base", [P, EXPERTS])
        place = sb("place", big)
        prod = sb("prod", big)
        slot = sb("slot", [P, TOPK, TILES])
        tile_i = sb("tile_i", [P, PAIRS], I32)
        row_i = sb("row_i", [P, PAIRS], I32)
        tile_f = sb("tile_f", [P, PAIRS])
        row_f = sb("row_f", [P, PAIRS])
        iota_r = sb("iota_r", [P, P])
        iota_s = sb("iota_s", [P, SLOTS])
        tok = sb("tok", [P, TILES])
        ge = sb("ge", [P, SLOTS, EXPERTS])
        emap = sb("emap", [P, SLOTS])
        isnew = sb("isnew", [P, SLOTS])
        oh_row = sb("oh_row", [P, 2, PART, P], F32R)
        oh_tile = sb("oh_tile", [P, PART, SLOTS])
        tok_tile = sb("tok_tile", [P, 2, PART, SLOTS], F32R)
        psB = ctx.enter_context(nc.psum_tensor("psB", [P, D], F32))
        psT = ctx.enter_context(nc.psum_tensor("psTot", [P, D], F32))
        psI = ctx.enter_context(nc.psum_tensor("psI", [P, D], F32))

        bias_in = sem("bias_in")
        iotas, tri_set, tri_done = sem("iotas"), sem("tri_set"), sem("tri_done")
        d = sem("route_steps")
        lg_done, e_done = sem("lg_done"), sem("ex_done")
        mask_done, counts_mm = sem("mask_done"), sem("counts_mm")
        split_done = sem("split_done")
        row_done, tile_done, tok_done = sem("oh_row_done"), sem("oh_tile_done"), sem("tok_tile_done")
        id_mm = sem("id_mm")
        ids_done = sem("ids_done")
        block = ctx.block()

        @block.sync
        def _(sp):
            for n, name in enumerate(("br", "rb")):
                sp.dma_start(bias2[:, n], io[name].partition_broadcast(P)).then_inc(bias_in, 16)

        @block.gpsimd
        def _(pool):
            f = dict(allow_small_or_imprecise_dtypes=True)
            pool.iota(iota_r[:, :], pattern=[[1, P]], base=0, channel_multiplier=0, **f).then_inc(iotas, 1)
            pool.iota(iota_s[:, :], pattern=[[1, SLOTS]], base=0, channel_multiplier=0, **f).then_inc(iotas, 1)
            pool.iota(tok[:, :], pattern=[[P, TILES]], base=0, channel_multiplier=1, **f).then_inc(iotas, 1)
            pool.iota(rev[:, :], pattern=[[-1, EXPERTS]], base=EXPERTS, channel_multiplier=0, **f).then_inc(iotas, 1)
            pool.memset(all_f[:, :], 1.0).then_inc(tri_set, 1)
            pool.wait_ge(tri_set, 1)
            pool.affine_select(out=tri_f[:, :], in_=all_f[:, :], compare_op=ALU.is_gt, fill=0.0, base=0,
                               pattern=[[1, P]], channel_multiplier=-1).then_inc(tri_done, 1)
            ctx.clear_previous(pool)
            for n in range(PAIRS // PART):
                pool.wait_ge(tile_done, n + 1)
                if n >= 2:
                    pool.wait_ge(id_mm, n - 1)
                pool.tensor_tensor(tok_tile[:, n % 2], oh_tile[:, :, :],
                                   keep["tok2"][:, n * PART:(n + 1) * PART].unsqueeze(2)
                                   .broadcast_to((P, PART, SLOTS)), ALU.mult).then_inc(tok_done, 1)

        @block.scalar
        def _(act):
            act.wait_ge(lg_done, 1)
            act.activation(pr[:, :, :], lg[:, :, :], ACT.Exp, scale=-1.0).then_inc(e_done, 1)

        @block.vector
        def _(dve):
            at = [0]

            def then(ins):
                at[0] += 1
                ins.then_inc(d, 1)
                dve.wait_ge(d, at[0])

            def over_tiles(x):
                return x[:, :].unsqueeze(1).broadcast_to(tuple(big))

            def over_experts(x):
                return x.unsqueeze(2).broadcast_to(tuple(big))

            then(dve.memset(isnew[:, :], 0.0))
            dve.wait_ge(bias_in, 32)
            dve.wait_ge(iotas, 4)
            dve.wait_ge(tri_done, 1)
            then(dve.tensor_copy(tri[:, :], tri_f[:, :]))
            then(dve.tensor_copy(all_r[:, :], all_f[:, :]))
            then(dve.tensor_copy(keep["tok2"][:, 0:TILES], tok[:, :]))
            then(dve.tensor_copy(keep["tok2"][:, TILES:PAIRS], tok[:, :]))
            then(dve.tensor_tensor(bias[:, :], bias2[:, 0], bias2[:, 1], ALU.add))
            dve.tensor_tensor(lg[:, :, :], keep["logits"][:, :, :], over_tiles(bias), ALU.add).then_inc(lg_done, 1)
            dve.wait_ge(e_done, 1)
            then(dve.tensor_scalar_add(pr[:, :, :], pr[:, :, :], 1.0))
            then(dve.reciprocal(pr[:, :, :], pr[:, :, :]))
            for k in range(TOPK):
                then(dve.reduce_max(top[:, k], pr[:, :, :], AX_X))
                then(dve.tensor_tensor(key[:, :, :], pr[:, :, :], over_experts(top[:, k]), ALU.is_equal))
                then(dve.tensor_tensor(key[:, :, :], key[:, :, :], over_tiles(rev), ALU.mult))
                then(dve.reduce_max(kmax[:, :], key[:, :, :], AX_X))
                then(dve.tensor_tensor(oh[k][:, :, :], key[:, :, :], over_experts(kmax[:, :]), ALU.is_equal))
                if k == 0:
                    then(dve.scalar_tensor_tensor(pr[:, :, :], oh[0][:, :, :], -2.0, pr[:, :, :], ALU.mult, ALU.add))
            dve.tensor_tensor(mask[:, :, :], oh[0][:, :, :], oh[1][:, :, :], ALU.add).then_inc(mask_done, 1)
            then(dve.tensor_tensor(den[:, :], top[:, 0], top[:, 1], ALU.add))
            then(dve.reciprocal(den[:, :], den[:, :]))
            for k in range(TOPK):
                then(dve.tensor_tensor(keep["w"][:, k], top[:, k], den[:, :], ALU.mult))
            dve.wait_ge(counts_mm, 1)
            then(dve.tensor_copy(scan[0][:, :, :].rearrange("p t e -> p (t e)"), psT[:, 0:TE]))
            then(dve.tensor_copy(before[:, :, :], scan[0][:, :, :]))
            n, step = 0, 1
            while step < TILES:
                a, b = scan[n], scan[1 - n]
                then(dve.tensor_tensor(b[:, step:], a[:, step:], a[:, :TILES - step], ALU.add))
                then(dve.tensor_copy(b[:, :step], a[:, :step]))
                n, step = 1 - n, 2 * step
            total = scan[n]
            then(dve.tensor_copy(n_i[:, :], total[:, TILES - 1]))
            then(dve.tensor_scalar(t_i[:, :], n_i[:, :], P.bit_length() - 1, None, ALU.arith_shift_right))
            then(dve.tensor_copy(tiles[:, :], t_i[:, :]))
            then(dve.tensor_scalar_add(tiles[:, :], tiles[:, :], 1.0))
            then(dve.tensor_copy(ends[0][:, :], tiles[:, :]))
            m, step = 0, 1
            while step < EXPERTS:
                a, b = ends[m], ends[1 - m]
                then(dve.tensor_tensor(b[:, step:], a[:, step:], a[:, :EXPERTS - step], ALU.add))
                then(dve.tensor_copy(b[:, :step], a[:, :step]))
                m, step = 1 - m, 2 * step
            end = ends[m]
            then(dve.tensor_tensor(base[:, :], end[:, :], tiles[:, :], ALU.subtract))
            then(dve.tensor_scalar_mul(base[:, :], base[:, :], float(P)))
            then(dve.tensor_tensor(before[:, :, :], total[:, :, :], before[:, :, :], ALU.subtract))
            then(dve.tensor_tensor(place[:, :, :], before[:, :, :], over_tiles(base), ALU.add))
            then(dve.tensor_tensor(place[:, :, :], place[:, :, :],
                                   psB[:, 0:TE].rearrange("p (t e) -> p t e", e=EXPERTS), ALU.add))
            for k in range(TOPK):
                then(dve.tensor_tensor(prod[:, :, :], place[:, :, :], oh[k][:, :, :], ALU.mult))
                then(dve.reduce_sum(slot[:, k], prod[:, :, :], AX_X))
            then(dve.tensor_copy(keep["slot_i"][:, :], slot[:, :, :].rearrange("p k t -> p (k t)")))
            then(dve.tensor_scalar(tile_i[:, :], keep["slot_i"][:, :], P.bit_length() - 1, None, ALU.arith_shift_right))
            then(dve.tensor_scalar(row_i[:, :], keep["slot_i"][:, :], P - 1, None, ALU.bitwise_and))
            dve.tensor_copy(tile_f[:, :], tile_i[:, :]).then_inc(split_done, 1)
            dve.tensor_copy(row_f[:, :], row_i[:, :]).then_inc(split_done, 1)
            dve.wait_ge(split_done, 2)
            wide = (P, SLOTS, EXPERTS)
            then(dve.tensor_tensor(ge[:, :, :], iota_s[:, :].unsqueeze(2).broadcast_to(wide),
                                   end[:, :].unsqueeze(1).broadcast_to(wide), ALU.is_ge))
            then(dve.reduce_sum(emap[:, :], ge[:, :, :], AX_X))
            then(dve.tensor_scalar_min(emap[:, :], emap[:, :], float(EXPERTS - 1)))
            then(dve.tensor_copy(keep["tile_expert"][:, :], emap[:, :]))
            then(dve.tensor_tensor(isnew[:, 1:], emap[:, 1:], emap[:, :SLOTS - 1], ALU.is_gt))
            then(dve.tensor_tensor(isnew[:, 1:], isnew[:, 1:], emap[:, 1:], ALU.mult))
            then(dve.scalar_tensor_tensor(isnew[:, 1:], isnew[:, 1:], float(EXPERTS - 1), isnew[:, 1:],
                                          ALU.is_lt, ALU.mult))
            then(dve.tensor_copy(keep["turn"][:, 1:], isnew[:, :]))
            then(dve.tensor_copy(keep["turn"][:, 0:1], isnew[:, 0:1]))
            for n in range(PAIRS // PART):
                part = slice(n * PART, (n + 1) * PART)
                wide = (P, PART, SLOTS)
                if n >= 1:
                    dve.wait_ge(tok_done, n)
                dve.tensor_tensor(oh_tile[:, :, :], iota_s[:, :].unsqueeze(1).broadcast_to(wide),
                                  tile_f[:, part].unsqueeze(2).broadcast_to(wide), ALU.is_equal).then_inc(tile_done, 1)
                if n >= 2:
                    dve.wait_ge(id_mm, n - 1)
                wide = (P, PART, P)
                dve.tensor_tensor(oh_row[:, n % 2], iota_r[:, :].unsqueeze(1).broadcast_to(wide),
                                  row_f[:, part].unsqueeze(2).broadcast_to(wide), ALU.is_equal).then_inc(row_done, 1)
            dve.wait_ge(id_mm, PAIRS // PART)
            dve.tensor_copy(keep["ids"][:, :], psI[:, 0:SLOTS]).then_inc(ids_done, 1)

        @block.tensor
        def _(pe):
            pe.wait_ge(mask_done, 1)
            m = mask[:, :, :].rearrange("p t e -> p (t e)")
            pe.matmul(psB[:, 0:TE], tri[:, :], m, start=True, stop=True)
            pe.matmul(psT[:, 0:TE], all_r[:, :], m, start=True, stop=True).then_inc(counts_mm, 1)
            for n in range(PAIRS // PART):
                pe.wait_ge(row_done, n + 1)
                pe.wait_ge(tok_done, n + 1)
                for m in range(PART):
                    last = pe.matmul(psI[:, 0:SLOTS], oh_row[:, n % 2, m], tok_tile[:, n % 2, m],
                                     start=(n == 0 and m == 0), stop=(n == PAIRS // PART - 1 and m == PART - 1))
                last.then_inc(id_mm, 1)


def routed_experts(nc, io, keep):
    with Stage(nc, keep, "re") as ctx:
        sem, count = ctx.sem, ctx.count

        def sb(name, shape, dt=F32):
            return ctx.enter_context(nc.sbuf_tensor(name, shape, dt))

        def psum(name, shape):
            return ctx.enter_context(nc.psum_tensor(name, shape, F32))

        U = 8
        YB = 4
        LAG = U + 1
        idx = sb("idx", [P, U], I32)
        hg = sb("hg", [P, U, D])
        hgT = sb("hgT", [P, 2, 2, D], F32R)
        sil = sb("sil2", [P, FF])
        act_t = sb("act_t2", [P, FPAD])
        aT = sb("aT", [P, 2, FPAD], F32R)
        y = sb("y_t", [P, YB, D])
        psT = psum("psT2", [P, D])
        psG = psum("psG2", [P, D])
        psU = psum("psU2", [P, D])
        psA = psum("psA2", [P, D])
        psY = [psum(f"psY2{n}", [P, D]) for n in range(2)]

        idx_done = count("idx_done", U)
        idx_seen = sem("idx_seen")
        g_in = [sem(f"g_in{n}") for n in range(U)]
        y_out = [sem(f"y_out{n}") for n in range(YB)]
        pad_done = sem("pad_done2")
        t_mm, hi_done, lo_done = count("t_mm2", U), count("hgT_hi"), count("hgT_lo", 1)
        g_mm, u_mm = count("g_mm2"), count("u_mm2", 2)
        sil_done, a_done = count("sil_done2", 1), count("a_done2", 1)
        ta_mm, ahi_done, alo_done = count("ta_mm2", 1), count("ahi_done"), count("alo_done", 1)
        y_mm, y_done = count("y_mm2", 1), count("y_done", 2)
        block = ctx.block()
        y_tiles = io["y"].rearrange("(s p) d -> s p d", p=P)

        def slots(eng, step):
            with eng.Fori(0, SLOTS // U - 1) as i:
                for r in range(U):
                    step(i, r, False)
            for r in range(U):
                step(SLOTS // U - 1, r, True)

        def in_range(r, n, last):
            return not last or r + n < U

        def on(i, r, n):
            return i + (r + n) // U, (r + n) % U

        @block.sync
        def _(sp):
            for n in range(YB):
                sp.sem_inc(y_out[n], 16)
            with sp.Fori(0, SLOTS // YB) as i:
                for r in range(YB):
                    y_done.wait(sp, YB * i + r + 1)
                    sp.dma_start(y_tiles[YB * i + r], y[:, r]).then_inc(y_out[r], 16)
            for n in range(YB):
                sp.wait_ge(y_out[n], 16 * (SLOTS // YB + 1))

        @block.gpsimd
        def _(pool):
            def gather(s, r):
                t_mm.wait(pool, s - U + 1)
                pool.tensor_copy(idx[:, r:r + 1], keep["ids"][:, bass.ds(s, 1)]).then_inc(idx_done.sem, 1)
                idx_done.wait(pool, s + 1)
                pool.sem_inc(idx_seen, 1)
                pool.indirect_dma_start(out=hg[:, r], out_offset=None, in_=io["h2"],
                                        in_offset=bass.IndirectOffsetOnAxis(ap=idx[:, r:r + 1].bitcast(U32), axis=0))\
                    .then_inc(g_in[r], 16)

            def check(s, at):
                e = pool.value_load(keep["turn"][0:1, bass.ds(at, 1)], min_val=0, max_val=EXPERTS - 1)
                with pool.If(e > 0):
                    y_mm.wait(pool, s)
                    pool.wait_ge(keep["raw_in"], 16 * RAW_DMAS * (e + 2))
                    with pool.If(e % 2 == 0):
                        split_expert(pool, keep, 1, e + 1)
                    with pool.If(e % 2 == 1):
                        split_expert(pool, keep, 0, e + 1)
                    with pool.If(e < EXPERTS - 2):
                        early = pool.value_load(keep["turn"][0:1, bass.ds(at, 1)], min_val=1, max_val=EXPERTS - 3)
                        pool.wait_ge(keep["split_done"], SPLIT_STEPS * (e + 2))
                        load_expert(pool, io, keep, early + 2)

            idx_done.start(pool)
            for r in range(U):
                gather(r, r)
            ctx.clear_previous(pool)
            with pool.Fori(1, SLOTS // U) as i:
                for r in range(U):
                    gather(U * i + r, r)
                    check(U * i + r - LAG, U * i + r - LAG + 1)
            with pool.Fori(SLOTS - LAG, SLOTS) as s:
                check(s, s + 1)

        @block.scalar
        def _(act):
            def upper(i, r):
                s = U * i + r
                t_mm.wait(act, s + 1)
                u_mm.wait(act, s - 1)
                act.activation(hgT[:, r % 2, 0], psT[:, :], ACT.Copy).then_inc(hi_done.sem, 1)

            def silu(i, r):
                s = U * i + r
                g_mm.wait(act, s + 1)
                a_done.wait(act, s)
                act.activation(sil[:, :], psG[:, 0:FF], ACT.Silu).then_inc(sil_done.sem, 1)

            def upper_a(i, r):
                s = U * i + r
                ta_mm.wait(act, s + 1)
                y_mm.wait(act, s)
                act.activation(aT[:, 0], psA[:, 0:FPAD], ACT.Copy).then_inc(ahi_done.sem, 1)

            def copy_y(i, r):
                s = U * i + r
                y_mm.wait(act, s + 1)
                act.wait_ge(y_out[r % YB], 16 * (U // YB * i + r // YB + 1))
                act.activation(y[:, r % YB], psY[r % 2][:, :], ACT.Copy).then_inc(y_done.sem, 1)

            def step(i, r, last):
                upper_a(i, r)
                if in_range(r, 2, last):
                    upper(*on(i, r, 2))
                if in_range(r, 1, last):
                    silu(*on(i, r, 1))
                copy_y(i, r)

            for x in (sil_done, y_done):
                x.start(act)
            act.wait_ge(pad_done, 1)
            upper(0, 0)
            upper(0, 1)
            silu(0, 0)
            slots(act, step)

        @block.vector
        def _(dve):
            def lower(i, r):
                s = U * i + r
                hi_done.wait(dve, s + 1)
                dve.tensor_tensor(hgT[:, r % 2, 1], psT[:, :], hgT[:, r % 2, 0].bitcast(F32), ALU.subtract)\
                   .then_inc(lo_done.sem, 1)

            def gated(i, r):
                s = U * i + r
                sil_done.wait(dve, s + 1)
                u_mm.wait(dve, s + 1)
                ta_mm.wait(dve, s)
                dve.tensor_tensor(act_t[:, 0:FF], sil[:, :], psU[:, 0:FF], ALU.mult).then_inc(a_done.sem, 1)

            def lower_a(i, r):
                ahi_done.wait(dve, U * i + r + 1)
                dve.tensor_tensor(aT[:, 1], psA[:, 0:FPAD], aT[:, 0].bitcast(F32), ALU.subtract)\
                   .then_inc(alo_done.sem, 1)

            def step(i, r, last):
                lower_a(i, r)
                if in_range(r, 2, last):
                    lower(*on(i, r, 2))
                if in_range(r, 1, last):
                    gated(*on(i, r, 1))

            for x in (lo_done, a_done, alo_done):
                x.start(dve)
            dve.memset(act_t[:, :], 0.0).then_inc(pad_done, 1)
            dve.wait_ge(pad_done, 1)
            lower(0, 0)
            lower(0, 1)
            gated(0, 0)
            slots(dve, step)

        @block.tensor
        def _(pe):
            def transpose_h(i, r):
                s = U * i + r
                pe.wait_ge(g_in[r], 16 * (i + 1))
                lo_done.wait(pe, s)
                for c in range(KC):
                    last = pe.transpose(psT[:, c * P:(c + 1) * P], hg[:, r, c * P:(c + 1) * P], keep["ident"][:, :])
                last.then_inc(t_mm.sem, 1)

            def expert(i, r):
                e = pe.value_load(keep["tile_expert"][0:1, bass.ds(U * i + r, 1)], min_val=0, max_val=EXPERTS - 1)
                return e, e % 2

            def gate_up(i, r):
                s = U * i + r
                e, buf = expert(i, r)
                pe.wait_ge(keep["split_done"], SPLIT_STEPS * (e + 1))
                lo_done.wait(pe, s + 1)
                for n, (ps, done, free) in enumerate(((psG, g_mm, sil_done), (psU, u_mm, a_done))):
                    free.wait(pe, s)
                    todo = split_products(KC)
                    for m, (a, w, c) in enumerate(todo):
                        last = pe.matmul(ps[:, 0:FF], hgT[:, r % 2, a, c * P:(c + 1) * P],
                                         keep["gu_x"][:, buf, w, c, n * FF:(n + 1) * FF],
                                         start=(m == 0), stop=(m == len(todo) - 1))
                    last.then_inc(done.sem, 1)

            def transpose_a(i, r):
                s = U * i + r
                a_done.wait(pe, s + 1)
                alo_done.wait(pe, s)
                for c in range(NF):
                    last = pe.transpose(psA[:, c * P:(c + 1) * P], act_t[:, c * P:(c + 1) * P], keep["ident"][:, :])
                last.then_inc(ta_mm.sem, 1)

            def down(i, r):
                s = U * i + r
                e, buf = expert(i, r)
                alo_done.wait(pe, s + 1)
                y_done.wait(pe, s - 1)
                todo = split_products(NF)
                for m, (a, w, c) in enumerate(todo):
                    f = FCH[c]
                    last = pe.matmul(psY[r % 2][:, :], aT[0:f, a, c * P:(c + 1) * P], keep["dn_x"][0:f, buf, w, c],
                                     start=(m == 0), stop=(m == len(todo) - 1))
                last.then_inc(y_mm.sem, 1)

            def step(i, r, last):
                transpose_a(i, r)
                if in_range(r, 2, last):
                    transpose_h(*on(i, r, 2))
                if in_range(r, 1, last):
                    gate_up(*on(i, r, 1))
                down(i, r)

            for x in (t_mm, u_mm, ta_mm, y_mm):
                x.start(pe)
            transpose_h(0, 0)
            transpose_h(0, 1)
            gate_up(0, 0)
            slots(pe, step)


def combine(nc, io, keep):
    with Stage(nc, keep, "cb") as ctx:
        sem, count = ctx.sem, ctx.count

        def sb(name, shape, dt=F32):
            return ctx.enter_context(nc.sbuf_tensor(name, shape, dt))

        def psum(name, shape):
            return ctx.enter_context(nc.psum_tensor(name, shape, F32))

        U = 8
        gate = sb("gate_", [P, B, D])
        idx = sb("idx_", [P, U, TOPK], I32)
        yk = sb("yk", [P, U, TOPK, D])
        x1 = sb("x1_t", [P, U, D])
        act_t = sb("act_t3", [P, 2, FF])
        aT = sb("aT_", [P, 2, 2, FPAD], F32R)
        y0 = sb("y0", [P, 2, D])
        y01 = sb("y01", [P, 2, D])
        ysum = sb("ysum", [P, 2, D])
        ygate = sb("ygate", [P, 2, D])
        psA = [psum(f"psA3{n}", [P, D]) for n in range(2)]
        psY = [psum(f"psY3{n}", [P, D]) for n in range(2)]
        gate_in = sem("gatec_in")
        idx_done = count("idxc_done")
        idx_seen = sem("idxc_seen")
        pad_done = sem("pad_done3")
        y_in = [sem(f"y_in{n}") for n in range(U)]
        x1_in = [sem(f"x1c_in{n}") for n in range(U)]
        out_done = [sem(f"out_done{n}") for n in range(U)]
        act_here = count("act_here")
        ta_mm, ahi_done, alo_done = count("ta_mm3", 2), count("ahi3_done"), count("alo3_done", 2)
        y_mm = count("y_mm3", 2)
        y0_done, y01_done = count("y0_done"), count("y01_done", U)
        ysum_done, ygate_done = count("ysum_done", 2), count("ygate_done", 2)
        out_sum = count("out_sum", 2)
        x1_tiles = io["x1"].rearrange("(t p) d -> t p d", p=P)
        out_tiles = io["out"].rearrange("(t p) d -> t p d", p=P)
        block = ctx.block()

        def slots(eng, step):
            with eng.Fori(0, B - 1) as i:
                for tt in range(TPB):
                    step(i, tt, False)
            for tt in range(TPB):
                step(B - 1, tt, True)

        def in_range(tt, n, last):
            return not last or tt + n < TPB


        @block.sync
        def _(sp):
            def load(i, tt):
                sp.wait_ge(out_done[tt % U], 16 * ((TPB // U) * i + tt // U + 1))
                sp.dma_start(x1[:, tt % U], x1_tiles[TPB * i + tt]).then_inc(x1_in[tt % U], 16)

            def store(i, tt):
                out_sum.wait(sp, TPB * i + tt + 1)
                sp.dma_start(out_tiles[TPB * i + tt], x1[:, tt % U]).then_inc(out_done[tt % U], 16)

            def step(i, tt, last):
                if in_range(tt, U - 1, last):
                    load(*ahead(i, tt, U - 1))
                store(i, tt)

            for n in range(U):
                sp.sem_inc(out_done[n], 16)
            for b in range(B):
                sp.dma_start(gate[:, b], io["modrows"][R_GB, b].partition_broadcast(P)).then_inc(gate_in, 16)
            for n in range(U - 1):
                load(0, n)
            slots(sp, step)
            for n in range(U):
                sp.wait_ge(out_done[n], 16 * (TILES // U + 1))

        @block.gpsimd
        def _(pool):
            with pool.Fori(0, TILES // U) as i:
                for r in range(U):
                    t = U * i + r
                    y01_done.wait(pool, t - U + 1)
                    for k in range(TOPK):
                        pool.tensor_copy(idx[:, r, k:k + 1], keep["slot_i"][:, bass.ds(k * TILES + t, 1)])\
                            .then_inc(idx_done.sem, 1)
                    idx_done.wait(pool, TOPK * (t + 1))
                    pool.sem_inc(idx_seen, 1)
                    for k in range(TOPK):
                        pool.indirect_dma_start(out=yk[:, r, k], out_offset=None, in_=io["y"],
                                                in_offset=bass.IndirectOffsetOnAxis(
                                                    ap=idx[:, r, k:k + 1].bitcast(U32), axis=0)).then_inc(y_in[r], 16)
            ctx.clear_previous(pool)

        @block.scalar
        def _(act):
            def place(i, tt):
                t = TPB * i + tt
                ta_mm.wait(act, t - 1)
                act.activation(act_t[:, tt % 2].unsqueeze(1), keep["act"][:, bass.ds(t, 1)], ACT.Copy)\
                   .then_inc(act_here.sem, 1)

            def upper_a(i, tt):
                t = TPB * i + tt
                ta_mm.wait(act, t + 1)
                y_mm.wait(act, t - 1)
                act.activation(aT[:, tt % 2, 0], psA[tt % 2][:, 0:FPAD], ACT.Copy).then_inc(ahi_done.sem, 1)

            def weigh(i, tt):
                t = TPB * i + tt
                act.wait_ge(y_in[tt % U], 16 * TOPK * ((TPB // U) * i + tt // U + 1))
                y01_done.wait(act, t - 1)
                act.activation(y0[:, tt % 2], yk[:, tt % U, 0], ACT.Copy,
                               scale=keep["w"][:, 0, bass.ds(t, 1)]).then_inc(y0_done.sem, 1)

            def step(i, tt, last):
                if in_range(tt, 2, last):
                    place(*ahead(i, tt, 2))
                if in_range(tt, 1, last):
                    upper_a(*ahead(i, tt, 1))
                    weigh(*ahead(i, tt, 1))

            act.wait_ge(pad_done, 2)
            place(0, 0)
            place(0, 1)
            upper_a(0, 0)
            weigh(0, 0)
            slots(act, step)

        @block.vector
        def _(dve):
            def lower_a(i, tt):
                ahi_done.wait(dve, TPB * i + tt + 1)
                dve.tensor_tensor(aT[:, tt % 2, 1], psA[tt % 2][:, 0:FPAD], aT[:, tt % 2, 0].bitcast(F32),
                                  ALU.subtract).then_inc(alo_done.sem, 1)

            def add_experts(i, tt):
                t = TPB * i + tt
                y0_done.wait(dve, t + 1)
                ysum_done.wait(dve, t - 1)
                dve.scalar_tensor_tensor(y01[:, tt % 2], yk[:, tt % U, 1], keep["w"][:, 1, bass.ds(t, 1)],
                                         y0[:, tt % 2], ALU.mult, ALU.add).then_inc(y01_done.sem, 1)

            def finish(i, tt):
                t = TPB * i + tt
                y01_done.wait(dve, t + 1)
                y_mm.wait(dve, t + 1)
                ygate_done.wait(dve, t - 1)
                dve.tensor_tensor(ysum[:, tt % 2], psY[tt % 2][:, :], y01[:, tt % 2], ALU.add).then_inc(ysum_done.sem, 1)
                ysum_done.wait(dve, t + 1)
                out_sum.wait(dve, t - 1)
                dve.tensor_tensor(ygate[:, tt % 2].unsqueeze(1), ysum[:, tt % 2].unsqueeze(1),
                                  gate[:, bass.ds(i, 1)], ALU.mult).then_inc(ygate_done.sem, 1)
                ygate_done.wait(dve, t + 1)
                dve.wait_ge(x1_in[tt % U], 16 * ((TPB // U) * i + tt // U + 1))
                dve.tensor_tensor(x1[:, tt % U], ygate[:, tt % 2], x1[:, tt % U], ALU.add).then_inc(out_sum.sem, 1)

            def step(i, tt, last):
                if in_range(tt, 1, last):
                    lower_a(*ahead(i, tt, 1))
                    add_experts(*ahead(i, tt, 1))
                finish(i, tt)

            for x in (alo_done, y01_done, ysum_done, ygate_done, out_sum):
                x.start(dve)
            for n in range(2):
                dve.memset(psA[n][:, 0:FPAD], 0.0).then_inc(pad_done, 1)
            dve.wait_ge(gate_in, 16 * B)
            lower_a(0, 0)
            add_experts(0, 0)
            slots(dve, step)

        @block.tensor
        def _(pe):
            def transpose_a(i, tt):
                t = TPB * i + tt
                act_here.wait(pe, t + 1)
                alo_done.wait(pe, t - 1)
                for c in range(NF):
                    f = FCH[c]
                    last = pe.transpose(psA[tt % 2][0:f, c * P:(c + 1) * P], act_t[:, tt % 2, c * P:c * P + f],
                                        keep["ident"][:, :])
                last.then_inc(ta_mm.sem, 1)

            def down(i, tt):
                t = TPB * i + tt
                alo_done.wait(pe, t + 1)
                ysum_done.wait(pe, t - 1)
                todo = split_products(NF)
                for m, (a, w, c) in enumerate(todo):
                    f = FCH[c]
                    last = pe.matmul(psY[tt % 2][:, :], aT[0:f, tt % 2, a, c * P:(c + 1) * P], keep["dn"][0:f, w, c],
                                     start=(m == 0), stop=(m == len(todo) - 1))
                last.then_inc(y_mm.sem, 1)

            def step(i, tt, last):
                if in_range(tt, 1, last):
                    transpose_a(*ahead(i, tt, 1))
                down(i, tt)

            for x in (ta_mm, y_mm):
                x.start(pe)
            pe.wait_ge(pad_done, 2)
            transpose_a(0, 0)
            slots(pe, step)


def block_program(nc, io):
    with ExitStack() as ctx:
        def sb(name, shape, dt=F32):
            return ctx.enter_context(nc.sbuf_tensor(name, shape, dt))

        keep = {
            "ident": sb("ident", [P, P]),
            "ones": sb("ones", [P, P], F32R),
            "rstd2": sb("rstd2", [P, B, TPB]),
            "nmr2": sb("nmr2", [P, B, TPB]),
            "logits": sb("logits", [P, TILES, EXPERTS]),
            "w": sb("w", [P, TOPK, TILES]),
            "slot_i": sb("slot_i", [P, TOPK * TILES], I32),
            "tok2": sb("tok2", [P, TOPK * TILES]),
            "ids": sb("ids", [P, SLOTS], I32),
            "tile_expert": sb("tile_expert", [P, SLOTS], I32),
            "turn": sb("turn", [P, SLOTS + 1], I32),
        }
        with ExitStack() as attn:
            def ab(name, shape, dt=F32):
                return attn.enter_context(nc.sbuf_tensor(name, shape, dt))

            keep["modc"] = ab("modc", [P, B, 2, KC])
            keep["kvT"] = ab("kvT", [P, B, D])
            keep["ks_hi"] = ab("ks_hi", [P, B, 2 * KVH], F32R)
            keep["ks_lo"] = ab("ks_lo", [P, B, 2 * KVH], F32R)
            keep["wq_hi"] = ab("wq_hi", [P, HEADS, KC, P], F32R)
            keep["wq_lo"] = ab("wq_lo", [P, HEADS, KC, P], F32R)
            with ExitStack() as kv:
                keep["wkv_hi"] = kv.enter_context(nc.sbuf_tensor("wkv_hi", [P, 2, KC, D], F32R))
                keep["wkv_lo"] = kv.enter_context(nc.sbuf_tensor("wkv_lo", [P, 2, KC, D], F32R))
                keep["front"] = [kv.enter_context(nc.sbuf_tensor(name, [P, TB] + more, F32)) for name, more in
                                 (("xt", [D]), ("zt", [D]), ("st", [6]), ("mv", [2]), ("var", []), ("sd", []),
                                  ("rstd", []), ("nmr", []))]
                setup(nc, io, keep)
                keys_values(nc, io, keep)
            queries(nc, io, keep)
        def late(name, shape, dt=F32):
            keep[name] = sb(name, shape, dt)

        late("act", [P, TILES, FF])
        late("dn", [P, 2, NF, D], F32R)
        with ExitStack() as ffn:
            def fb(name, shape, dt=F32):
                keep[name] = ffn.enter_context(nc.sbuf_tensor(name, shape, dt))

            fb("gu_raw", [P, KC, GU])
            fb("dn_raw", [P, NF, D])
            fb("gu_x", [P, 2, 2, KC, GU], F32R)
            fb("dn_x", [P, 2, 2, NF, D], F32R)
            for name in ("raw_in", "upper_done", "split_done"):
                keep[name] = ctx.enter_context(nc.semaphore(name))
            shared_expert(nc, io, keep)
            route(nc, io, keep)
            routed_experts(nc, io, keep)
        combine(nc, io, keep)
        with nc.Block() as block:
            @block.gpsimd
            def _(pool):
                for s in keep["previous"].sems:
                    pool.sem_clear(s)

        keep["previous"].held.close()


def chunked(w):
    k, n = w.shape
    return w.reshape(k // P, P, n).transpose(1, 0, 2)


def kernel(**inputs):
    import concourse.bacc as bacc
    from concourse.bass_utils import run_bass_kernel_spmd

    a = {k.split("_", 1)[1]: np.asarray(v) for k, v in inputs.items()}
    laid_out = {
        "x": a["attn_hidden_states"].reshape(TOK, D),
        "wqT": chunked(a["attn_Wq"].T).reshape(P, KC, HEADS, P).transpose(0, 2, 1, 3),
        "bq": a["attn_bq"].reshape(HEADS, P).T,
        "wkvT": np.stack([chunked(a["attn_Wk"].T), chunked(a["attn_Wv"].T)], 1),
        "bk": a["attn_bk"],
        "bv": a["attn_bv"],
        "woT": a["attn_Wo"].T.reshape(HEADS, P, D).transpose(1, 0, 2),
        "cT": chunked(a["c"].T).reshape(P, KC * B),
        "wmod": chunked(a["wmod"]).reshape(P, KC, 3, 2 * D).transpose(0, 2, 1, 3),
        "br": a["ffn_br"],
        "rb": a["ffn_rb"],
        "gu_s": chunked(np.concatenate([a["ffn_Wg_s"], a["ffn_Wr"], a["ffn_Wu_s"]], 1)),
        "dn_s": a["ffn_Wd_s"],
        "gu_e": np.stack([chunked(w) for w in np.concatenate([a["ffn_Wg"], a["ffn_Wu"]], 2)]),
        "dn_e": a["ffn_Wd"],
    }
    laid_out = {k: np.ascontiguousarray(v) for k, v in laid_out.items()}
    nc = bacc.Bacc("TRN2", target_bir_lowering=False, num_devices=1)
    io = {k: nc.dram_tensor(f"in_{k}", v.shape, F32, kind="ExternalInput").ap() for k, v in laid_out.items()}
    out = nc.dram_tensor("out", (TOK, D), F32, kind="ExternalOutput").ap()
    io["out"] = out
    for name, rows in (("x1", TOK), ("h2", TOK), ("y", SLOTS * P)):
        io[name] = nc.dram_tensor(f"dram_{name}", (rows, D), F32, kind="Internal").ap()
    io["modrows"] = nc.dram_tensor("modrows", (len(ROWS), B, D), F32, kind="Internal").ap()
    io["hTs"] = nc.dram_tensor("hTs", (B * BB, P, 2, KC, BLK), F32, kind="Internal").ap()
    block_program(nc, io)
    r = run_bass_kernel_spmd(nc, [{f"in_{k}": v for k, v in laid_out.items()}], core_ids=[0])
    return r.results[0]["out"].reshape(B, S, D)
```
